# Optimizing a Trainium2 kernel written in Bass

```python
import numpy as np
import jax
import jax.numpy as jnp

def _softmax(x, axis=-1):
    return jax.nn.softmax(x, axis=axis)

def _gelu(x):
    return jax.nn.gelu(x, approximate=True)

def _silu(x):
    return jax.nn.silu(x)

def _sigmoid(x):
    return jax.nn.sigmoid(x)

def _layernorm(x, axis=-1, eps=1e-05):
    m = jnp.mean(x, axis=axis, keepdims=True)
    v = jnp.var(x, axis=axis, keepdims=True)
    return (x - m) / jnp.sqrt(v + eps)

def _scatter_add(tgt, idx, src, axis=0):
    return tgt.at[idx].add(src)

def _segment_sum(src, seg, n):
    return jax.ops.segment_sum(src, seg, n)
kernel_name = 'mk_xattn_seq_d4_seqx_r8_ba9286'

def setup_inputs(seed: int=0):
    np.random.seed(seed)
    _w = jnp.asarray

    def _rec_inputs():
        import jax
        import jax.numpy as jnp
        _rk = jax.random.key(seed)
        x = -0.0005207 + 1.001 * jax.random.normal(jax.random.fold_in(_rk, 1), (64, 64, 128), jnp.float32)
        _lenS = 64 - jax.random.randint(jax.random.fold_in(_rk, 7), (64,), 0, max(1, 64 // 4) + 1, jnp.int32)
        _lenS2 = 64 - jax.random.randint(jax.random.fold_in(_rk, 8), (64,), 0, max(1, 64 // 4) + 1, jnp.int32)
        _ctx_1024P = jax.random.normal(jax.random.fold_in(_rk, 11), (64, 16, 128), jnp.float32)
        _ctx_1024c = jax.random.dirichlet(jax.random.fold_in(_rk, 511), 0.3 * jnp.ones((16,), jnp.float32), (64, 64))
        _ctx_1024t = jnp.einsum('bsk,bkd->bsd', _ctx_1024c, _ctx_1024P)
        _ctx_1024t = _ctx_1024t * jax.lax.rsqrt(jnp.mean(jnp.square(_ctx_1024t)) + 1e-12) * 0.953939
        ctx_1024 = -0.000514642 + 1.00011 * (_ctx_1024t + 0.3 * jax.random.normal(jax.random.fold_in(_rk, 611), (64, 64, 128), jnp.float32))
        _validS = jnp.arange(64)[None, :] < _lenS[:, None]
        _validS2 = jnp.arange(64)[None, :] < _lenS2[:, None]
        _causal = jnp.tril(jnp.ones((64, 64), dtype=bool))
        mask_BxSx1_ff1 = jnp.where(jnp.ones((64, 64, 1), dtype=bool), 1.0, 0.0).astype(jnp.float32)
        mask_BxSx1024_bf0 = jnp.logical_not(jnp.ones((64, 64, 128), dtype=bool))
        mask_Bx1xSxS2_if1 = jnp.where(jnp.ones((64, 1, 64, 64), dtype=bool), 1, 0).astype(jnp.int32)
        mask_Bx1xSxS2_ik0 = jnp.where(jnp.broadcast_to(_validS2[:, None, None, :], (64, 1, 64, 64)), 0, 1).astype(jnp.int32)
        return (x, ctx_1024, mask_BxSx1_ff1, mask_BxSx1024_bf0, mask_Bx1xSxS2_if1, mask_Bx1xSxS2_ik0)
    x, ctx_1024, mask_BxSx1_ff1, mask_BxSx1024_bf0, mask_Bx1xSxS2_if1, mask_Bx1xSxS2_ik0 = _rec_inputs()

    def _L0_xattn_setup():
        import jax, jax.numpy as jnp
        import numpy as np
        B, Q, M, D, H, K = (4, 64, 64, 128, 16, 64)

        def layer_norm(x, g, b, eps=1e-05):
            mu = x.mean(-1, keepdims=True)
            var = ((x - mu) ** 2).mean(-1, keepdims=True)
            return (x - mu) * jax.lax.rsqrt(var + eps) * g + b

        def rel_shift(x):
            b, h, q, k = x.shape
            x = jnp.pad(x, ((0, 0), (0, 0), (0, 0), (1, 0)))
            x = x.reshape(b, h, k + 1, q)[:, :, 1:, :]
            return x.reshape(b, h, q, k)
        key = jax.random.key(seed)
        ks = jax.random.split(key, 16)
        w = lambda i, shape: jax.random.normal(ks[i], shape, jnp.float32) * 0.02
        return {'layer_input': jax.random.normal(ks[0], (B, Q, D), jnp.float32), 'memory': jax.random.normal(ks[1], (B, M, D), jnp.float32), 'content_bias': w(2, (H, K)), 'position_bias': w(3, (H, K)), 'non_pad_mask': jnp.ones((B, Q, 1), jnp.float32), 'Wq': w(4, (D, H * K)), 'Wk': w(5, (D, H * K)), 'Wv': w(6, (D, H * K)), 'Wr': w(7, (D, H * K)), 'Wo': w(8, (H * K, D)), 'ln1_g': jnp.ones((D,), jnp.float32), 'ln1_b': jnp.zeros((D,), jnp.float32), 'W1': w(9, (D, 4 * D)), 'b1': jnp.zeros((4 * D,), jnp.float32), 'W2': w(10, (4 * D, D)), 'b2': jnp.zeros((D,), jnp.float32), 'ln2_g': jnp.ones((D,), jnp.float32), 'ln2_b': jnp.zeros((D,), jnp.float32), 'slf_attn_mask': jnp.zeros((B, Q, M + Q), bool)}
    _L0_xattn_all = _L0_xattn_setup()
    _L0_xattn_in = {k: v for k, v in _L0_xattn_all.items() if k in ('content_bias', 'position_bias', 'Wq', 'Wk', 'Wv', 'Wr', 'Wo', 'ln1_g', 'ln1_b', 'W1', 'b1', 'W2', 'b2', 'ln2_g', 'ln2_b')}
    del _L0_xattn_all

    def _L1_xattn_setup():
        import jax, jax.numpy as jnp
        import numpy as np
        B, S, E, H, FF = (2, 256, 128, 16, 512)
        HD = E // H
        EPS = 1e-05

        def _layernorm(x, g, b):
            mu = jnp.mean(x, axis=-1, keepdims=True)
            var = jnp.mean(jnp.square(x - mu), axis=-1, keepdims=True)
            return (x - mu) * jax.lax.rsqrt(var + EPS) * g + b

        def _attention(v_in, k_in, q_in, mask, Wv, Wk, Wq, Wo, bo):
            N, Sk, _ = k_in.shape
            Sq = q_in.shape[1]
            v = v_in.reshape(N, Sk, H, HD)
            k = k_in.reshape(N, Sk, H, HD)
            q = q_in.reshape(N, Sq, H, HD)
            v = jnp.einsum('nkhd,ed->nkhe', v, Wv)
            k = jnp.einsum('nkhd,ed->nkhe', k, Wk)
            q = jnp.einsum('nqhd,ed->nqhe', q, Wq)
            energy = jnp.einsum('nqhd,nkhd->nhqk', q, k)
            energy = jnp.where(mask == 0, jnp.float32(-1e+20), energy)
            attn = jax.nn.softmax(energy / jnp.sqrt(jnp.float32(E)), axis=-1)
            out = jnp.einsum('nhqk,nkhd->nqhd', attn, v).reshape(N, Sq, E)
            return out @ Wo.T + bo
        key = jax.random.key(seed)
        ks = jax.random.split(key, 16)
        p = lambda k, shp: jax.random.normal(k, shp, dtype=jnp.float32) * 0.02
        x = jax.random.normal(ks[0], (B, S, E), dtype=jnp.float32)
        encoder_output = jax.random.normal(ks[1], (B, S, E), dtype=jnp.float32)
        tgt_mask = jnp.tril(jnp.ones((S, S), dtype=jnp.int32))[None, None].repeat(B, 0)
        src_mask = jnp.ones((B, 1, S, S), dtype=jnp.int32)
        return {'x': x, 'encoder_output': encoder_output, 'src_mask': src_mask, 'tgt_mask': tgt_mask, 'msa_Wv': p(ks[2], (HD, HD)), 'msa_Wk': p(ks[3], (HD, HD)), 'msa_Wq': p(ks[4], (HD, HD)), 'msa_Wo': p(ks[5], (E, E)), 'msa_bo': jnp.zeros((E,), jnp.float32), 'ca_Wv': p(ks[6], (HD, HD)), 'ca_Wk': p(ks[7], (HD, HD)), 'ca_Wq': p(ks[8], (HD, HD)), 'ca_Wo': p(ks[9], (E, E)), 'ca_bo': jnp.zeros((E,), jnp.float32), 'ff_W1': p(ks[10], (FF, E)), 'ff_b1': jnp.zeros((FF,), jnp.float32), 'ff_W2': p(ks[11], (E, FF)), 'ff_b2': jnp.zeros((E,), jnp.float32), 'ln1_g': jnp.ones((E,), jnp.float32), 'ln1_b': jnp.zeros((E,), jnp.float32), 'ln2_g': jnp.ones((E,), jnp.float32), 'ln2_b': jnp.zeros((E,), jnp.float32), 'ln3_g': jnp.ones((E,), jnp.float32), 'ln3_b': jnp.zeros((E,), jnp.float32)}
    _L1_xattn_all = _L1_xattn_setup()
    _L1_xattn_in = {k: v for k, v in _L1_xattn_all.items() if k in ('msa_Wv', 'msa_Wk', 'msa_Wq', 'msa_Wo', 'msa_bo', 'ca_Wv', 'ca_Wk', 'ca_Wq', 'ca_Wo', 'ca_bo', 'ff_W1', 'ff_b1', 'ff_W2', 'ff_b2', 'ln1_g', 'ln1_b', 'ln2_g', 'ln2_b', 'ln3_g', 'ln3_b')}
    del _L1_xattn_all

    def _L2_xattn_setup():
        import jax, jax.numpy as jnp
        import numpy as np
        NUM_ITERATIONS = 3
        LN_EPS = 1e-05
        key = jax.random.key(seed)
        ks = jax.random.split(key, 10)
        B, L, Lv, H = (8, 256, 32, 128)
        s = 1.0 / np.sqrt(H)
        s2 = 1.0 / np.sqrt(2 * H)
        return {'text_feat': jax.random.normal(ks[0], (B, L, H), dtype=jnp.float32), 'vision_feat': jax.random.normal(ks[1], (B, Lv, H), dtype=jnp.float32), 'Wt': jax.random.uniform(ks[2], (H, H), jnp.float32, -s, s), 'bt': jax.random.uniform(ks[3], (H,), jnp.float32, -s, s), 'Wv': jax.random.uniform(ks[4], (H, H), jnp.float32, -s, s), 'bv': jax.random.uniform(ks[5], (H,), jnp.float32, -s, s), 'Wg': jax.random.uniform(ks[6], (H, 2 * H), jnp.float32, -s2, s2), 'bg': jax.random.uniform(ks[7], (H,), jnp.float32, -s2, s2), 'gamma': jnp.ones((H,), jnp.float32), 'beta': jnp.zeros((H,), jnp.float32)}
    _L2_xattn_all = _L2_xattn_setup()
    _L2_xattn_in = {k: v for k, v in _L2_xattn_all.items() if k in ('Wt', 'bt', 'Wv', 'bv', 'Wg', 'bg', 'gamma', 'beta')}
    del _L2_xattn_all

    def _L3_xattn_setup():
        import jax, jax.numpy as jnp
        import numpy as np
        D, H, E, K, DFF = (128, 16, 8, 2, 512)
        B, L, T = (4, 64, 256)
        EPS = 1e-05

        def _xavier(key, shape):
            fan_in, fan_out = (shape[-1], shape[-2])
            a = jnp.sqrt(6.0 / (fan_in + fan_out))
            return jax.random.uniform(key, shape, jnp.float32, -a, a)

        def _ln(x, g, b):
            m = x.mean(-1, keepdims=True)
            v = ((x - m) ** 2).mean(-1, keepdims=True)
            return (x - m) / jnp.sqrt(v + EPS) * g + b

        def _mha(q_in, kv_in, in_w, in_b, out_w, out_b):
            wq, wk, wv = jnp.split(in_w, 3, axis=0)
            bq, bk, bv = jnp.split(in_b, 3, axis=0)
            dh = D // H

            def heads(x, w, b):
                y = x @ w.T + b
                return y.reshape(x.shape[0], x.shape[1], H, dh).transpose(0, 2, 1, 3)
            q = heads(q_in, wq, bq)
            k = heads(kv_in, wk, bk)
            v = heads(kv_in, wv, bv)
            scores = jnp.einsum('bhqd,bhkd->bhqk', q, k) / jnp.sqrt(jnp.float32(dh))
            attn = jax.nn.softmax(scores, axis=-1)
            out = jnp.einsum('bhqk,bhkd->bhqd', attn, v)
            out = out.transpose(0, 2, 1, 3).reshape(q_in.shape[0], q_in.shape[1], D)
            return out @ out_w.T + out_b

        def _fuse_moe(x, ln_g, ln_b, rw, rb, fc1_w, fc1_b, fc2_w, fc2_b):
            h = _ln(x, ln_g, ln_b)
            logits = h @ rw.T + rb
            vals, idx = jax.lax.top_k(logits, K)
            gates = jax.nn.softmax(vals, axis=-1)
            N = x.shape[0] * x.shape[1]
            hf = h.reshape(N, D)
            h1 = jax.nn.gelu(jnp.einsum('nd,efd->enf', hf, fc1_w) + fc1_b[:, None, :], approximate=False)
            eo = jnp.einsum('enf,edf->end', h1, fc2_w) + fc2_b[:, None, :]
            idx_f = idx.reshape(N, K)
            gates_f = gates.reshape(N, K)
            gathered = eo[idx_f, jnp.arange(N)[:, None], :]
            mixed = (gathered * gates_f[..., None]).sum(axis=1).reshape(x.shape)
            return x + mixed
        key = jax.random.key(seed)
        ks = jax.random.split(key, 16)
        inp = {'latents': jax.random.normal(ks[0], (B, L, D), jnp.float32), 'tokens': jax.random.normal(ks[1], (B, T, D), jnp.float32), 'sa_ln_g': jnp.ones((D,)), 'sa_ln_b': jnp.zeros((D,)), 'sa_in_w': _xavier(ks[2], (3 * D, D)), 'sa_in_b': jnp.zeros((3 * D,)), 'sa_out_w': _xavier(ks[3], (D, D)), 'sa_out_b': jnp.zeros((D,)), 'ca_q_ln_g': jnp.ones((D,)), 'ca_q_ln_b': jnp.zeros((D,)), 'ca_kv_ln_g': jnp.ones((D,)), 'ca_kv_ln_b': jnp.zeros((D,)), 'ca_in_w': _xavier(ks[4], (3 * D, D)), 'ca_in_b': jnp.zeros((3 * D,)), 'ca_out_w': _xavier(ks[5], (D, D)), 'ca_out_b': jnp.zeros((D,)), 'moe_ln_g': jnp.ones((D,)), 'moe_ln_b': jnp.zeros((D,)), 'router_w': _xavier(ks[6], (E, D)), 'router_b': jnp.zeros((E,)), 'e_fc1_w': jax.vmap(lambda k: _xavier(k, (DFF, D)))(jax.random.split(ks[7], E)), 'e_fc1_b': jnp.zeros((E, DFF)), 'e_fc2_w': jax.vmap(lambda k: _xavier(k, (D, DFF)))(jax.random.split(ks[8], E)), 'e_fc2_b': jnp.zeros((E, D))}
        return inp
    _L3_xattn_all = _L3_xattn_setup()
    _L3_xattn_in = {k: v for k, v in _L3_xattn_all.items() if k in ('sa_ln_g', 'sa_ln_b', 'sa_in_w', 'sa_in_b', 'sa_out_w', 'sa_out_b', 'ca_q_ln_g', 'ca_q_ln_b', 'ca_kv_ln_g', 'ca_kv_ln_b', 'ca_in_w', 'ca_in_b', 'ca_out_w', 'ca_out_b', 'moe_ln_g', 'moe_ln_b', 'router_w', 'router_b', 'e_fc1_w', 'e_fc1_b', 'e_fc2_w', 'e_fc2_b')}
    del _L3_xattn_all
    return {'x': x, 'ctx_1024': ctx_1024, 'mask_BxSx1_ff1': mask_BxSx1_ff1, 'mask_BxSx1024_bf0': mask_BxSx1024_bf0, 'mask_Bx1xSxS2_if1': mask_Bx1xSxS2_if1, 'mask_Bx1xSxS2_ik0': mask_Bx1xSxS2_ik0, 'L0_xattn_content_bias': _L0_xattn_in['content_bias'], 'L0_xattn_position_bias': _L0_xattn_in['position_bias'], 'L0_xattn_Wq': _L0_xattn_in['Wq'], 'L0_xattn_Wk': _L0_xattn_in['Wk'], 'L0_xattn_Wv': _L0_xattn_in['Wv'], 'L0_xattn_Wr': _L0_xattn_in['Wr'], 'L0_xattn_Wo': _L0_xattn_in['Wo'], 'L0_xattn_ln1_g': _L0_xattn_in['ln1_g'], 'L0_xattn_ln1_b': _L0_xattn_in['ln1_b'], 'L0_xattn_W1': _L0_xattn_in['W1'], 'L0_xattn_b1': _L0_xattn_in['b1'], 'L0_xattn_W2': _L0_xattn_in['W2'], 'L0_xattn_b2': _L0_xattn_in['b2'], 'L0_xattn_ln2_g': _L0_xattn_in['ln2_g'], 'L0_xattn_ln2_b': _L0_xattn_in['ln2_b'], 'L1_xattn_msa_Wv': _L1_xattn_in['msa_Wv'], 'L1_xattn_msa_Wk': _L1_xattn_in['msa_Wk'], 'L1_xattn_msa_Wq': _L1_xattn_in['msa_Wq'], 'L1_xattn_msa_Wo': _L1_xattn_in['msa_Wo'], 'L1_xattn_msa_bo': _L1_xattn_in['msa_bo'], 'L1_xattn_ca_Wv': _L1_xattn_in['ca_Wv'], 'L1_xattn_ca_Wk': _L1_xattn_in['ca_Wk'], 'L1_xattn_ca_Wq': _L1_xattn_in['ca_Wq'], 'L1_xattn_ca_Wo': _L1_xattn_in['ca_Wo'], 'L1_xattn_ca_bo': _L1_xattn_in['ca_bo'], 'L1_xattn_ff_W1': _L1_xattn_in['ff_W1'], 'L1_xattn_ff_b1': _L1_xattn_in['ff_b1'], 'L1_xattn_ff_W2': _L1_xattn_in['ff_W2'], 'L1_xattn_ff_b2': _L1_xattn_in['ff_b2'], 'L1_xattn_ln1_g': _L1_xattn_in['ln1_g'], 'L1_xattn_ln1_b': _L1_xattn_in['ln1_b'], 'L1_xattn_ln2_g': _L1_xattn_in['ln2_g'], 'L1_xattn_ln2_b': _L1_xattn_in['ln2_b'], 'L1_xattn_ln3_g': _L1_xattn_in['ln3_g'], 'L1_xattn_ln3_b': _L1_xattn_in['ln3_b'], 'L2_xattn_Wt': _L2_xattn_in['Wt'], 'L2_xattn_bt': _L2_xattn_in['bt'], 'L2_xattn_Wv': _L2_xattn_in['Wv'], 'L2_xattn_bv': _L2_xattn_in['bv'], 'L2_xattn_Wg': _L2_xattn_in['Wg'], 'L2_xattn_bg': _L2_xattn_in['bg'], 'L2_xattn_gamma': _L2_xattn_in['gamma'], 'L2_xattn_beta': _L2_xattn_in['beta'], 'L3_xattn_sa_ln_g': _L3_xattn_in['sa_ln_g'], 'L3_xattn_sa_ln_b': _L3_xattn_in['sa_ln_b'], 'L3_xattn_sa_in_w': _L3_xattn_in['sa_in_w'], 'L3_xattn_sa_in_b': _L3_xattn_in['sa_in_b'], 'L3_xattn_sa_out_w': _L3_xattn_in['sa_out_w'], 'L3_xattn_sa_out_b': _L3_xattn_in['sa_out_b'], 'L3_xattn_ca_q_ln_g': _L3_xattn_in['ca_q_ln_g'], 'L3_xattn_ca_q_ln_b': _L3_xattn_in['ca_q_ln_b'], 'L3_xattn_ca_kv_ln_g': _L3_xattn_in['ca_kv_ln_g'], 'L3_xattn_ca_kv_ln_b': _L3_xattn_in['ca_kv_ln_b'], 'L3_xattn_ca_in_w': _L3_xattn_in['ca_in_w'], 'L3_xattn_ca_in_b': _L3_xattn_in['ca_in_b'], 'L3_xattn_ca_out_w': _L3_xattn_in['ca_out_w'], 'L3_xattn_ca_out_b': _L3_xattn_in['ca_out_b'], 'L3_xattn_moe_ln_g': _L3_xattn_in['moe_ln_g'], 'L3_xattn_moe_ln_b': _L3_xattn_in['moe_ln_b'], 'L3_xattn_router_w': _L3_xattn_in['router_w'], 'L3_xattn_router_b': _L3_xattn_in['router_b'], 'L3_xattn_e_fc1_w': _L3_xattn_in['e_fc1_w'], 'L3_xattn_e_fc1_b': _L3_xattn_in['e_fc1_b'], 'L3_xattn_e_fc2_w': _L3_xattn_in['e_fc2_w'], 'L3_xattn_e_fc2_b': _L3_xattn_in['e_fc2_b']}

def reference(x, ctx_1024, mask_BxSx1_ff1, mask_BxSx1024_bf0, mask_Bx1xSxS2_if1, mask_Bx1xSxS2_ik0, L0_xattn_content_bias, L0_xattn_position_bias, L0_xattn_Wq, L0_xattn_Wk, L0_xattn_Wv, L0_xattn_Wr, L0_xattn_Wo, L0_xattn_ln1_g, L0_xattn_ln1_b, L0_xattn_W1, L0_xattn_b1, L0_xattn_W2, L0_xattn_b2, L0_xattn_ln2_g, L0_xattn_ln2_b, L1_xattn_msa_Wv, L1_xattn_msa_Wk, L1_xattn_msa_Wq, L1_xattn_msa_Wo, L1_xattn_msa_bo, L1_xattn_ca_Wv, L1_xattn_ca_Wk, L1_xattn_ca_Wq, L1_xattn_ca_Wo, L1_xattn_ca_bo, L1_xattn_ff_W1, L1_xattn_ff_b1, L1_xattn_ff_W2, L1_xattn_ff_b2, L1_xattn_ln1_g, L1_xattn_ln1_b, L1_xattn_ln2_g, L1_xattn_ln2_b, L1_xattn_ln3_g, L1_xattn_ln3_b, L2_xattn_Wt, L2_xattn_bt, L2_xattn_Wv, L2_xattn_bv, L2_xattn_Wg, L2_xattn_bg, L2_xattn_gamma, L2_xattn_beta, L3_xattn_sa_ln_g, L3_xattn_sa_ln_b, L3_xattn_sa_in_w, L3_xattn_sa_in_b, L3_xattn_sa_out_w, L3_xattn_sa_out_b, L3_xattn_ca_q_ln_g, L3_xattn_ca_q_ln_b, L3_xattn_ca_kv_ln_g, L3_xattn_ca_kv_ln_b, L3_xattn_ca_in_w, L3_xattn_ca_in_b, L3_xattn_ca_out_w, L3_xattn_ca_out_b, L3_xattn_moe_ln_g, L3_xattn_moe_ln_b, L3_xattn_router_w, L3_xattn_router_b, L3_xattn_e_fc1_w, L3_xattn_e_fc1_b, L3_xattn_e_fc2_w, L3_xattn_e_fc2_b):
    import jax
    import jax.numpy as jnp

    def _L0_xattn_ref(layer_input, memory, content_bias, position_bias, non_pad_mask, Wq, Wk, Wv, Wr, Wo, ln1_g, ln1_b, W1, b1, W2, b2, ln2_g, ln2_b, slf_attn_mask):
        import jax, jax.numpy as jnp
        import numpy as np
        B, Q, M, D, H, K = (4, 64, 64, 128, 16, 64)

        def layer_norm(x, g, b, eps=1e-05):
            mu = x.mean(-1, keepdims=True)
            var = ((x - mu) ** 2).mean(-1, keepdims=True)
            return (x - mu) * jax.lax.rsqrt(var + eps) * g + b

        def rel_shift(x):
            b, h, q, k = x.shape
            x = jnp.pad(x, ((0, 0), (0, 0), (0, 0), (1, 0)))
            x = x.reshape(b, h, k + 1, q)[:, :, 1:, :]
            return x.reshape(b, h, q, k)
        b, q_len, d_model = layer_input.shape
        n_head, d_head = content_bias.shape
        kv = jnp.concatenate([memory, layer_input], axis=1)
        kl = kv.shape[1]
        pos = jnp.arange(kl - 1, -1, -1, dtype=jnp.float32)
        inv_freq = 1.0 / 10000.0 ** (jnp.arange(0, d_model, 2, dtype=jnp.float32) / d_model)
        ang = pos[:, None] * inv_freq
        pe = jnp.concatenate([jnp.sin(ang), jnp.cos(ang)], axis=-1)
        q = (layer_input @ Wq).reshape(b, q_len, n_head, d_head)
        k = (kv @ Wk).reshape(b, kl, n_head, d_head)
        v = (kv @ Wv).reshape(b, kl, n_head, d_head)
        r = (pe @ Wr).reshape(kl, n_head, d_head)
        ac = jnp.einsum('bqhd,bkhd->bhqk', q + content_bias, k)
        bd = rel_shift(jnp.einsum('bqhd,khd->bhqk', q + position_bias, r))
        scores = (ac + bd) * (1.0 / np.sqrt(d_head))
        scores = jnp.where(slf_attn_mask[:, None, :, :], jnp.float32(-1000000000.0), scores)
        attn = jax.nn.softmax(scores, axis=-1)
        ctx = jnp.einsum('bhqk,bkhd->bqhd', attn, v).reshape(b, q_len, n_head * d_head)
        out = layer_norm(layer_input + ctx @ Wo, ln1_g, ln1_b)
        out = out * non_pad_mask
        h = jax.nn.relu(out @ W1 + b1)
        out = layer_norm(out + (h @ W2 + b2), ln2_g, ln2_b)
        return out * non_pad_mask

    def _L1_xattn_ref(x, encoder_output, src_mask, tgt_mask, msa_Wv, msa_Wk, msa_Wq, msa_Wo, msa_bo, ca_Wv, ca_Wk, ca_Wq, ca_Wo, ca_bo, ff_W1, ff_b1, ff_W2, ff_b2, ln1_g, ln1_b, ln2_g, ln2_b, ln3_g, ln3_b):
        import jax, jax.numpy as jnp
        import numpy as np
        B, S, E, H, FF = (2, 256, 128, 16, 512)
        HD = E // H
        EPS = 1e-05

        def _layernorm(x, g, b):
            mu = jnp.mean(x, axis=-1, keepdims=True)
            var = jnp.mean(jnp.square(x - mu), axis=-1, keepdims=True)
            return (x - mu) * jax.lax.rsqrt(var + EPS) * g + b

        def _attention(v_in, k_in, q_in, mask, Wv, Wk, Wq, Wo, bo):
            N, Sk, _ = k_in.shape
            Sq = q_in.shape[1]
            v = v_in.reshape(N, Sk, H, HD)
            k = k_in.reshape(N, Sk, H, HD)
            q = q_in.reshape(N, Sq, H, HD)
            v = jnp.einsum('nkhd,ed->nkhe', v, Wv)
            k = jnp.einsum('nkhd,ed->nkhe', k, Wk)
            q = jnp.einsum('nqhd,ed->nqhe', q, Wq)
            energy = jnp.einsum('nqhd,nkhd->nhqk', q, k)
            energy = jnp.where(mask == 0, jnp.float32(-1e+20), energy)
            attn = jax.nn.softmax(energy / jnp.sqrt(jnp.float32(E)), axis=-1)
            out = jnp.einsum('nhqk,nkhd->nqhd', attn, v).reshape(N, Sq, E)
            return out @ Wo.T + bo
        sa = _attention(x, x, x, tgt_mask, msa_Wv, msa_Wk, msa_Wq, msa_Wo, msa_bo)
        out = _layernorm(x + sa, ln1_g, ln1_b)
        ca = _attention(encoder_output, encoder_output, out, src_mask, ca_Wv, ca_Wk, ca_Wq, ca_Wo, ca_bo)
        out = _layernorm(out + ca, ln2_g, ln2_b)
        h = jax.nn.relu(out @ ff_W1.T + ff_b1)
        ff = h @ ff_W2.T + ff_b2
        out = _layernorm(out + ff, ln3_g, ln3_b)
        return out

    def _L2_xattn_ref(text_feat, vision_feat, Wt, bt, Wv, bv, Wg, bg, gamma, beta):
        import jax, jax.numpy as jnp
        import numpy as np
        NUM_ITERATIONS = 3
        LN_EPS = 1e-05
        B, L, H = text_feat.shape
        vision_pooled = jnp.mean(vision_feat, axis=1, keepdims=True)
        text_proj = jnp.einsum('blh,oh->blo', text_feat, Wt) + bt
        vision_proj = jnp.einsum('bkh,oh->bko', vision_pooled, Wv) + bv
        vision_proj = jnp.broadcast_to(vision_proj, (B, L, H))
        agreement = jnp.sum(text_proj * vision_proj, axis=-1, keepdims=True)
        coupling = jnp.zeros((B, L, 1), dtype=text_feat.dtype)
        fused = text_feat
        for _ in range(NUM_ITERATIONS):
            routing_weights = jax.nn.softmax(coupling, axis=1)
            weighted_vision = routing_weights * vision_proj
            Wg_t, Wg_v = (Wg[:, :H], Wg[:, H:])
            gate_pre = jnp.einsum('blh,oh->blo', text_proj, Wg_t) + jnp.einsum('blh,oh->blo', weighted_vision, Wg_v) + bg
            gate = jax.nn.sigmoid(gate_pre)
            fused = text_feat + gate * weighted_vision
            coupling = coupling + agreement
        mu = jnp.mean(fused, axis=-1, keepdims=True)
        var = jnp.mean(jnp.square(fused - mu), axis=-1, keepdims=True)
        out = (fused - mu) / jnp.sqrt(var + LN_EPS) * gamma + beta
        return out

    def _L3_xattn_ref(latents, tokens, sa_ln_g, sa_ln_b, sa_in_w, sa_in_b, sa_out_w, sa_out_b, ca_q_ln_g, ca_q_ln_b, ca_kv_ln_g, ca_kv_ln_b, ca_in_w, ca_in_b, ca_out_w, ca_out_b, moe_ln_g, moe_ln_b, router_w, router_b, e_fc1_w, e_fc1_b, e_fc2_w, e_fc2_b):
        import jax, jax.numpy as jnp
        import numpy as np
        D, H, E, K, DFF = (128, 16, 8, 2, 512)
        B, L, T = (4, 64, 256)
        EPS = 1e-05

        def _xavier(key, shape):
            fan_in, fan_out = (shape[-1], shape[-2])
            a = jnp.sqrt(6.0 / (fan_in + fan_out))
            return jax.random.uniform(key, shape, jnp.float32, -a, a)

        def _ln(x, g, b):
            m = x.mean(-1, keepdims=True)
            v = ((x - m) ** 2).mean(-1, keepdims=True)
            return (x - m) / jnp.sqrt(v + EPS) * g + b

        def _mha(q_in, kv_in, in_w, in_b, out_w, out_b):
            wq, wk, wv = jnp.split(in_w, 3, axis=0)
            bq, bk, bv = jnp.split(in_b, 3, axis=0)
            dh = D // H

            def heads(x, w, b):
                y = x @ w.T + b
                return y.reshape(x.shape[0], x.shape[1], H, dh).transpose(0, 2, 1, 3)
            q = heads(q_in, wq, bq)
            k = heads(kv_in, wk, bk)
            v = heads(kv_in, wv, bv)
            scores = jnp.einsum('bhqd,bhkd->bhqk', q, k) / jnp.sqrt(jnp.float32(dh))
            attn = jax.nn.softmax(scores, axis=-1)
            out = jnp.einsum('bhqk,bhkd->bhqd', attn, v)
            out = out.transpose(0, 2, 1, 3).reshape(q_in.shape[0], q_in.shape[1], D)
            return out @ out_w.T + out_b

        def _fuse_moe(x, ln_g, ln_b, rw, rb, fc1_w, fc1_b, fc2_w, fc2_b):
            h = _ln(x, ln_g, ln_b)
            logits = h @ rw.T + rb
            vals, idx = jax.lax.top_k(logits, K)
            gates = jax.nn.softmax(vals, axis=-1)
            N = x.shape[0] * x.shape[1]
            hf = h.reshape(N, D)
            h1 = jax.nn.gelu(jnp.einsum('nd,efd->enf', hf, fc1_w) + fc1_b[:, None, :], approximate=False)
            eo = jnp.einsum('enf,edf->end', h1, fc2_w) + fc2_b[:, None, :]
            idx_f = idx.reshape(N, K)
            gates_f = gates.reshape(N, K)
            gathered = eo[idx_f, jnp.arange(N)[:, None], :]
            mixed = (gathered * gates_f[..., None]).sum(axis=1).reshape(x.shape)
            return x + mixed
        q = _ln(latents, sa_ln_g, sa_ln_b)
        x = latents + _mha(q, q, sa_in_w, sa_in_b, sa_out_w, sa_out_b)
        qc = _ln(x, ca_q_ln_g, ca_q_ln_b)
        kv = _ln(tokens, ca_kv_ln_g, ca_kv_ln_b)
        x = x + _mha(qc, kv, ca_in_w, ca_in_b, ca_out_w, ca_out_b)
        return _fuse_moe(x, moe_ln_g, moe_ln_b, router_w, router_b, e_fc1_w, e_fc1_b, e_fc2_w, e_fc2_b)
    x = _L0_xattn_ref(x, ctx_1024, L0_xattn_content_bias, L0_xattn_position_bias, mask_BxSx1_ff1, L0_xattn_Wq, L0_xattn_Wk, L0_xattn_Wv, L0_xattn_Wr, L0_xattn_Wo, L0_xattn_ln1_g, L0_xattn_ln1_b, L0_xattn_W1, L0_xattn_b1, L0_xattn_W2, L0_xattn_b2, L0_xattn_ln2_g, L0_xattn_ln2_b, mask_BxSx1024_bf0)
    x = _L1_xattn_ref(x, ctx_1024, mask_Bx1xSxS2_if1, mask_Bx1xSxS2_ik0, L1_xattn_msa_Wv, L1_xattn_msa_Wk, L1_xattn_msa_Wq, L1_xattn_msa_Wo, L1_xattn_msa_bo, L1_xattn_ca_Wv, L1_xattn_ca_Wk, L1_xattn_ca_Wq, L1_xattn_ca_Wo, L1_xattn_ca_bo, L1_xattn_ff_W1, L1_xattn_ff_b1, L1_xattn_ff_W2, L1_xattn_ff_b2, L1_xattn_ln1_g, L1_xattn_ln1_b, L1_xattn_ln2_g, L1_xattn_ln2_b, L1_xattn_ln3_g, L1_xattn_ln3_b)
    x = _L2_xattn_ref(x, ctx_1024, L2_xattn_Wt, L2_xattn_bt, L2_xattn_Wv, L2_xattn_bv, L2_xattn_Wg, L2_xattn_bg, L2_xattn_gamma, L2_xattn_beta)
    x = _L3_xattn_ref(x, ctx_1024, L3_xattn_sa_ln_g, L3_xattn_sa_ln_b, L3_xattn_sa_in_w, L3_xattn_sa_in_b, L3_xattn_sa_out_w, L3_xattn_sa_out_b, L3_xattn_ca_q_ln_g, L3_xattn_ca_q_ln_b, L3_xattn_ca_kv_ln_g, L3_xattn_ca_kv_ln_b, L3_xattn_ca_in_w, L3_xattn_ca_in_b, L3_xattn_ca_out_w, L3_xattn_ca_out_b, L3_xattn_moe_ln_g, L3_xattn_moe_ln_b, L3_xattn_router_w, L3_xattn_router_b, L3_xattn_e_fc1_w, L3_xattn_e_fc1_b, L3_xattn_e_fc2_w, L3_xattn_e_fc2_b)
    return x

_drawn_inputs = setup_inputs


def setup_inputs(seed=0):
    import zlib

    import numpy as np

    out = dict(_drawn_inputs(seed))
    spreads = {'L0_xattn_ln1_g': (1.0, 0.2),
     'L0_xattn_ln1_b': (0.0, 0.1),
     'L0_xattn_b1': (0.0, 0.1),
     'L0_xattn_b2': (0.0, 0.1),
     'L0_xattn_ln2_g': (1.0, 0.2),
     'L0_xattn_ln2_b': (0.0, 0.1),
     'L1_xattn_msa_bo': (0.0, 0.1),
     'L1_xattn_ca_bo': (0.0, 0.1),
     'L1_xattn_ff_b1': (0.0, 0.1),
     'L1_xattn_ff_b2': (0.0, 0.1),
     'L1_xattn_ln1_g': (1.0, 0.2),
     'L1_xattn_ln1_b': (0.0, 0.1),
     'L1_xattn_ln2_g': (1.0, 0.2),
     'L1_xattn_ln2_b': (0.0, 0.1),
     'L1_xattn_ln3_g': (1.0, 0.2),
     'L1_xattn_ln3_b': (0.0, 0.1),
     'L2_xattn_gamma': (1.0, 0.2),
     'L2_xattn_beta': (0.0, 0.1),
     'L3_xattn_sa_ln_g': (1.0, 0.2),
     'L3_xattn_sa_ln_b': (0.0, 0.1),
     'L3_xattn_sa_in_b': (0.0, 0.1),
     'L3_xattn_sa_out_b': (0.0, 0.1),
     'L3_xattn_ca_q_ln_g': (1.0, 0.2),
     'L3_xattn_ca_q_ln_b': (0.0, 0.359),
     'L3_xattn_ca_kv_ln_g': (1.0, 0.2),
     'L3_xattn_ca_kv_ln_b': (0.0, 0.1),
     'L3_xattn_ca_in_b': (0.0, 0.1),
     'L3_xattn_ca_out_b': (0.0, 0.1),
     'L3_xattn_moe_ln_g': (1.0, 0.2),
     'L3_xattn_moe_ln_b': (0.0, 0.1),
     'L3_xattn_router_b': (0.0, 0.1),
     'L3_xattn_e_fc1_b': (0.0, 0.1),
     'L3_xattn_e_fc2_b': (0.0, 0.1)}
    factors = {'L0_xattn_content_bias': 8.0,
     'L0_xattn_position_bias': 33.981,
     'L0_xattn_Wq': 7.975,
     'L0_xattn_Wk': 8.0,
     'L0_xattn_Wr': 8.0,
     'L1_xattn_msa_Wv': 2.926,
     'L1_xattn_msa_Wk': 49.167,
     'L1_xattn_msa_Wq': 45.249,
     'L1_xattn_msa_Wo': 3.583,
     'L1_xattn_ca_Wv': 2.863,
     'L1_xattn_ca_Wk': 64.0,
     'L1_xattn_ca_Wq': 58.991,
     'L1_xattn_ca_Wo': 2.849,
     'L2_xattn_Wt': 3.252,
     'L2_xattn_bt': 32.344,
     'L2_xattn_Wv': 3.287,
     'L2_xattn_bv': 5.87,
     'L2_xattn_Wg': 8.0,
     'L2_xattn_bg': 64.0}
    for name, (base, spread) in spreads.items():
        noise = np.random.default_rng([zlib.crc32(name.encode()), seed]).standard_normal(out[name].shape)
        drawn = base * np.exp(spread * noise) if base else spread * noise
        out[name] = jnp.asarray(drawn.astype(out[name].dtype))
    for name, factor in factors.items():
        out[name] = (out[name] * factor).astype(out[name].dtype)
    return out
```

```python
from contextlib import ExitStack

import numpy as np

import concourse.bass as bass
from concourse import mybir

F32 = mybir.dt.float32
BF16 = mybir.dt.bfloat16
U8 = mybir.dt.uint8
I32 = mybir.dt.int32
U32 = mybir.dt.uint32
ALU = mybir.AluOpType
ACT = mybir.ActivationFunctionType
AX = mybir.AxisListType

P = 128
S = 64
D = 128
H = 16
KL = 128
DK = 64
HD = D // H
FF = 512
FC = FF // P
NE = 8
QT = 4
EPS = 1e-5
MASKED = -1e20
LOWEST = -3e38

COLS = {}
for _name, _n in (("l0_b1", FC), ("l1_b1", FC), ("bt", 1), ("bv", 1), ("bg", 1), ("sa_g", 1), ("sa_b", 1),
                  ("caq_g", 1), ("caq_b", 1), ("cakv_g", 1), ("cakv_b", 1), ("moe_g", 1), ("moe_b", 1),
                  ("sa_bq", 1), ("sa_bk", 1), ("ca_bq", 1), ("ca_bk", 1), ("e_b1", NE * FC),
                  ("group", 4), ("place", 4)):
    COLS[_name] = (sum(n for _, n in COLS.values()), _n)
NCOLS = sum(n for _, n in COLS.values())
ROWS = ("ln01_g", "ln01_b", "l0_b2", "ln02_g", "ln02_b", "msa_bo", "ln11_g", "ln11_b", "ca1_bo", "ln12_g",
        "ln12_b", "l1_b2", "ln13_g", "ln13_b", "l2_g", "l2_b", "sa_bv", "sa_bo", "ca_bv", "ca_bo", "misc")


def wait(e, sem, value):
    if not (isinstance(value, int) and value <= 0):
        e.wait_ge(sem, value)


def wait_alone(e, sem, value):
    wait(e, sem, value)
    e.nop(nofuse=True)


def opening(k):
    return isinstance(k, int) and k == -1


def walk(e, units, step):
    step(-1, 0, True, False, False)
    step(-1, 1, True, True, False)
    with e.Fori(0, units // 2 - 1) as k:
        step(k, 0, True, True, True)
        step(k, 1, True, True, True)
    step(units // 2 - 1, 0, False, True, True)
    step(units // 2 - 1, 1, False, False, True)


def walk_late(e, units, step):
    step(-1, 0, True, False, False, False)
    step(-1, 1, True, True, False, False)
    step(0, 0, True, True, True, False)
    step(0, 1, True, True, True, True)
    with e.Fori(1, units // 2 - 1) as k:
        step(k, 0, True, True, True, True)
        step(k, 1, True, True, True, True)
    step(units // 2 - 1, 0, False, True, True, True)
    step(units // 2 - 1, 1, False, False, True, True)
    step(units // 2, 0, False, False, False, True)


def build(nc, a, out, phases=None):
    NB = a["x"].shape[0]
    NT = NB * S // P
    NQ = NT // QT
    ctx = ExitStack()
    with ctx:
        def sb(name, shape, dt=F32):
            return ctx.enter_context(nc.sbuf_tensor("sb_" + name, shape, dt))

        sems = {}

        def sem(name):
            if name not in sems:
                sems[name] = ctx.enter_context(nc.semaphore("is_" + name))
            return sems[name]

        PS = ctx.enter_context(nc.psum_tensor("PS", [P, 8, 512], F32))
        X = sb("X", [P, NT, D])
        cols = sb("cols", [P, NCOLS])
        rows = sb("rows", [P, len(ROWS), D])
        ident = sb("ident", [P, P])
        twice = sb("twice", [S, P], BF16)
        token_mask = sb("token_mask", [P, NT])
        half_power = sb("half_power", [P, QT])
        w_l0ff1 = sb("w_l0ff1", [P, FF])
        w_l0ff2 = sb("w_l0ff2", [P, FC, D])
        w_l1ff1 = sb("w_l1ff1", [P, FF])
        w_l1ff2 = sb("w_l1ff2", [P, FC, D])
        w_att = {n: sb("w_" + n, [P, 3, D]) for n in ("msa", "ca1", "sa", "ca")}
        w_out = {n: sb("wo_" + n, [S, 2, D]) for n in ("msa", "ca1", "sa", "ca")}
        w_l2 = sb("w_l2", [P, 4, D])
        w_router = sb("w_router", [P, NE])
        w_eb2 = sb("w_eb2", [NE, D])
        pooled = sb("pooled", [P, NB])
        tables = sb("tables", [P, 3, H, P])
        w_e1 = sb("w_e1", [P, NE, FF])
        w_e2 = sb("w_e2", [P, NE, FC, D])
        work = sb("work", [P, 19600])

        def col(name):
            at, n = COLS[name]
            return cols[:, at:at + n]

        def row(name):
            return rows[:, ROWS.index(name), :]

        taken = [0]

        def carve(shape, start=None):
            if start is not None:
                taken[0] = start
            n = int(np.prod(shape))
            v = work[:, taken[0]:taken[0] + n]
            taken[0] += n
            assert taken[0] <= 19600, taken[0]
            if len(shape) == 2:
                v = v.rearrange("p (a b) -> p a b", a=shape[0])
            elif len(shape) == 3:
                v = v.rearrange("p (a b c) -> p a b c", a=shape[0], b=shape[1])
            elif len(shape) == 4:
                v = v.rearrange("p (a b c d) -> p a b c d", a=shape[0], b=shape[1], c=shape[2])
            return v

        loads = [(cols[:, :], a["cols"]), (rows[:, :, :], a["rows"].partition_broadcast(P)),
                 (ident[:, :], a["ident"]), (token_mask[:, :], a["token_mask"]),
                 (w_l0ff1[:, :], a["l0_W1"]), (w_l0ff2[:, :, :], a["l0_W2"]),
                 (w_l1ff1[:, :], a["l1_W1"]), (w_l1ff2[:, :, :], a["l1_W2"]),
                 (w_l2[:, :, :], a["l2_W"]), (w_router[:, :], a["router"]), (w_eb2[:, :], a["e_b2"]),
                 (X[:, :, :], a["x"].rearrange("(t b) s d -> (b s) t d", b=2))]
        loads += [(w_att[n][:, :, :], a["w_" + n]) for n in w_att]
        loads += [(w_out[n][:, :, :], a["wo_" + n]) for n in w_out]

        def meet(e, phase):
            e.drain().then_inc(sem("phase_done"), 1)
            e.wait_ge(sem("phase_done"), 5 * (phase + 1))

        QK, QR, VO = (tables[:, i] for i in range(3))
        wqT = carve((H, P), 0)[0:DK]
        wkT = carve((H, P))[0:DK]
        wvT = carve((H, P))[0:DK]
        wo0 = carve((H, P))[0:DK]
        wr = carve((H, DK))
        peT = carve((KL,))
        rT = carve((H, KL))[0:DK]
        cbT = carve((H,))[0:DK]
        pbT = carve((H,))[0:DK]
        pb_wide = carve((H, P))[0:DK]
        key_bias = sb("key_bias", [P, H])
        rel_bias = sb("rel_bias", [P, H, KL])
        l0_loads = [(wqT, a["l0_WqT"]), (wkT, a["l0_WkT"]), (wvT, a["l0_WvT"]), (wo0, a["l0_Wo"]),
                    (wr, a["l0_Wr"]), (peT, a["peT"]), (cbT, a["l0_cb"]), (pbT, a["l0_pb"])]

        kv_tok = carve((2, 2, D), 0)
        kvT = carve((2, 2, 2, S))
        qkT = carve((2, H, S))
        rel_sb = carve((H, KL + 1))
        rel_shifted = carve((2, 8, KL))
        probs = carve((2, 2, 8, KL))
        probsT = carve((2, 8 * P))
        pkvT = carve((H, P))
        row_max = carve((2, 2, 8))
        neg_max = carve((2, 2, 8))
        row_sum = carve((2, 2, 8))
        row_inv = carve((2, 2, 8))
        mask8 = ctx.enter_context(nc.sbuf_tensor("mask8", [S, 2, 2, KL], U8))
        mask_bias = ctx.enter_context(nc.sbuf_tensor("mask_bias", [S, 2, 2, KL], BF16))
        scratch = nc.dram_tensor("rel_scratch", [2, H, S * (KL + 1)], F32, kind="Internal").ap()
        SCALE0 = float(DK) ** -0.5
        ctx_in, x_in = a["ctx"], a["x"]

        def use_head(m):
            return m if isinstance(m, int) and m < 2 else 9 * m

        def use_rel(m, g):
            return 2 + g if isinstance(m, int) and m == 0 else 9 * m + 1 + g

        def use_qk(m, g):
            return use_rel(m, g) + 4

        def l0_sync(e, c):
            for i, (dst, src) in enumerate(l0_loads):
                e.dma_start(dst, src).then_inc(sem("l0_weights_loaded"), 16)
            for dst, src in loads:
                e.dma_start(dst, src).then_inc(sem("params_loaded"), 16)
            e.wait_ge(sem("params_loaded"), 16 * len(loads))
            for dst, src in ((w_e1[:, :, :], a["e_W1"]), (w_e2[:, :, :, :], a["e_W2"])):
                e.dma_start(dst, src).then_inc(sem("experts_loaded"), 16)
            meet(e, 0)

            def load_tokens(k, u, m):
                wait_alone(e, sem("l0_context_done"), 8 * (m - 1))
                wait_alone(e, sem("l0_mask_ready"), m - 1)
                e.dma_start(kv_tok[0:S, u], ctx_in[bass.ds(2 * m, 2)].rearrange("b s d -> s b d"))\
                    .then_inc(sem(f"l0_kv_loaded{u}"), 16)
                e.dma_start(kv_tok[S:P, u], x_in[bass.ds(2 * m, 2)].rearrange("b s d -> s b d"))\
                    .then_inc(sem(f"l0_kv_loaded{u}"), 16)
                e.dma_start(mask8[:, u], a["mask0"][bass.ds(2 * m, 2)].rearrange("b s k -> s b k"))\
                    .then_inc(sem(f"l0_mask_loaded{u}"), 16)

            def shift_relative(m):
                wait_alone(e, sem("l0_projections_drained"), use_rel(m, 3) + 1)
                wait_alone(e, sem("l0_rel_read"), 32 * m)
                for b in range(2):
                    e.dma_start(scratch[b].rearrange("h (q c) -> q h c", q=S), rel_sb[S * b:S * b + S])\
                        .then_inc(sem("l0_rel_written"), 16)
                wait_alone(e, sem("l0_rel_written"), 32 * m + 32)
                wait_alone(e, sem("l0_rows_done"), 4 * m)
                for hh in range(2):
                    src = scratch[:, :, S:S + S * KL].rearrange("b (n two) (q k) -> two q (b n) k", two=2, q=S)
                    e.dma_start(rel_shifted[S * hh:S * hh + S].rearrange("p b n k -> p (b n) k"), src[hh])\
                        .then_inc(sem("l0_rel_read"), 16)

            def step(k, u, head, front, back):
                n = 2 * k + u
                if head and opening(k):
                    load_tokens(k, u, n + 2)
                if front:
                    shift_relative(n + 1)
                if head and not opening(k):
                    load_tokens(k, u, n + 2)
            walk(e, NT, step)

        def l0_pool(e, c):
            e.memset(half_power[:, :], -0.5)
            e.wait_ge(sem("params_loaded"), 16 * len(loads))
            for i in range(2):
                e.tensor_copy(twice[:, S * i:S * i + S], ident[0:S, 0:S])
            meet(e, 0)
            e.memset(rel_sb[:, :, 0:1], 0.0).then_inc(sem("l0_rel_pad"), 1)

            def step(k, u, head, front, back):
                if head:
                    m = 2 * k + u + 2
                    e.wait_ge(sem(f"l0_mask_loaded{u}"), 16 * (k + 2))
                    wait_alone(e, sem("l0_rows_done"), 4 * (m - 1))
                    e.tensor_scalar(mask_bias[:, u], mask8[:, u], MASKED, None, ALU.mult)\
                        .then_inc(sem("l0_mask_ready"), 1)
            walk(e, NT, step)

        def l0_tensor(e, c):
            e.wait_ge(sem("l0_weights_loaded"), 16 * len(l0_loads))
            used = [0]

            def bank():
                n = used[0]
                used[0] += 1
                wait(e, sem("l0_table_drained"), n - 1)
                return PS[:, n % 2]
            e.wait_ge(sem("l0_pb_wide"), 1)
            for q in range(4):
                o = bank()
                for i in range(4):
                    h = 4 * q + i
                    ins = e.matmul(o[0:DK, i * KL:(i + 1) * KL], wr[:, h], peT, start=True, stop=True)
                ins.then_inc(sem("l0_table_done"), 1)
            o = bank()
            for h in range(H):
                ins = e.matmul(o[:, h:h + 1], wkT[:, h], cbT[:, h:h + 1], start=True, stop=True)
            ins.then_inc(sem("l0_table_done"), 1)
            e.wait_ge(sem("l0_table_drained"), 4)
            for left, right in ((wqT, wkT), (wvT, wo0), (wqT, rT), (pb_wide, rT)):
                for q in range(4):
                    o = bank()
                    for i in range(4):
                        h = 4 * q + i
                        ins = e.matmul(o[:, i * P:(i + 1) * P], left[:, h], right[:, h], start=True, stop=True)
                    ins.then_inc(sem("l0_table_done"), 1)
            meet(e, 0)

            def step(k, u, head, front, back):
                n = 2 * k + u
                m, v = n + 1, 1 - u
                if opening(k):
                    transpose_kv(k, u, n + 2)
                shift = 0 if opening(k) else u
                if front:
                    e.wait_ge(sem("l0_projections_drained"), use_head(m) + 1)
                    for g in range(4):
                        wait(e, sem("l0_projections_drained"), use_rel(m, g) - 1)
                        e.matmul(PS[:, (shift + g) % 2], kvT[:, v, 1], QR[:, 4 * g:4 * g + 4],
                                 start=True, stop=True).then_inc(sem("l0_projected"), 1)

                def drained(j):
                    if j == 0:
                        wait(e, sem("l0_context_drained"), 8 * n)
                    elif j == 1:
                        wait(e, sem("l0_out_added"), n)
                    else:
                        wait(e, sem("l0_context_drained"), 8 * n + j - 1)
                    return PS[:, 2 + (u + j) % 2]

                def transpose_probs(b):
                    e.wait_ge(sem("l0_probs_ready"), 2 * n + b + 1)
                    for g in range(2):
                        o = drained(2 * b + g)
                        for i in range(4):
                            ins = e.transpose(o[:, i * P:i * P + P], probs[:, u, b, 4 * g + i], ident[:, :])
                        ins.then_inc(sem("l0_context_done"), 1)
                if back:
                    transpose_probs(0)
                if front:
                    for g in range(4):
                        wait(e, sem("l0_projections_drained"), use_qk(m, g) - 1)
                        for i in range(4):
                            ins = e.matmul(PS[:, (shift + g) % 2, i * P:i * P + P], QK[:, 4 * g + i],
                                           kvT[:, v, 1], start=True, stop=True)
                        ins.then_inc(sem("l0_projected"), 1)
                if back:
                    transpose_probs(1)
                    for g in range(2):
                        for b in range(2):
                            o = drained(4 + 2 * g + b)
                            e.wait_ge(sem("l0_context_drained"), 8 * n + 2 * b + g + 1)
                            e.matmul(o, kv_tok[:, u, b], probsT[:, b, 512 * g:512 * g + 512], start=True, stop=True)\
                                .then_inc(sem("l0_context_done"), 1)
                    o = drained(8)
                    for h in range(H):
                        if h % 8 == 0:
                            e.wait_ge(sem("l0_context_drained"), 8 * n + 6 + h // 4)
                        ins = e.matmul(o[:, 0:D], pkvT[:, h], VO[:, h], start=(h == 0), stop=(h == H - 1))
                    ins.then_inc(sem("l0_out_done"), 1)
                if front:
                    e.wait_ge(sem("l0_projections_drained"), use_qk(m, 3) + 1)
                    e.wait_ge(sem("l0_mask_ready"), m + 1)
                    for g in range(4):
                        b = g // 2
                        if g == 2 and head and not opening(k):
                            transpose_kv(k, u, n + 2)
                        o = PS[:, 4 + g]
                        wait(e, sem("l0_rows_done"), 4 * (m - 1) + g + 1)
                        e.matmul(o.rearrange("p (i k) -> p i k", i=4), twice[:, :],
                                 mask_bias[:, v, b].unsqueeze(1).to_broadcast([S, 4, KL]),
                                 start=True, stop=False, skip_group_check=True)
                        for i in range(4):
                            h = 8 * (g % 2) + 2 * i
                            ins = e.matmul(o[:, i * KL:i * KL + KL], qkT[:, b, h:h + 2],
                                           kvT[:, v, :, b], start=False, stop=(i == 3), skip_group_check=True)
                        ins.then_inc(sem("l0_scores_done"), 1)

            def transpose_kv(k, u, m):
                e.wait_ge(sem(f"l0_kv_loaded{u}"), 32 * (k + 2))
                wait(e, sem("l0_projections_drained"), use_head(m) - 1)
                for b in range(2):
                    ins = e.transpose(PS[:, u, b * P:b * P + P], kv_tok[:, u, b], ident[:, :])
                ins.then_inc(sem("l0_projected"), 1)
            walk(e, NT, step)

        def l0_vector(e, c):
            e.wait_ge(sem("l0_weights_loaded"), 16 * len(l0_loads))
            e.tensor_copy(pb_wide, pbT.unsqueeze(2).to_broadcast([DK, H, P])).then_inc(sem("l0_pb_wide"), 1)
            n = 0
            for q in range(4):
                e.wait_ge(sem("l0_table_done"), n + 1)
                e.tensor_copy(rT[:, 4 * q:4 * q + 4], PS[0:DK, n % 2].rearrange("p (i k) -> p i k", i=4))\
                    .then_inc(sem("l0_table_drained"), 1)
                n += 1
            e.wait_ge(sem("l0_table_done"), n + 1)
            e.tensor_copy(key_bias[:, :], PS[:, n % 2, 0:H]).then_inc(sem("l0_table_drained"), 1)
            n += 1
            for table in (QK, VO, QR, rel_bias):
                for q in range(4):
                    e.wait_ge(sem("l0_table_done"), n + 1)
                    e.tensor_copy(table[:, 4 * q:4 * q + 4], PS[:, n % 2].rearrange("p (i k) -> p i k", i=4))\
                        .then_inc(sem("l0_table_drained"), 1)
                    n += 1
            meet(e, 0)
            e.wait_ge(sem("l0_rel_pad"), 1)

            def keep_kvT(m, u):
                e.wait_ge(sem("l0_projected"), use_head(m) + 1)
                wait(e, sem("l0_scores_done"), 4 * (m - 1))
                e.tensor_copy(kvT[:, u], PS[:, u, 0:2 * KL].rearrange("p (b a k) -> p a b k", b=2, a=2))\
                    .then_inc(sem("l0_projections_drained"), 1)

            def step(k, u, head, front, back):
                n = 2 * k + u
                m, v = n + 1, 1 - u
                shift = 0 if opening(k) else u
                if opening(k):
                    keep_kvT(n + 2, u)

                def normalise(b):
                    e.wait_ge(sem("l0_exp_done"), 2 * n + b + 1)
                    e.reciprocal(row_inv[:, u, b], row_sum[:, u, b]).then_inc(sem("l0_inv_ready"), 1)
                    e.wait_ge(sem("l0_inv_ready"), 2 * n + b + 1)
                    e.tensor_tensor(probs[:, u, b], probs[:, u, b],
                                    row_inv[:, u, b].unsqueeze(2).to_broadcast([P, 8, KL]), ALU.mult)\
                        .then_inc(sem("l0_probs_ready"), 1)
                if front:
                    wait(e, sem("l0_rel_written"), 32 * m)
                    for g in range(4):
                        if g == 2 and back:
                            normalise(0)
                        e.wait_ge(sem("l0_projected"), use_rel(m, g) + 1)
                        e.tensor_tensor(rel_sb[:, 4 * g:4 * g + 4, 1:KL + 1],
                                        PS[:, (shift + g) % 2].rearrange("p (i k) -> p i k", i=4),
                                        rel_bias[:, 4 * g:4 * g + 4], ALU.add)\
                            .then_inc(sem("l0_projections_drained"), 1)
                if back:
                    if not front:
                        normalise(0)
                    normalise(1)
                if front:
                    wait(e, sem("l0_scores_done"), 4 * m)
                    for g in range(4):
                        e.wait_ge(sem("l0_projected"), use_qk(m, g) + 1)
                        e.tensor_tensor(qkT[:, :, 4 * g:4 * g + 4].rearrange("p b i q -> p i b q"),
                                        PS[:, (shift + g) % 2].rearrange("p (i b q) -> p i b q", i=4, b=2),
                                        key_bias[:, 4 * g:4 * g + 4].unsqueeze(2).unsqueeze(3)
                                        .to_broadcast([P, 4, 2, S]), ALU.add)\
                            .then_inc(sem("l0_projections_drained"), 1)
                if back:
                    e.wait_ge(sem("l0_out_done"), n + 1)
                    xn = X[:, bass.ds(n, 1)].rearrange("p a d -> p (a d)")
                    e.tensor_tensor(xn, xn, PS[:, 2 + u, 0:D], ALU.add).then_inc(sem("l0_out_added"), 1)
                if front:
                    e.wait_ge(sem("l0_rel_read"), 32 * m + 32)
                    for g in range(4):
                        b = g // 2
                        wait_alone(e, sem("l0_scores_done"), 4 * m + g + 1)
                        for i in range(4):
                            hp = 4 * (g % 2) + i
                            ins = e.tensor_tensor_reduce(probs[:, v, b, hp], PS[:, 4 + g, i * KL:i * KL + KL],
                                                         rel_shifted[:, b, hp], 1.0, LOWEST, ALU.add, ALU.max,
                                                         row_max[:, v, b, hp:hp + 1])
                        ins.then_inc(sem("l0_rows_done"), 1)
                        if g % 2:
                            e.wait_ge(sem("l0_rows_done"), 4 * m + g + 1)
                            e.tensor_scalar(neg_max[:, v, b], row_max[:, v, b], -SCALE0, None, ALU.mult)\
                                .then_inc(sem("l0_max_ready"), 1)
                        if g == 1 and head and not opening(k):
                            keep_kvT(n + 2, u)
            walk(e, NT, step)

        def l0_scalar(e, c):
            meet(e, 0)

            def step(k, u, head, front, back):
                n = 2 * k + u
                if back:
                    for b in range(2):
                        for g in range(2):
                            j = 2 * b + g
                            e.wait_ge(sem("l0_context_done"), 8 * n + j + 1)
                            if j == 0:
                                wait(e, sem("l0_context_done"), 8 * n)
                            e.activation(probsT[:, b, 512 * g:512 * g + 512], PS[:, 2 + (u + j) % 2], ACT.Copy)\
                                .then_inc(sem("l0_context_drained"), 1)
                    wait(e, sem("l0_out_done"), n)
                    for g in range(2):
                        for b in range(2):
                            j = 4 + 2 * g + b
                            e.wait_ge(sem("l0_context_done"), 8 * n + j + 1)
                            e.activation(pkvT[:, 8 * g:8 * g + 8, S * b:S * b + S],
                                         PS[:, 2 + (u + j) % 2].rearrange("p (h q) -> p h q", h=8), ACT.Copy)\
                                .then_inc(sem("l0_context_drained"), 1)
                if front:
                    m, v = n + 1, 1 - u
                    for b in range(2):
                        e.wait_ge(sem("l0_max_ready"), 2 * m + b + 1)
                        for hp in range(8):
                            ins = e.activation(probs[:, v, b, hp], probs[:, v, b, hp], ACT.Exp,
                                               bias=neg_max[:, v, b, hp:hp + 1], scale=SCALE0,
                                               accum_out=row_sum[:, v, b, hp:hp + 1])
                        ins.then_inc(sem("l0_exp_done"), 1)
            walk(e, NT, step)

        y_tok = carve((2, D), 0)
        c_tok = carve((2, D))
        c_norm = carve((2, D))
        norm_a = carve((D,))
        norm_b = carve((D,))
        y_stats = carve((2, 6))
        c_stats = carve((2, 6))
        moments = carve((2, 2, 2))
        var_eps = carve((2, 2))
        inv_std = carve((2, 2))
        yT = carve((2, P))
        cT = carve((2, P))
        q_sb = carve((2, P))
        k_sb = carve((2, P))
        q_masked = carve((2, 2, 4, S))
        k_masked = carve((2, 2, 4, S))
        v_ones = sb("v_ones", [P, 2, 2, H, HD + 1])
        att_probs = carve((2, 2, 8, S))
        att_max = carve((2, 2, 8))
        att_probsT = carve((2, 4, P))
        den_inv = carve((2, 8))
        att_ctx = carve((2, 8, HD))
        att_ctxT = carve((2, 2, S))[0:S]
        mask_int = ctx.enter_context(nc.sbuf_tensor("mask_int", [S, 2, 2, S], I32))
        att_mask = ctx.enter_context(nc.sbuf_tensor("att_mask", [S, 2, 2, S], BF16))

        SCALE1, SCALE3 = float(D) ** -0.5, float(HD) ** -0.5
        ATT = [
            dict(name="msa", i=0, g="ln02_g", b="ln02_b", token_mask=True, mask="mask1", mi=0, cross=None,
                 bias="msa_bo", scale=SCALE1),
            dict(name="ca1", i=1, g="ln11_g", b="ln11_b", token_mask=False, mask="mask2", mi=1, cross=0,
                 bias="ca1_bo", scale=SCALE1),
            dict(name="sa", i=2, pre=("sa_g", "sa_b"), mask=None, cross=None, bias="sa_bo", scale=SCALE3,
                 qkb=("sa_bq", "sa_bk"), vb="sa_bv"),
            dict(name="ca", i=3, pre=("caq_g", "caq_b"), mask=None, cross=1, cnorm=("cakv_g", "cakv_b"),
                 bias="ca_bo", scale=SCALE3, qkb=("ca_bq", "ca_bk"), vb="ca_bv"),
        ]

        def tile(t):
            return X[:, bass.ds(t, 1)].rearrange("p a d -> p (a d)")

        def att_sync(e, c):
            cross, masked = c["cross"], c["mask"]

            def step(k, u, head, front, back, late=False):
                m = 2 * k + u + 2
                if head and cross is not None:
                    if "cnorm" in c:
                        wait_alone(e, sem("att_c_normed"), m - 1)
                    else:
                        wait_alone(e, sem("att_transposed"), c["i"] * NT + m - 1)
                    e.dma_start(c_tok[:, u], ctx_in[bass.ds(2 * m, 2)].rearrange("b s d -> (b s) d"))\
                        .then_inc(sem(f"att_c_loaded{u}"), 16)
                if head and masked:
                    wait_alone(e, sem("att_mask_ready"), c["mi"] * NT + m - 1)
                    e.dma_start(mask_int[:, u], a[masked][bass.ds(2 * m, 2)].rearrange("b s k -> s b k"))\
                        .then_inc(sem(f"att_mask_loaded{u}"), 16)
            walk(e, NT, step)

        def att_pool(e, c):
            base = c["i"] * NT
            norm_cross = "cnorm" in c

            def step(k, u, head, front, back, late=False):
                n = 2 * k + u
                if head:
                    m = base + n + 2
                    parts = 2 if norm_cross else 1
                    wait_alone(e, sem("att_moments"), m + 1)
                    e.tensor_scalar(var_eps[:, u, 0:parts], moments[:, u, 0:parts, 1], EPS, None, ALU.add)\
                        .then_inc(sem("att_var_eps"), 1)
                    wait_alone(e, sem("att_var_eps"), m + 1)
                    e.tensor_tensor(inv_std[:, u, 0:parts], var_eps[:, u, 0:parts], half_power[:, 0:parts], ALU.pow)\
                        .then_inc(sem("att_inv_std"), 1)
                if front:
                    m, v = base + n + 1, 1 - u
                    e.wait_ge(sem("att_qk_kept"), m + 1)
                    wait(e, sem("att_scores_done"), 2 * (m - 1))
                    e.tensor_tensor(k_masked[:, v], k_sb[:, v].rearrange("p (b k) -> p b k", b=2).unsqueeze(2)
                                    .to_broadcast([P, 2, 4, S]),
                                    col("place").unsqueeze(1).unsqueeze(3).to_broadcast([P, 2, 4, S]), ALU.mult)\
                        .then_inc(sem("att_k_masked"), 1)
                if head:
                    m = base + n + 2
                    if c["mask"]:
                        mm = c["mi"] * NT + n + 2
                        kk = (c["mi"] * NT) // 2 + k
                        e.wait_ge(sem(f"att_mask_loaded{u}"), 16 * (kk + 2))
                        wait_alone(e, sem("att_scores_done"), 2 * (m - 1))
                        e.tensor_scalar(att_mask[:, u], mask_int[:, u], 0.0, MASKED, ALU.is_equal, ALU.mult)\
                            .then_inc(sem("att_mask_ready"), 1)
                    e.wait_ge(sem("att_normed"), m + 1)
                    xn = tile(n + 2)
                    e.tensor_tensor(xn, xn if "pre" in c else y_tok[:, u], row(c["bias"]), ALU.add)\
                        .then_inc(sem("att_base_ready"), 1)
            walk(e, NT, step)

        def att_tensor(e, c):
            base = c["i"] * NT
            cross, norm_cross = c["cross"], "cnorm" in c
            wq, wk, wv = (w_att[c["name"]][:, i] for i in range(3))
            wo = w_out[c["name"]]

            def step(k, u, head, front, back, late=False):
                n = base + 2 * k + u
                if front:
                    m, v = n + 1, 1 - u
                    e.wait_ge(sem("att_T_kept"), m + 1)
                    wait(e, sem("att_qk_kept"), m)
                    wait(e, sem("att_v_ready"), m)
                    src = yT if cross is None else cT
                    e.matmul(PS[:, 1, 0:P], wq, yT[:, v], start=True, stop=True)
                    e.matmul(PS[:, 1, P:2 * P], wk, src[:, v], start=True, stop=True)
                    for b in range(2):
                        for half in range(2):
                            ins = e.matmul(PS[S * half:S * half + S, 1, (2 + b) * P:(3 + b) * P],
                                           src[:, v, S * b:S * b + S], wv, start=True, stop=True)
                    ins.then_inc(sem("att_projected"), 1)
                if late:
                    e.wait_ge(sem("att_ctx_ready"), n)
                    wait_alone(e, sem("att_added"), n - 1)
                    for b in range(2):
                        ins = e.transpose(PS[0:S, 7, P * b:P * b + P], att_ctx[:, b], ident[:, :])
                    ins.then_inc(sem("att_ctxT_done"), 1)
                if back:
                    for b in range(2):
                        e.wait_ge(sem("att_exp_done"), 2 * n + b + 1)
                        for i in range(4):
                            ins = e.transpose(PS[:, 4 + b, i * P:i * P + P], att_probs[:, u, b, 2 * i:2 * i + 2],
                                              ident[:, :])
                        ins.then_inc(sem("att_probsT_done"), 1)
                if late:
                    e.wait_ge(sem("att_ctxT_kept"), n)
                    for gg in range(2):
                        ins = e.matmul(PS[:, 7, 2 * P:3 * P], att_ctxT[:, gg], wo[:, gg], start=(gg == 0),
                                       stop=(gg == 1))
                    ins.then_inc(sem("att_out_done"), 1)
                if head:
                    e.wait_ge(sem("att_normed"), n + 3)
                    wait(e, sem("att_T_kept"), n + 2)
                    ins = e.transpose(PS[:, 0, 0:P], y_tok[:, u], ident[:, :])
                    if cross is not None:
                        if norm_cross:
                            e.wait_ge(sem("att_c_normed"), n - base + 3)
                            ins = e.transpose(PS[:, 0, P:2 * P], c_norm[:, u], ident[:, :])
                        else:
                            e.wait_ge(sem(f"att_c_loaded{u}"), 16 * (cross * NT // 2 + k + 2))
                            ins = e.transpose(PS[:, 0, P:2 * P], c_tok[:, u], ident[:, :])
                    ins.then_inc(sem("att_transposed"), 1)
                if front:
                    e.wait_ge(sem("att_q_masked"), m + 1)
                    e.wait_ge(sem("att_k_masked"), m + 1)
                    if c["mask"]:
                        e.wait_ge(sem("att_mask_ready"), m - base + c["mi"] * NT + 1)
                    for b in range(2):
                        wait(e, sem("att_shifted"), 2 * m + b - 1)
                        o = PS[:, 2 + b]
                        if c["mask"]:
                            e.matmul(o.rearrange("p (i k) -> p i k", i=8), twice[:, :],
                                     att_mask[:, v, b].unsqueeze(1).to_broadcast([S, 8, S]),
                                     start=True, stop=False, skip_group_check=True)
                        for g in range(2):
                            ins = e.matmul(o[:, 256 * g:256 * g + 256], q_masked[:, v, b, 2 * g:2 * g + 2],
                                           k_masked[:, v, b], start=not c["mask"], stop=True,
                                           skip_group_check=True)
                        ins.then_inc(sem("att_scores_done"), 1)
                if back:
                    e.wait_ge(sem("att_probsT_kept"), 2 * n + 2)
                    wait(e, sem("att_ctx_ready"), n)
                    for b in range(2):
                        for i in range(4):
                            for gg in range(2):
                                h = 4 * (2 * (i // 2) + gg) + 2 * (i % 2)
                                ins = e.matmul(PS[S * gg:S * gg + S, 6, (4 * b + i) * 18:(4 * b + i) * 18 + 18],
                                               att_probsT[:, b, i, S * gg:S * gg + S], v_ones[:, u, b, h:h + 2],
                                               start=True, stop=True, skip_group_check=True)
                    ins.then_inc(sem("att_pv_done"), 1)
            walk_late(e, NT, step)

        def att_vector(e, c):
            base = c["i"] * NT
            cross, norm_cross = c["cross"], "cnorm" in c
            if c["i"] == 0:
                e.memset(v_ones[:, :], 0.0).then_inc(sem("att_v_zeroed"), 1)
                e.wait_ge(sem("att_v_zeroed"), 1)
                for u in range(2):
                    for half in range(2):
                        e.memset(v_ones[S * half:S * half + S, u].rearrange("p b (h two) w -> p (b h) two w", two=2)
                                 [:, :, half, HD:HD + 1], 1.0).then_inc(sem("att_v_zeroed"), 1)
                e.wait_ge(sem("att_v_zeroed"), 5)

            def step(k, u, head, front, back, late=False):
                n = base + 2 * k + u
                if head:
                    m = n + 2
                    e.bn_stats(y_stats[:, u], tile(m - base)).then_inc(sem("att_stats"), 1)
                    wait_alone(e, sem("att_stats"), m + 1)
                    ins = e.bn_aggr(moments[:, u, 0], y_stats[:, u])
                    if norm_cross:
                        e.wait_ge(sem(f"att_c_loaded{u}"), 16 * (cross * NT // 2 + k + 2))
                        e.bn_stats(c_stats[:, u], c_tok[:, u]).then_inc(sem("att_c_stats"), 1)
                        wait_alone(e, sem("att_c_stats"), m - base + 1)
                        ins = e.bn_aggr(moments[:, u, 1], c_stats[:, u])
                    ins.then_inc(sem("att_moments"), 1)
                if head:
                    m = n + 2
                    mean = moments[:, u, 0, 0:1]
                    e.wait_ge(sem("att_inv_std"), m + 1)
                    wait(e, sem("att_transposed"), m - 1)
                    wait(e, sem("att_base_ready"), m - 1)
                    if "pre" in c:
                        if norm_cross:
                            e.tensor_scalar(c_norm[:, u], c_tok[:, u], moments[:, u, 1, 0:1], inv_std[:, u, 1:2],
                                            ALU.subtract, ALU.mult).then_inc(sem("att_c_normed"), 1)
                        e.tensor_scalar(y_tok[:, u], tile(m - base), mean, inv_std[:, u, 0:1],
                                        ALU.subtract, ALU.mult).then_inc(sem("att_normed"), 1)
                    else:
                        e.scalar_tensor_tensor(norm_a, tile(m - base), mean, row(c["g"]), ALU.subtract, ALU.mult)\
                            .then_inc(sem("att_scaled"), 1)
                        e.wait_ge(sem("att_scaled"), m + 1)
                        to = norm_b if c["token_mask"] else y_tok[:, u]
                        ins = e.scalar_tensor_tensor(to, norm_a, inv_std[:, u, 0:1], row(c["b"]), ALU.mult, ALU.add)
                        if c["token_mask"]:
                            ins.then_inc(sem("att_biased"), 1)
                            e.wait_ge(sem("att_biased"), m + 1)
                            ins = e.tensor_scalar(y_tok[:, u], norm_b, token_mask[:, bass.ds(m - base, 1)], None, ALU.mult)
                        ins.then_inc(sem("att_normed"), 1)
                if front:
                    m, v = n + 1, 1 - u
                    e.wait_ge(sem("att_qk_kept"), m + 1)
                    wait(e, sem("att_scores_done"), 2 * (m - 1))
                    e.tensor_tensor(q_masked[:, v], q_sb[:, v].rearrange("p (b q) -> p b q", b=2).unsqueeze(2)
                                    .to_broadcast([P, 2, 4, S]),
                                    col("group").unsqueeze(1).unsqueeze(3).to_broadcast([P, 2, 4, S]), ALU.mult)\
                        .then_inc(sem("att_q_masked"), 1)
                    if cross == 0:
                        e.tensor_reduce(pooled[:, bass.ds(2 * (m - base), 2)],
                                        cT[:, v].rearrange("p (b s) -> p b s", b=2), AX.X, ALU.add)
                    e.wait_ge(sem("att_projected"), m + 1)
                    wait(e, sem("att_pv_done"), m - 1)
                    for half in range(2):
                        r = slice(S * half, S * half + S)
                        to = v_ones[r, v].rearrange("p b (h two) w -> p (b h) two w", two=2)[:, :, half, 0:HD]
                        of = PS[r, 1, 2 * P:4 * P].rearrange("p (n two w) -> p n two w", two=2, w=HD)[:, :, half]
                        if "vb" in c:
                            for b in range(2):
                                vb = row(c["vb"])[r].rearrange("p (h two w) -> p h two w", two=2, w=HD)[:, :, half]
                                ins = e.tensor_tensor(to[:, 8 * b:8 * b + 8], of[:, 8 * b:8 * b + 8], vb, ALU.add)
                        else:
                            ins = e.tensor_copy(to, of)
                    ins.then_inc(sem("att_v_ready"), 1)
                if late:
                    e.wait_ge(sem("att_out_done"), n)
                    e.wait_ge(sem("att_base_ready"), n)
                    e.tensor_tensor(tile(n - base - 1), tile(n - base - 1), PS[:, 7, 2 * P:3 * P], ALU.add)\
                        .then_inc(sem("att_added"), 1)
                if front:
                    m = n + 1
                    for b in range(2):
                        s3 = PS[:, 2 + b].rearrange("p (i k) -> p i k", i=8)
                        e.wait_ge(sem("att_scores_done"), 2 * m + b + 1)
                        e.tensor_reduce(att_max[:, v, b], s3, AX.X, ALU.max).then_inc(sem("att_max_ready"), 1)
                        e.wait_ge(sem("att_max_ready"), 2 * m + b + 1)
                        e.tensor_tensor(att_probs[:, v, b], s3, att_max[:, v, b].unsqueeze(2)
                                        .to_broadcast([P, 8, S]), ALU.subtract).then_inc(sem("att_shifted"), 1)
                if back:
                    e.wait_ge(sem("att_pv_done"), n + 1)
                    pv = PS[:, 6, 0:16 * (HD + 1)].rearrange("p (b i w) -> p b i w", b=2, w=HD + 1)
                    e.reciprocal(den_inv, pv[:, :, :, HD]).then_inc(sem("att_den_ready"), 1)
                    e.wait_ge(sem("att_den_ready"), n + 1)
                    wait(e, sem("att_ctxT_done"), n)
                    e.tensor_tensor(att_ctx, pv[:, :, :, 0:HD], den_inv.unsqueeze(3).to_broadcast([P, 2, 8, HD]),
                                    ALU.mult).then_inc(sem("att_ctx_ready"), 1)
            walk_late(e, NT, step)

        def att_scalar(e, c):
            base = c["i"] * NT
            cross = c["cross"]

            def step(k, u, head, front, back, late=False):
                n = base + 2 * k + u
                if front:
                    m, v = n + 1, 1 - u
                    e.wait_ge(sem("att_projected"), m + 1)
                    wait(e, sem("att_q_masked"), m - 1)
                    wait(e, sem("att_k_masked"), m - 1)
                    for i, (to, of) in enumerate(((q_sb, PS[:, 1, 0:P]), (k_sb, PS[:, 1, P:2 * P]))):
                        if "qkb" in c:
                            ins = e.activation(to[:, v], of, ACT.Identity, bias=col(c["qkb"][i]))
                        else:
                            ins = e.activation(to[:, v], of, ACT.Copy)
                    ins.then_inc(sem("att_qk_kept"), 1)
                if late:
                    e.wait_ge(sem("att_ctxT_done"), n)
                    wait(e, sem("att_out_done"), n - 1)
                    e.activation(att_ctxT.rearrange("p g b q -> p b g q"),
                                 PS[0:S, 7, 0:2 * P].rearrange("p (b g q) -> p b g q", b=2, g=2), ACT.Copy)\
                        .then_inc(sem("att_ctxT_kept"), 1)
                if back:
                    wait(e, sem("att_pv_done"), n)
                    for b in range(2):
                        e.wait_ge(sem("att_probsT_done"), 2 * n + b + 1)
                        e.activation(att_probsT[:, b].rearrange("p i q -> p (i q)"), PS[:, 4 + b], ACT.Copy)\
                            .then_inc(sem("att_probsT_kept"), 1)
                if head:
                    e.wait_ge(sem("att_transposed"), n + 3)
                    wait(e, sem("att_projected"), n + 1)
                    if cross == 0:
                        wait(e, sem("att_v_ready"), n + 1)
                    for i, (to, of, gb) in enumerate(((yT, PS[:, 0, 0:P], c.get("pre")),
                                                      (cT, PS[:, 0, P:2 * P], c.get("cnorm")))[:1 if cross is None else 2]):
                        if gb:
                            ins = e.activation(to[:, u], of, ACT.Identity, bias=col(gb[1]), scale=col(gb[0]))
                        else:
                            ins = e.activation(to[:, u], of, ACT.Copy)
                    ins.then_inc(sem("att_T_kept"), 1)
                if front:
                    for b in range(2):
                        e.wait_ge(sem("att_shifted"), 2 * m + b + 1)
                        e.activation(att_probs[:, v, b], att_probs[:, v, b], ACT.Exp, scale=c["scale"])\
                            .then_inc(sem("att_exp_done"), 1)
            walk_late(e, NT, step)

        q_tok = carve((2, QT, D), 0)
        qT = carve((2, QT * P))
        q_stats = carve((2, QT, 6))
        q_moments = carve((2, QT, 2))
        q_var_eps = carve((2, QT))
        q_inv_std = carve((2, QT))
        qn_a = carve((QT, D))
        qn_b = carve((QT, D))
        quad_end = taken[0]

        def tiles(m):
            return X[:, bass.ds(QT * m, QT)]

        def quad_norm_pool(e, base, k, u):
            m = base + 2 * k + u + 2
            wait_alone(e, sem("quad_moments"), m + 1)
            e.tensor_scalar(q_var_eps[:, u], q_moments[:, u, :, 1], EPS, None, ALU.add).then_inc(sem("quad_var_eps"), 1)
            wait_alone(e, sem("quad_var_eps"), m + 1)
            e.tensor_tensor(q_inv_std[:, u], q_var_eps[:, u], half_power[:, :], ALU.pow)\
                .then_inc(sem("quad_inv_std"), 1)

        def quad_moments_vector(e, base, k, u):
            m = base + 2 * k + u + 2
            for t in range(QT):
                ins = e.bn_stats(q_stats[:, u, t], X[:, bass.ds(QT * (m - base) + t, 1)].rearrange("p a d -> p (a d)"))
            ins.then_inc(sem("quad_stats"), 1)
            wait_alone(e, sem("quad_stats"), m + 1)
            for t in range(QT):
                ins = e.bn_aggr(q_moments[:, u, t], q_stats[:, u, t])
            ins.then_inc(sem("quad_moments"), 1)

        def quad_norm_vector(e, base, k, u, gb, masked, done_before):
            m = base + 2 * k + u + 2
            e.wait_ge(sem("quad_inv_std"), m + 1)
            wait(e, sem("quad_transposed"), m - 1)
            if done_before is not None:
                wait(e, done_before, m - 1)
            one = lambda t: X[:, bass.ds(QT * (m - base) + t, 1)].rearrange("p a d -> p (a d)")
            if gb is None:
                for t in range(QT):
                    ins = e.tensor_scalar(q_tok[:, u, t], one(t), q_moments[:, u, t, 0:1], q_inv_std[:, u, t:t + 1],
                                          ALU.subtract, ALU.mult)
                ins.then_inc(sem("quad_normed"), 1)
                return
            for t in range(QT):
                ins = e.scalar_tensor_tensor(qn_a[:, t], one(t), q_moments[:, u, t, 0:1], row(gb[0]),
                                             ALU.subtract, ALU.mult)
            ins.then_inc(sem("quad_scaled"), 1)
            e.wait_ge(sem("quad_scaled"), m + 1)
            for t in range(QT):
                ins = e.scalar_tensor_tensor(qn_b[:, t] if masked else q_tok[:, u, t], qn_a[:, t],
                                             q_inv_std[:, u, t:t + 1], row(gb[1]), ALU.mult, ALU.add)
            if masked:
                ins.then_inc(sem("quad_shifted"), 1)
                e.wait_ge(sem("quad_shifted"), m + 1)
                ins = e.tensor_tensor(q_tok[:, u], qn_b, token_mask[:, bass.ds(QT * (m - base), QT)].unsqueeze(2)
                                      .to_broadcast([P, QT, D]), ALU.mult)
            ins.then_inc(sem("quad_normed"), 1)

        def quad_transpose_tensor(e, base, k, u):
            m = base + 2 * k + u + 2
            e.wait_ge(sem("quad_normed"), m + 1)
            wait(e, sem("quad_T_kept"), m)
            for t in range(QT):
                ins = e.transpose(PS[:, 0, P * t:P * t + P], q_tok[:, u, t], ident[:, :])
            ins.then_inc(sem("quad_transposed"), 1)

        def quad_keep_scalar(e, base, k, u, gb=None):
            m = base + 2 * k + u + 2
            e.wait_ge(sem("quad_transposed"), m + 1)
            if gb:
                ins = e.activation(qT[:, u], PS[:, 0], ACT.Identity, bias=col(gb[1]), scale=col(gb[0]))
            else:
                ins = e.activation(qT[:, u], PS[:, 0], ACT.Copy)
            ins.then_inc(sem("quad_T_kept"), 1)

        ff_h = carve((2, FC, QT * P), quad_end)
        FFN = [dict(i=0, q=0, w1=w_l0ff1, w2=w_l0ff2, b1="l0_b1", b2="l0_b2", norm=("ln01_g", "ln01_b"), masked=True),
               dict(i=1, q=1, w1=w_l1ff1, w2=w_l1ff2, b1="l1_b1", b2="l1_b2", norm=("ln12_g", "ln12_b"), masked=False)]

        def ff_pool(e, c):
            def step(k, u, head, front, back):
                if head:
                    m = 2 * k + u + 2
                    quad_norm_pool(e, c["q"] * NQ, k, u)
                    e.wait_ge(sem("quad_normed"), c["q"] * NQ + m + 1)
                    e.tensor_tensor(tiles(m), q_tok[:, u], row(c["b2"]).unsqueeze(1).to_broadcast([P, QT, D]), ALU.add)\
                        .then_inc(sem("ff_base_ready"), 1)
            walk(e, NQ, step)

        def ff_tensor(e, c):
            def step(k, u, head, front, back):
                n = c["i"] * NQ + 2 * k + u
                if front:
                    m, v = n + 1, 1 - u
                    e.wait_ge(sem("quad_T_kept"), (c["q"] - c["i"]) * NQ + m + 1)
                    for f in range(FC):
                        wait(e, sem("ff_h_ready"), FC * (m - 1) + f + 1)
                        e.matmul(PS[:, 1 + f], c["w1"][:, P * f:P * f + P], qT[:, v], start=True, stop=True)\
                            .then_inc(sem("ff_h_done"), 1)
                if back:
                    e.wait_ge(sem("ff_h_ready"), FC * n + FC)
                    wait(e, sem("ff_added"), n)
                    for t in range(QT):
                        for f in range(FC):
                            ins = e.matmul(PS[:, 5 + u, D * t:D * t + D], ff_h[:, u, f, P * t:P * t + P], c["w2"][:, f],
                                           start=(f == 0), stop=(f == FC - 1))
                    ins.then_inc(sem("ff_out_done"), 1)
                if head:
                    quad_transpose_tensor(e, c["q"] * NQ, k, u)
            walk(e, NQ, step)

        def ff_vector(e, c):
            base = c["q"] * NQ

            def step(k, u, head, front, back):
                n = c["i"] * NQ + 2 * k + u
                if head:
                    quad_moments_vector(e, base, k, u)
                    quad_norm_vector(e, base, k, u, c["norm"], c["masked"], sem("ff_base_ready"))
                if back:
                    e.wait_ge(sem("ff_out_done"), n + 1)
                    e.wait_ge(sem("ff_base_ready"), n + 1)
                    xs = tiles(n - c["i"] * NQ)
                    e.tensor_tensor(xs, xs, PS[:, 5 + u].rearrange("p (t d) -> p t d", t=QT), ALU.add)\
                        .then_inc(sem("ff_added"), 1)
            walk(e, NQ, step)

        def ff_scalar(e, c):
            def step(k, u, head, front, back):
                n = c["i"] * NQ + 2 * k + u
                if front:
                    m, v = n + 1, 1 - u
                    wait(e, sem("ff_out_done"), m - 1)
                    for f in range(FC):
                        e.wait_ge(sem("ff_h_done"), FC * m + f + 1)
                        e.activation(ff_h[:, v, f], PS[:, 1 + f], ACT.Relu, bias=col(c["b1"])[:, f:f + 1])\
                            .then_inc(sem("ff_h_ready"), 1)
                if head:
                    wait(e, sem("ff_h_done"), FC * (n + 1))
                    quad_keep_scalar(e, c["q"] * NQ, k, u)
            walk(e, NQ, step)

        NBU = QT * P // S
        vis = carve((NB,), quad_end)
        vis_gate = carve((NB,))
        neg_bg = carve((1,))
        ones = carve((P,))
        tp = carve((2, QT * P))
        tv = carve((NBU, S))
        weight = carve((NBU, S))
        gate = carve((NBU, S))
        wv = carve((NBU, S))
        part = carve((NBU, S))
        fused = carve((2, QT * P))
        l2_max = carve((NBU,))
        l2_sum = carve((NBU,))
        l2_inv = carve((NBU,))
        f_stats = carve((QT, 6))
        f_moments = carve((QT, 2))
        f_var_eps = carve((QT,))
        f_inv_std = carve((QT,))
        LQ = 2

        def l2_pool(e, c):
            def step(k, u, head, front, back):
                n = 2 * k + u
                if head:
                    quad_norm_pool(e, LQ * NQ, k, u)
                if back:
                    wait_alone(e, sem("l2_f_moments"), n + 1)
                    e.tensor_scalar(f_var_eps, f_moments[:, :, 1], EPS, None, ALU.add).then_inc(sem("l2_f_var_eps"), 1)
                    wait_alone(e, sem("l2_f_var_eps"), n + 1)
                    e.tensor_tensor(f_inv_std, f_var_eps, half_power[:, :], ALU.pow).then_inc(sem("l2_f_inv_std"), 1)
            walk(e, NQ, step)

        def l2_tensor(e, c):
            e.matmul(PS[:, 5, 0:NB], w_l2[:, 1], pooled[:, :], start=True, stop=True).then_inc(sem("l2_vis_done"), 1)
            e.wait_ge(sem("l2_vis_kept"), 1)
            e.matmul(PS[:, 5, 128:128 + NB], w_l2[:, 3], vis, start=True, stop=True).then_inc(sem("l2_vis_done"), 1)
            e.wait_ge(sem("l2_ones"), 1)

            def step(k, u, head, front, back):
                n = 2 * k + u
                if front:
                    m, v = n + 1, 1 - u
                    e.wait_ge(sem("quad_T_kept"), LQ * NQ + m + 1)
                    wait(e, sem("l2_tp_ready"), m)
                    e.matmul(PS[:, 1], w_l2[:, 0], qT[:, v], start=True, stop=True).then_inc(sem("l2_tp_done"), 1)
                    e.wait_ge(sem("l2_tp_ready"), m + 1)
                    wait(e, sem("l2_gate_summed"), m)
                    e.matmul(PS[:, 3], w_l2[:, 2], tp[:, v], start=True, stop=True).then_inc(sem("l2_gate_done"), 1)
                    e.wait_ge(sem("l2_tv_ready"), m + 1)
                    wait(e, sem("l2_agree_shifted"), m)
                    e.matmul(PS[:, 2], ones, tv.rearrange("p b s -> p (b s)"), start=True, stop=True)\
                        .then_inc(sem("l2_agree_done"), 1)
                if back:
                    e.wait_ge(sem("l2_fused"), n + 1)
                    wait(e, sem("l2_f_scaled"), n)
                    for t in range(QT):
                        ins = e.transpose(PS[:, 4, P * t:P * t + P], fused[:, u, P * t:P * t + P], ident[:, :])
                    ins.then_inc(sem("l2_f_transposed"), 1)
                if head:
                    quad_transpose_tensor(e, LQ * NQ, k, u)
            walk(e, NQ, step)

        def l2_vector(e, c):
            e.memset(ones, 1.0).then_inc(sem("l2_ones"), 1)
            e.tensor_scalar(neg_bg, col("bg"), -1.0, None, ALU.mult).then_inc(sem("l2_neg_bg"), 1)
            e.wait_ge(sem("l2_vis_kept"), 2)
            chain = [0]

            def step(k, u, head, front, back):
                n = 2 * k + u

                if head:
                    quad_moments_vector(e, LQ * NQ, k, u)
                if front:
                    m, v = n + 1, 1 - u
                    wide = lambda x: x.unsqueeze(2).to_broadcast([P, NBU, S])
                    of_unit = lambda x: wide(x[:, bass.ds(NBU * m, NBU)])
                    e.wait_ge(sem("l2_tp_ready"), m + 1)
                    wait(e, sem("l2_agree_done"), m)
                    e.tensor_tensor(tv, tp[:, v].rearrange("p (b s) -> p b s", b=NBU), of_unit(vis), ALU.mult)\
                        .then_inc(sem("l2_tv_ready"), 1)
                    e.wait_ge(sem("l2_agree_done"), m + 1)
                    agree = PS[:, 2].rearrange("p (b s) -> p b s", b=NBU)
                    e.tensor_reduce(l2_max, agree, AX.X, ALU.max).then_inc(sem("l2_max_ready"), 1)
                    e.wait_ge(sem("l2_max_ready"), m + 1)
                    e.tensor_tensor(weight, agree, wide(l2_max), ALU.subtract).then_inc(sem("l2_agree_shifted"), 1)
                    e.wait_ge(sem("l2_exp_done"), m + 1)
                    e.tensor_reduce(l2_sum, weight, AX.X, ALU.add).then_inc(sem("l2_sum_ready"), 1)
                    e.wait_ge(sem("l2_sum_ready"), m + 1)
                    e.reciprocal(l2_inv, l2_sum).then_inc(sem("l2_inv_ready"), 1)
                    e.wait_ge(sem("l2_inv_ready"), m + 1)
                    e.tensor_tensor(weight, weight, wide(l2_inv), ALU.mult).then_inc(sem("l2_weight_ready"), 1)
                    e.wait_ge(sem("l2_weight_ready"), m + 1)
                    e.tensor_tensor(part, weight, of_unit(vis_gate), ALU.mult).then_inc(sem("l2_part_ready"), 1)
                    e.tensor_tensor(wv, weight, of_unit(vis), ALU.mult).then_inc(sem("l2_wv_ready"), 1)
                    e.wait_ge(sem("l2_part_ready"), m + 1)
                    e.wait_ge(sem("l2_gate_done"), m + 1)
                    e.tensor_tensor(gate, part, PS[:, 3].rearrange("p (b s) -> p b s", b=NBU), ALU.add)\
                        .then_inc(sem("l2_gate_summed"), 1)
                    e.wait_ge(sem("l2_gate_exp"), m + 1)
                    e.tensor_scalar(part, gate, 1.0, None, ALU.add).then_inc(sem("l2_gate_den"), 1)
                    e.wait_ge(sem("l2_gate_den"), m + 1)
                    e.reciprocal(tv, part).then_inc(sem("l2_gate_ready"), 1)
                    e.wait_ge(sem("l2_gate_ready"), m + 1)
                    e.wait_ge(sem("l2_wv_ready"), m + 1)
                    e.tensor_tensor(part, tv, wv, ALU.mult).then_inc(sem("l2_gated"), 1)
                    e.wait_ge(sem("l2_gated"), m + 1)
                    wait(e, sem("l2_f_transposed"), m - 1)
                    e.tensor_tensor(fused[:, v].rearrange("p (b s) -> p b s", b=NBU), part,
                                    qT[:, v].rearrange("p (b s) -> p b s", b=NBU), ALU.add)\
                        .then_inc(sem("l2_fused"), 1)
                if back:
                    e.wait_ge(sem("l2_f_transposed"), n + 1)
                    for t in range(QT):
                        ins = e.bn_stats(f_stats[:, t], PS[:, 4, P * t:P * t + P])
                    ins.then_inc(sem("l2_f_stats"), 1)
                    wait_alone(e, sem("l2_f_stats"), n + 1)
                    for t in range(QT):
                        ins = e.bn_aggr(f_moments[:, t], f_stats[:, t])
                    ins.then_inc(sem("l2_f_moments"), 1)
                if head:
                    quad_norm_vector(e, LQ * NQ, k, u, ("ln13_g", "ln13_b"), False, None)
                if back:
                    e.wait_ge(sem("l2_f_moments"), n + 1)
                    for t in range(QT):
                        ins = e.scalar_tensor_tensor(qn_b[:, t], PS[:, 4, P * t:P * t + P], f_moments[:, t, 0:1],
                                                     row("l2_g"), ALU.subtract, ALU.mult)
                    ins.then_inc(sem("l2_f_scaled"), 1)
                    e.wait_ge(sem("l2_f_scaled"), n + 1)
                    e.wait_ge(sem("l2_f_inv_std"), n + 1)
                    for t in range(QT):
                        e.scalar_tensor_tensor(X[:, bass.ds(QT * n + t, 1)].rearrange("p a d -> p (a d)"), qn_b[:, t],
                                               f_inv_std[:, t:t + 1], row("l2_b"), ALU.mult, ALU.add)
            walk(e, NQ, step)

        def l2_scalar(e, c):
            e.wait_ge(sem("l2_vis_done"), 1)
            e.activation(vis, PS[:, 5, 0:NB], ACT.Identity, bias=col("bv"), scale=1.0 / S).then_inc(sem("l2_vis_kept"), 1)
            e.wait_ge(sem("l2_vis_done"), 2)
            e.activation(vis_gate, PS[:, 5, 128:128 + NB], ACT.Copy).then_inc(sem("l2_vis_kept"), 1)
            e.wait_ge(sem("l2_neg_bg"), 1)

            def step(k, u, head, front, back):
                n = 2 * k + u
                if front:
                    m, v = n + 1, 1 - u
                    e.wait_ge(sem("l2_tp_done"), m + 1)
                    wait(e, sem("l2_gate_done"), m - 1)
                    wait(e, sem("l2_tv_ready"), m - 1)
                    e.activation(tp[:, v], PS[:, 1], ACT.Identity, bias=col("bt")).then_inc(sem("l2_tp_ready"), 1)
                    e.wait_ge(sem("l2_agree_shifted"), m + 1)
                    e.activation(weight, weight, ACT.Exp, scale=2.0).then_inc(sem("l2_exp_done"), 1)
                    e.wait_ge(sem("l2_gate_summed"), m + 1)
                    e.activation(gate, gate, ACT.Exp, scale=-1.0, bias=neg_bg).then_inc(sem("l2_gate_exp"), 1)
                if head:
                    wait(e, sem("l2_tp_done"), n + 1)
                    wait(e, sem("l2_fused"), n + 1)
                    quad_keep_scalar(e, LQ * NQ, k, u)
            walk(e, NQ, step)

        logits = carve((QT, NE), quad_end)
        top = carve((QT, NE))
        gap = carve((QT,))
        gap_exp = carve((QT,))
        gap_den = carve((QT,))
        gates = carve((2, QT))
        top_at_f = carve((2, QT))
        hit = carve((2, QT, NE))
        mix = carve((2, QT, NE))
        mixT = carve((QT, P))[0:NE]
        e_h = carve((2, FC, QT * P))
        top_at = sb("top_at", [P, QT, NE], U32)
        MQ = 3

        def moe_pool(e, c):
            def step(k, u, head, front, back):
                if head:
                    quad_norm_pool(e, MQ * NQ, k, u)
            walk(e, NQ, step)

        def moe_tensor(e, c):
            e.wait_ge(sem("experts_loaded"), 32)

            def step(k, u, head, front, back):
                n = 2 * k + u
                m, v = n + 1, 1 - u
                if front:
                    e.wait_ge(sem("quad_T_kept"), MQ * NQ + m + 1)
                    wait(e, sem("moe_base_ready"), m)
                    for t in range(QT):
                        ins = e.matmul(PS[:, 1, NE * t:NE * t + NE], qT[:, v, P * t:P * t + P], w_router[:, :],
                                       start=True, stop=True)
                    ins.then_inc(sem("moe_logits_done"), 1)

                def up(x):
                    for f in range(FC):
                        if x:
                            e.wait_ge(sem("moe_h_ready"), (n * NE + x - 1) * FC + f + 1)
                        e.matmul(PS[:, 2 + f], w_e1[:, x, P * f:P * f + P], qT[:, u], start=True, stop=True)\
                            .then_inc(sem("moe_h_done"), 1)

                def down(x):
                    e.wait_ge(sem("moe_h_ready"), (n * NE + x + 1) * FC)
                    wait(e, sem("moe_added"), n * NE + max(x - 1, 0))
                    for t in range(QT):
                        for f in range(FC):
                            ins = e.matmul(PS[:, 6 + x % 2, D * t:D * t + D], e_h[:, x % 2, f, P * t:P * t + P],
                                           w_e2[:, x, f], start=(f == 0), stop=(f == FC - 1))
                    ins.then_inc(sem("moe_down_done"), 1)
                for x in range(NE + 1):
                    if back and x < NE:
                        up(x)
                    if back and x:
                        down(x - 1)
                    if front and x == 1:
                        e.wait_ge(sem("moe_mix_ready"), m + 1)
                        for t in range(QT):
                            ins = e.transpose(PS[0:NE, 1, P * t:P * t + P], mix[:, v, t], ident[:, :])
                        ins.then_inc(sem("moe_mixT_done"), 1)
                    if front and x == 3:
                        e.wait_ge(sem("moe_mixT_kept"), m + 1)
                        for t in range(QT):
                            ins = e.matmul(PS[:, 1, D * t:D * t + D], mixT[:, t], w_eb2[:, :], start=True, stop=True)
                        ins.then_inc(sem("moe_biases_done"), 1)
                    if head and x == 5:
                        quad_transpose_tensor(e, MQ * NQ, k, u)
            walk(e, NQ, step)

        def moe_vector(e, c):
            def step(k, u, head, front, back):
                n = 2 * k + u
                m, v = n + 1, 1 - u
                if head:
                    quad_moments_vector(e, MQ * NQ, k, u)
                if front:
                    misc = row("misc")
                    each = lambda x: x.unsqueeze(2).to_broadcast([P, QT, NE])
                    e.wait_ge(sem("moe_logits_done"), m + 1)
                    e.tensor_tensor(logits, PS[:, 1, 0:QT * NE].rearrange("p (t x) -> p t x", t=QT),
                                    misc[:, 0:NE].unsqueeze(1).to_broadcast([P, QT, NE]), ALU.add)\
                        .then_inc(sem("moe_logits_ready"), 1)
                    wait_alone(e, sem("moe_logits_ready"), m + 1)
                    for t in range(QT):
                        ins = e.max(top[:, t], logits[:, t])
                    ins.then_inc(sem("moe_top_ready"), 1)
                    e.wait_ge(sem("moe_top_ready"), m + 1)
                    e.tensor_tensor(gap, top[:, :, 1], top[:, :, 0], ALU.subtract).then_inc(sem("moe_gap_ready"), 1)
                    for t in range(QT):
                        ins = e.max_index(top_at[:, t], top[:, t], logits[:, t])
                    ins.then_inc(sem("moe_top_at_ready"), 1)
                    e.wait_ge(sem("moe_top_at_ready"), m + 1)
                    e.tensor_copy(top_at_f, top_at[:, :, 0:2].rearrange("p t i -> p i t")).then_inc(sem("moe_at_f_ready"), 1)
                    e.wait_ge(sem("moe_gap_exp"), m + 1)
                    e.tensor_scalar(gap_den, gap_exp, 1.0, None, ALU.add).then_inc(sem("moe_den_ready"), 1)
                    e.wait_ge(sem("moe_at_f_ready"), m + 1)
                    for i in range(2):
                        ins = e.tensor_tensor(hit[:, i], misc[:, NE:2 * NE].unsqueeze(1).to_broadcast([P, QT, NE]),
                                              each(top_at_f[:, i]), ALU.is_equal)
                    ins.then_inc(sem("moe_hits_ready"), 1)
                    e.wait_ge(sem("moe_den_ready"), m + 1)
                    e.reciprocal(gates[:, 0], gap_den).then_inc(sem("moe_gate0_ready"), 1)
                    e.wait_ge(sem("moe_gate0_ready"), m + 1)
                    e.tensor_tensor(gates[:, 1], gap_exp, gates[:, 0], ALU.mult).then_inc(sem("moe_gate1_ready"), 1)
                    e.wait_ge(sem("moe_hits_ready"), m + 1)
                    e.wait_ge(sem("moe_gate1_ready"), m + 1)
                    for i in range(2):
                        ins = e.tensor_tensor(hit[:, i], hit[:, i], each(gates[:, i]), ALU.mult)
                    ins.then_inc(sem("moe_parts_ready"), 1)
                    e.wait_ge(sem("moe_parts_ready"), m + 1)
                    e.tensor_tensor(mix[:, v], hit[:, 0], hit[:, 1], ALU.add).then_inc(sem("moe_mix_ready"), 1)
                for x in range(NE):
                    if back:
                        e.wait_ge(sem("moe_down_done"), n * NE + x + 1)
                        if x:
                            e.wait_ge(sem("moe_added"), n * NE + x)
                        else:
                            e.wait_ge(sem("moe_base_ready"), n + 1)
                        for t in range(QT):
                            xt = X[:, bass.ds(QT * n + t, 1)].rearrange("p a d -> p (a d)")
                            ins = e.scalar_tensor_tensor(xt, PS[:, 6 + x % 2, D * t:D * t + D], mix[:, u, t, x:x + 1], xt,
                                                         ALU.mult, ALU.add)
                        ins.then_inc(sem("moe_added"), 1)
                    if front and x == 3:
                        e.wait_ge(sem("moe_biases_done"), m + 1)
                        e.tensor_tensor(tiles(m), tiles(m), PS[:, 1].rearrange("p (t d) -> p t d", t=QT), ALU.add)\
                            .then_inc(sem("moe_base_ready"), 1)
                    if head and x == 3:
                        quad_norm_vector(e, MQ * NQ, k, u, None, False, None)
            walk(e, NQ, step)

        def moe_scalar(e, c):
            def step(k, u, head, front, back):
                n = 2 * k + u
                m, v = n + 1, 1 - u
                if front:
                    e.wait_ge(sem("moe_gap_ready"), m + 1)
                    wait(e, sem("moe_gate1_ready"), m)
                    e.activation(gap_exp, gap, ACT.Exp).then_inc(sem("moe_gap_exp"), 1)
                for x in range(NE):
                    if back:
                        if x:
                            wait(e, sem("moe_down_done"), n * NE + x - 1)
                        for f in range(FC):
                            e.wait_ge(sem("moe_h_done"), (n * NE + x) * FC + f + 1)
                            e.activation(e_h[:, x % 2, f], PS[:, 2 + f], ACT.Gelu,
                                         bias=col("e_b1")[:, FC * x + f:FC * x + f + 1]).then_inc(sem("moe_h_ready"), 1)
                    if front and x == 1:
                        e.wait_ge(sem("moe_mixT_done"), m + 1)
                        wait(e, sem("moe_biases_done"), m)
                        e.activation(mixT.rearrange("p t c -> p (t c)"), PS[0:NE, 1], ACT.Copy)\
                            .then_inc(sem("moe_mixT_kept"), 1)
                    if head and x == 7:
                        wait(e, sem("moe_h_done"), (n + 1) * NE * FC)
                        quad_keep_scalar(e, MQ * NQ, k, u, ("moe_g", "moe_b"))
            walk(e, NQ, step)

        def moe_sync(e, c):
            def step(k, u, head, front, back):
                n = 2 * k + u
                if back:
                    wait_alone(e, sem("moe_added"), (n + 1) * NE)
                    e.dma_start(out[bass.ds(NBU * n, NBU)].rearrange("(t b) s d -> (b s) t d", b=2), tiles(n))\
                        .then_inc(sem(f"out_written{u}"), 16)
            walk(e, NQ, step)

        L0 = dict(sync=l0_sync, gpsimd=l0_pool, tensor=l0_tensor, vector=l0_vector, scalar=l0_scalar)
        AT = dict(sync=att_sync, gpsimd=att_pool, tensor=att_tensor, vector=att_vector, scalar=att_scalar)
        FN = dict(gpsimd=ff_pool, tensor=ff_tensor, vector=ff_vector, scalar=ff_scalar)
        L2 = dict(gpsimd=l2_pool, tensor=l2_tensor, vector=l2_vector, scalar=l2_scalar)
        MOE = dict(sync=moe_sync, gpsimd=moe_pool, tensor=moe_tensor, vector=moe_vector, scalar=moe_scalar)
        PHASES = [(L0, None), (FN, FFN[0]), (AT, ATT[0]), (AT, ATT[1]), (FN, FFN[1]), (L2, None), (AT, ATT[2]),
                  (AT, ATT[3]), (MOE, None)]
        if phases is not None:
            PHASES = [PHASES[i] for i in phases]
        block = ctx.enter_context(nc.Block())

        @block.sync
        def _(e):
            for n, (kind, c) in enumerate(PHASES):
                if "sync" in kind:
                    kind["sync"](e, c)
                meet(e, n + 1)
            if "out_written0" in sems:
                for u in range(2):
                    e.wait_ge(sem(f"out_written{u}"), 16 * NQ // 2)
            else:
                e.dma_start(out.rearrange("(t b) s d -> (b s) t d", b=2), X[:, :, :]).then_inc(sem("out_written"), 16)
                e.wait_ge(sem("out_written"), 16)

        @block.gpsimd
        def _(e):
            for n, (kind, c) in enumerate(PHASES):
                if "gpsimd" in kind:
                    kind["gpsimd"](e, c)
                meet(e, n + 1)

        @block.tensor
        def _(e):
            for n, (kind, c) in enumerate(PHASES):
                kind["tensor"](e, c)
                meet(e, n + 1)

        @block.vector
        def _(e):
            for n, (kind, c) in enumerate(PHASES):
                kind["vector"](e, c)
                meet(e, n + 1)

        @block.scalar
        def _(e):
            for n, (kind, c) in enumerate(PHASES):
                kind["scalar"](e, c)
                meet(e, n + 1)


def lay_out(i):
    c = np.ascontiguousarray
    f = {k: np.asarray(v) for k, v in i.items()}
    T = {}
    NB = f["x"].shape[0]
    T["x"] = f["x"]
    T["ctx"] = f["ctx_1024"]
    T["token_mask"] = c(f["mask_BxSx1_ff1"].reshape(NB * S // P, P).T)
    T["mask0"] = f["mask_BxSx1024_bf0"]
    T["mask1"] = f["mask_Bx1xSxS2_ik0"].reshape(NB, S, S)
    T["mask2"] = f["mask_Bx1xSxS2_if1"].reshape(NB, S, S)
    L0, L1, L2, L3 = ({k[len(p):]: v for k, v in f.items() if k.startswith(p)}
                      for p in ("L0_xattn_", "L1_xattn_", "L2_xattn_", "L3_xattn_"))
    for n in ("Wq", "Wk", "Wv"):
        T[f"l0_{n}T"] = c(L0[n].reshape(D, H, DK).transpose(2, 1, 0))
    T["l0_Wr"] = L0["Wr"].reshape(D, H, DK)
    T["l0_Wo"] = c(L0["Wo"].reshape(H, DK, D).transpose(1, 0, 2))
    T["l0_cb"] = c(L0["content_bias"].T)
    T["l0_pb"] = c(L0["position_bias"].T)
    T["l0_W1"] = L0["W1"]
    T["l0_W2"] = c(L0["W2"].reshape(FC, P, D).transpose(1, 0, 2))
    T["l1_W1"] = c(L1["ff_W1"].T)
    T["l1_W2"] = c(L1["ff_W2"].T.reshape(FC, P, D).transpose(1, 0, 2))

    def blocks(w):
        o = np.zeros((D, D), np.float32)
        for h in range(H):
            o[HD * h:HD * h + HD, HD * h:HD * h + HD] = w.T
        return o
    def out_rows(w):
        return c(w.T.reshape(2, 2, 4, HD, D).transpose(0, 2, 3, 1, 4).reshape(S, 2, D))
    for n, p in (("msa", "msa"), ("ca1", "ca")):
        T["w_" + n] = c(np.stack([blocks(L1[f"{p}_W{x}"]) for x in "qkv"], axis=1))
        T["wo_" + n] = out_rows(L1[f"{p}_Wo"])
    for n in ("sa", "ca"):
        T["w_" + n] = c(L3[n + "_in_w"].reshape(3, D, D).transpose(2, 0, 1))
        T["wo_" + n] = out_rows(L3[n + "_out_w"])
    T["l2_W"] = c(np.stack([L2["Wt"].T, L2["Wv"].T, L2["Wg"][:, :D].T, L2["Wg"][:, D:].T], axis=1))
    T["router"] = c(L3["router_w"].T)
    T["e_b2"] = L3["e_fc2_b"]
    T["e_W1"] = c(L3["e_fc1_w"].transpose(2, 0, 1))
    T["e_W2"] = c(L3["e_fc2_w"].reshape(NE, D, FC, P).transpose(3, 0, 2, 1))
    group = np.zeros((P, 4), np.float32)
    place = np.zeros((P, 4), np.float32)
    for p in range(P):
        group[p, p // 32] = 1
        place[p, p // HD % 4] = 1
    by_chunk = lambda b: b.reshape(-1, P).T
    vals = {"l0_b1": by_chunk(L0["b1"]), "l1_b1": by_chunk(L1["ff_b1"]), "bt": L2["bt"], "bv": L2["bv"],
            "bg": L2["bg"], "sa_g": L3["sa_ln_g"], "sa_b": L3["sa_ln_b"], "caq_g": L3["ca_q_ln_g"],
            "caq_b": L3["ca_q_ln_b"], "cakv_g": L3["ca_kv_ln_g"], "cakv_b": L3["ca_kv_ln_b"],
            "moe_g": L3["moe_ln_g"], "moe_b": L3["moe_ln_b"], "sa_bq": L3["sa_in_b"][:D],
            "sa_bk": L3["sa_in_b"][D:2 * D], "ca_bq": L3["ca_in_b"][:D], "ca_bk": L3["ca_in_b"][D:2 * D],
            "e_b1": L3["e_fc1_b"].reshape(NE * FC, P).T, "group": group, "place": place}
    T["cols"] = c(np.concatenate([vals[n].reshape(P, -1) for n in COLS], axis=1))
    misc = np.zeros(D, np.float32)
    misc[:NE] = L3["router_b"]
    misc[NE:2 * NE] = np.arange(NE)
    rowvals = {"ln01_g": L0["ln1_g"], "ln01_b": L0["ln1_b"], "l0_b2": L0["b2"], "ln02_g": L0["ln2_g"],
               "ln02_b": L0["ln2_b"], "msa_bo": L1["msa_bo"], "ln11_g": L1["ln1_g"], "ln11_b": L1["ln1_b"],
               "ca1_bo": L1["ca_bo"], "ln12_g": L1["ln2_g"], "ln12_b": L1["ln2_b"], "l1_b2": L1["ff_b2"],
               "ln13_g": L1["ln3_g"], "ln13_b": L1["ln3_b"], "l2_g": L2["gamma"], "l2_b": L2["beta"],
               "sa_bv": L3["sa_in_b"][2 * D:], "sa_bo": L3["sa_out_b"], "ca_bv": L3["ca_in_b"][2 * D:],
               "ca_bo": L3["ca_out_b"], "misc": misc}
    T["rows"] = c(np.stack([rowvals[n] for n in ROWS]))
    T["ident"] = np.eye(P, dtype=np.float32)
    pos = np.arange(KL - 1, -1, -1, dtype=np.float32)
    freq = (1.0 / 10000.0 ** (np.arange(0, D, 2, dtype=np.float32) / D)).astype(np.float32)
    angle = pos[:, None] * freq
    T["peT"] = c(np.concatenate([np.sin(angle), np.cos(angle)], axis=-1).T.astype(np.float32))
    return T


def kernel(**inputs):
    import concourse.bacc as _bacc
    from concourse.bass_utils import run_bass_kernel_spmd as _run

    T = lay_out(inputs)
    nc = _bacc.Bacc("TRN2", target_bir_lowering=False, num_devices=1)
    a = {n: nc.dram_tensor(n, v.shape, mybir.dt.from_np(v.dtype), kind="ExternalInput").ap() for n, v in T.items()}
    out = nc.dram_tensor("out_0_dram", T["x"].shape, F32, kind="ExternalOutput").ap()
    build(nc, a, out)
    r = _run(nc, [T], core_ids=[0])
    return r.results[0]["out_0_dram"]
```

```python
from contextlib import ExitStack

import numpy as np

import concourse.bass as bass
from concourse import mybir

F32 = mybir.dt.float32
F32R = mybir.dt.float32r
BF16 = mybir.dt.bfloat16
U8 = mybir.dt.uint8
I32 = mybir.dt.int32
U32 = mybir.dt.uint32
ALU = mybir.AluOpType
ACT = mybir.ActivationFunctionType
AX = mybir.AxisListType

P = 128
S = 64
D = 128
H = 16
KL = 128
DK = 64
HD = D // H
FF = 512
FC = FF // P
NE = 8
QT = 4
EPS = 1e-5
MASKED = -1e20
LOWEST = -3e38
WORK = 13472

COLS = {}
for _name, _n in (("l0_b1", FC), ("l1_b1", FC), ("bt", 1), ("bv", 1), ("bg", 1), ("sa_g", 1), ("sa_b", 1),
                  ("caq_g", 1), ("caq_b", 1), ("cakv_g", 1), ("cakv_b", 1), ("moe_g", 1), ("moe_b", 1),
                  ("sa_bq", 1), ("sa_bk", 1), ("ca_bq", 1), ("ca_bk", 1), ("e_b1", NE * FC),
                  ("group", 4), ("place", 4)):
    COLS[_name] = (sum(n for _, n in COLS.values()), _n)
NCOLS = sum(n for _, n in COLS.values())
ROWS = ("ln01_g", "ln01_b", "l0_b2", "ln02_g", "ln02_b", "msa_bo", "ln11_g", "ln11_b", "ca1_bo", "ln12_g",
        "ln12_b", "l1_b2", "ln13_g", "ln13_b", "l2_g", "l2_b", "sa_bv", "sa_bo", "ca_bv", "ca_bo", "misc")


def wait(e, sem, value):
    if not (isinstance(value, int) and value <= 0):
        e.wait_ge(sem, value)


def wait_alone(e, sem, value):
    wait(e, sem, value)
    e.nop(nofuse=True)


def opening(k):
    return isinstance(k, int) and k == -1


def walk(e, units, step):
    step(-1, 0, True, False, False)
    step(-1, 1, True, True, False)
    with e.Fori(0, units // 2 - 1) as k:
        step(k, 0, True, True, True)
        step(k, 1, True, True, True)
    step(units // 2 - 1, 0, False, True, True)
    step(units // 2 - 1, 1, False, False, True)


def walk_late(e, units, step):
    step(-1, 0, True, False, False, False)
    step(-1, 1, True, True, False, False)
    step(0, 0, True, True, True, False)
    step(0, 1, True, True, True, True)
    if units > 4:
        with e.Fori(1, units // 2 - 1) as k:
            step(k, 0, True, True, True, True)
            step(k, 1, True, True, True, True)
    step(units // 2 - 1, 0, False, True, True, True)
    step(units // 2 - 1, 1, False, False, True, True)
    step(units // 2, 0, False, False, False, True)


def build(nc, a, out):
    NB = a["x"].shape[0]
    NT = NB * S // P
    NQ = NT // QT
    ctx = ExitStack()
    with ctx:
        def sb(name, shape, dt=F32):
            return ctx.enter_context(nc.sbuf_tensor("sb_" + name, shape, dt))

        sems = {}

        def sem(name):
            if name not in sems:
                sems[name] = ctx.enter_context(nc.semaphore("is_" + name))
            return sems[name]

        PS = ctx.enter_context(nc.psum_tensor("PS", [P, 8, 512], F32))
        X = sb("X", [P, NT, D])
        cols = sb("cols", [P, NCOLS])
        rows = sb("rows", [P, len(ROWS), D])
        ident = sb("ident", [P, P])
        twice = sb("twice", [S, P], BF16)
        token_mask = sb("token_mask", [P, NT])
        half_power = sb("half_power", [P, QT])
        next_stats = sb("next_stats", [P, QT, 6])
        next_moments = sb("next_moments", [P, QT, 2])
        next_var_eps = sb("next_var_eps", [P, QT])
        tile_mean = sb("tile_mean", [P, NT])
        tile_inv_std = sb("tile_inv_std", [P, NT])
        ctx_mean = sb("ctx_mean", [P, NT])
        ctx_inv_std = sb("ctx_inv_std", [P, NT])
        c_stats = sb("c_stats", [P, 1, 6])
        c_moments = sb("c_moments", [P, 1, 2])
        c_var_eps = sb("c_var_eps", [P, 1])
        zeros = sb("zeros", [P, QT])
        no_weights = zeros[:, 0:1].unsqueeze(2).to_broadcast([P, 1, FF])
        w_l0ff1 = sb("w_l0ff1", [P, FF])
        w_l0ff2 = sb("w_l0ff2", [P, FC, D])
        w_l1ff1 = sb("w_l1ff1", [P, FF])
        w_l1ff2 = sb("w_l1ff2", [P, FC, D])
        w_att = {n: sb("w_" + n, [P, 3, D]) for n in ("msa", "ca1", "sa", "ca")}
        w_out = {n: sb("wo_" + n, [S, 2, D]) for n in ("msa", "ca1", "sa", "ca")}
        w_l2 = sb("w_l2", [P, 4, D])
        w_router = sb("w_router", [P, NE])
        w_eb2 = sb("w_eb2", [NE, D])
        pooled = sb("pooled", [P, NB])
        with ExitStack() as first:
            QR_parts, tables, rel_bias, probs_area, probsT = (
                first.enter_context(nc.sbuf_tensor("sb_" + name, shape, dt))
                for name, shape, dt in (("QR_parts", [P, 2, H, KL], F32R), ("tables", [P, 2, H, P], F32),
                                        ("rel_bias", [P, H, KL], F32), ("probs", [P, 2 * 2 * 8 * KL], F32), ("probsT", [P, 2, 8 * P], F32)))
        w_e2 = sb("w_e2", [P, NE, FC, D])
        w_e1_parts = [sb("w_e1_" + part, [P, NE, FF], F32R) for part in ("hi", "lo")]
        qT_parts = [sb("qT_" + part, [P, 2, QT * P], F32R) for part in ("hi", "lo")]
        w_ff1_parts = [[sb(f"w_l{i}ff1_{part}", [P, FF], F32R) for part in ("hi", "lo")] for i in range(2)]
        w_e1 = sb("w_e1", [P, NE, FF])
        work = sb("work", [P, WORK])

        def col(name):
            at, n = COLS[name]
            return cols[:, at:at + n]

        def row(name):
            return rows[:, ROWS.index(name), :]

        taken = [0]

        def carve(shape, start=None):
            if start is not None:
                taken[0] = start
            n = int(np.prod(shape))
            v = work[:, taken[0]:taken[0] + n]
            taken[0] += n
            assert taken[0] <= WORK, taken[0]
            if len(shape) == 2:
                v = v.rearrange("p (a b) -> p a b", a=shape[0])
            elif len(shape) == 3:
                v = v.rearrange("p (a b c) -> p a b c", a=shape[0], b=shape[1])
            elif len(shape) == 4:
                v = v.rearrange("p (a b c d) -> p a b c d", a=shape[0], b=shape[1], c=shape[2])
            return v

        loads = [(cols[:, :], a["cols"]), (rows[:, :, :], a["rows"].partition_broadcast(P)),
                 (ident[:, :], a["ident"]), (token_mask[:, :], a["token_mask"]),
                 (w_l0ff1[:, :], a["l0_W1"]), (w_l0ff2[:, :, :], a["l0_W2"]),
                 (w_l1ff1[:, :], a["l1_W1"]), (w_l1ff2[:, :, :], a["l1_W2"]),
                 (w_l2[:, :, :], a["l2_W"]), (w_router[:, :], a["router"]), (w_eb2[:, :], a["e_b2"]),
                 (X[:, :, :], a["x"].rearrange("(t b) s d -> (b s) t d", b=2))]
        loads += [(w_att[n][:, :, :], a["w_" + n]) for n in w_att]
        loads += [(w_out[n][:, :, :], a["wo_" + n]) for n in w_out]

        def meet(e, phase):
            e.drain().then_inc(sem("phase_done"), 1)
            e.wait_ge(sem("phase_done"), 5 * (phase + 1))

        def moments_vector(e, kind, count, source, stats, moments, tiles):
            wait_alone(e, sem(kind + "_moments_kept"), count - 1)
            for t in range(tiles):
                ins = e.bn_stats(stats[:, t], source(t))
            ins.then_inc(sem(kind + "_stats"), 1)
            wait_alone(e, sem(kind + "_stats"), count)
            for t in range(tiles):
                ins = e.bn_aggr(moments[:, t], stats[:, t])
            ins.then_inc(sem(kind + "_moments"), 1)

        def inv_std_pool(e, kind, count, moments, var_eps, mean, inv_std, t0, tiles):
            wait_alone(e, sem(kind + "_moments"), count)
            e.tensor_scalar(var_eps[:, 0:tiles], moments[:, 0:tiles, 1], EPS, None, ALU.add)\
                .then_inc(sem(kind + "_var_eps"), 1)
            e.tensor_tensor(mean[:, bass.ds(t0, tiles)], moments[:, 0:tiles, 0], zeros[:, 0:tiles], ALU.add)
            wait_alone(e, sem(kind + "_var_eps"), count)
            e.tensor_tensor(inv_std[:, bass.ds(t0, tiles)], var_eps[:, 0:tiles], half_power[:, 0:tiles], ALU.pow)\
                .then_inc(sem(kind + "_moments_kept"), 1)

        def x_moments_vector(e, kind, count, t0, tiles):
            moments_vector(e, kind, count, lambda t: X[:, bass.ds(t0 + t, 1)].rearrange("p a d -> p (a d)"),
                           next_stats, next_moments, tiles)

        def x_inv_std_pool(e, kind, count, t0, tiles):
            inv_std_pool(e, kind, count, next_moments, next_var_eps, tile_mean, tile_inv_std, t0, tiles)

        QK, VO = (tables[:, i] for i in range(2))
        own_hi, own_lo = (sb("own_" + part, [P, 2, P], F32R) for part in ("hi", "lo"))
        wqT = carve((H, P), 0)[0:DK]
        wkT = carve((H, P))[0:DK]
        wvT = carve((H, P))[0:DK]
        wo0 = carve((H, P))[0:DK]
        wr = carve((H, DK))
        peT = carve((KL,))
        rT = carve((H, KL))[0:DK]
        cbT = carve((H,))[0:DK]
        pbT = carve((H,))[0:DK]
        pb_wide = carve((H, P))[0:DK]
        key_bias = sb("key_bias", [P, H])
        l0_loads = {"rel": [(wr, a["l0_Wr"]), (peT, a["peT"]), (cbT, a["l0_cb"]), (pbT, a["l0_pb"])],
                    "qk": [(wkT, a["l0_WkT"]), (wqT, a["l0_WqT"])],
                    "vo": [(wvT, a["l0_WvT"]), (wo0, a["l0_Wo"])]}

        kv_tok = carve((2, 2, D), 0)
        kvT = carve((2, 2, 2, S))
        qkT = carve((2, H, S))
        rel_sb = carve((H, KL + 1))
        rel_shifted = carve((2, 8, KL))
        probs = probs_area[:, :].rearrange("p (u b h k) -> p u b h k", u=2, b=2, h=8)
        pkvT = carve((H, P))
        row_max = carve((2, 2, 8))
        neg_max = carve((2, 2, 8))
        row_sum = carve((2, 2, 8))
        row_inv = carve((2, 2, 8))
        kv_in = sb("kv_in", [P, 2, 2, D])
        mask8 = ctx.enter_context(nc.sbuf_tensor("mask8", [S, 2, 2, KL], U8))
        mask_bias = ctx.enter_context(nc.sbuf_tensor("mask_bias", [S, 2, 2, KL], BF16))
        scratch = nc.dram_tensor("rel_scratch", [2, H, S * (KL + 1)], F32, kind="Internal").ap()
        SCALE0 = float(DK) ** -0.5
        ctx_in, x_in = a["ctx"], a["x"]

        def use_head(m):
            return m if isinstance(m, int) and m < 2 else 9 * m

        def use_rel(m, g):
            return 2 + g if isinstance(m, int) and m == 0 else 9 * m + 1 + g

        def use_qk(m, g):
            return use_rel(m, g) + 4

        def kept_head(m):
            return m if isinstance(m, int) and m < 2 else 5 * m

        def kept_rel(m, g):
            return 2 + g if isinstance(m, int) and m == 0 else 5 * m + 1 + g

        def l0_sync(e, c):
            def load_tokens(u, m):
                e.dma_start(kv_in[0:S, u], ctx_in[bass.ds(2 * m, 2)].rearrange("b s d -> s b d"))\
                    .then_inc(sem(f"l0_kv_loaded{u}"), 16)
                e.dma_start(kv_in[S:P, u], x_in[bass.ds(2 * m, 2)].rearrange("b s d -> s b d"))\
                    .then_inc(sem(f"l0_kv_loaded{u}"), 16)
                e.dma_start(mask8[:, u], a["mask0"][bass.ds(2 * m, 2)].rearrange("b s k -> s b k"))\
                    .then_inc(sem(f"l0_mask_loaded{u}"), 16)

            for kind in ("rel", "qk", "vo"):
                for dst, src in l0_loads[kind]:
                    e.dma_start(dst, src).then_inc(sem(f"l0_{kind}_loaded"), 16)
            for u in range(2):
                load_tokens(u, u)
            for dst, src in loads:
                e.dma_start(dst, src).then_inc(sem("params_loaded"), 16)
            e.wait_ge(sem("params_loaded"), 16 * len(loads))
            e.dma_start(w_e1[:, :, :], a["e_W1"]).then_inc(sem("experts_loaded"), 16)
            meet(e, 0)

            def shift_relative(m):
                wait_alone(e, sem("l0_rel_kept"), kept_rel(m, 3) + 1)
                wait_alone(e, sem("l0_rel_read"), 32 * m)
                for b in range(2):
                    e.dma_start(scratch[b].rearrange("h (q c) -> q h c", q=S), rel_sb[S * b:S * b + S])\
                        .then_inc(sem("l0_rel_written"), 16)
                wait_alone(e, sem("l0_rel_written"), 32 * m + 32)
                wait_alone(e, sem("l0_rows_done"), 4 * m)
                for hh in range(2):
                    src = scratch[:, :, S:S + S * KL].rearrange("b (n two) (q k) -> two q (b n) k", two=2, q=S)
                    e.dma_start(rel_shifted[S * hh:S * hh + S].rearrange("p b n k -> p (b n) k"), src[hh])\
                        .then_inc(sem("l0_rel_read"), 16)

            def step(k, u, head, front, back):
                n = 2 * k + u
                m = n + 2
                if head and not opening(k):
                    wait_alone(e, sem("l0_kv_kept"), m - 1)
                    wait_alone(e, sem("l0_projected"), use_qk(m - 1, 0))
                    wait_alone(e, sem("l0_mask_ready"), m - 1)
                    load_tokens(u, m)
                if front:
                    shift_relative(n + 1)
            walk(e, NT, step)

        def l0_pool(e, c):
            e.memset(half_power[:, :], -0.5)
            e.memset(zeros[:, :], 0.0).then_inc(sem("no_weights"), 1)
            e.wait_ge(sem("params_loaded"), 16 * len(loads))
            for i in range(2):
                e.tensor_copy(twice[:, S * i:S * i + S], ident[0:S, 0:S])
            meet(e, 0)
            e.memset(rel_sb[:, :, 0:1], 0.0).then_inc(sem("l0_rel_pad"), 1)

            def step(k, u, head, front, back):
                if head:
                    m = 2 * k + u + 2
                    e.wait_ge(sem(f"l0_mask_loaded{u}"), 16 * (k + 2))
                    wait_alone(e, sem("l0_rows_done"), 4 * (m - 1))
                    e.tensor_scalar(mask_bias[:, u], mask8[:, u], MASKED, None, ALU.mult)\
                        .then_inc(sem("l0_mask_ready"), 1)
                if back:
                    n = 2 * k + u
                    x_inv_std_pool(e, "l0", n + 1, n, 1)
                if head:
                    m = 2 * k + u + 2
                    wait_alone(e, sem(f"l0_kv_loaded{u}"), 32 * (k + 2))
                    wait_alone(e, sem("l0_context_done"), 8 * (m - 1))
                    e.tensor_copy(kv_tok[:, u], kv_in[:, u]).then_inc(sem("l0_kv_kept"), 1)
            walk(e, NT, step)

        def l0_tensor(e, c):
            used = [0]

            def bank():
                n = used[0]
                used[0] += 1
                wait(e, sem("l0_table_drained"), n - 1)
                return PS[:, n % 2]
            e.wait_ge(sem("l0_rel_loaded"), 64)
            for q in range(4):
                o = bank()
                for i in range(4):
                    h = 4 * q + i
                    ins = e.matmul(o[0:DK, i * KL:(i + 1) * KL], wr[:, h], peT, start=True, stop=True)
                ins.then_inc(sem("l0_table_done"), 1)
            e.wait_ge(sem("l0_qk_loaded"), 32)
            o = bank()
            for h in range(H):
                ins = e.matmul(o[:, h:h + 1], wkT[:, h], cbT[:, h:h + 1], start=True, stop=True)
            ins.then_inc(sem("l0_table_done"), 1)
            e.wait_ge(sem("l0_table_drained"), 4)
            e.wait_ge(sem("l0_pb_wide"), 1)
            for left, right in ((wqT, wkT), (wqT, rT), (pb_wide, rT), (wvT, wo0)):
                if left is wvT:
                    e.wait_ge(sem("l0_vo_loaded"), 32)
                for q in range(4):
                    o = bank()
                    for i in range(4):
                        h = 4 * q + i
                        ins = e.matmul(o[:, i * P:(i + 1) * P], left[:, h], right[:, h], start=True, stop=True)
                    ins.then_inc(sem("l0_table_done"), 1)
            meet(e, 0)

            def step(k, u, head, front, back):
                n = 2 * k + u
                m, v = n + 1, 1 - u
                if opening(k):
                    transpose_kv(k, u, n + 2)
                shift = 0 if opening(k) else u
                if front:
                    e.wait_ge(sem("l0_own_split"), m + 1)
                    for g in range(4):
                        wait(e, sem("l0_rows_done"), 4 * (m - 1) + g + 1)
                        product_in_parts(e, PS[:, 4 + g], (own_hi[:, v], own_lo[:, v]),
                                         [QR_parts[:, i, 4 * g:4 * g + 4] for i in range(2)])\
                            .then_inc(sem("l0_projected"), 1)

                def drained(j):
                    if j == 0:
                        wait(e, sem("l0_pkvT_kept"), 4 * n)
                    elif j == 1:
                        wait(e, sem("l0_out_added"), n)
                    elif j < 6:
                        e.wait_ge(sem("l0_probsT_kept"), 4 * n + j - 1)
                    else:
                        e.wait_ge(sem("l0_pkvT_kept"), 4 * n + j - 5)
                    return PS[:, 2 + (u + j) % 2]

                def transpose_probs(b):
                    e.wait_ge(sem("l0_probs_ready"), 2 * n + b + 1)
                    for g in range(2):
                        o = drained(2 * b + g)
                        for i in range(4):
                            ins = e.transpose(o[:, i * P:i * P + P], probs[:, u, b, 4 * g + i], ident[:, :])
                        ins.then_inc(sem("l0_context_done"), 1)
                if front:
                    for g in range(4):
                        if opening(k) and g == 1:
                            e.wait_ge(sem("l0_rel_kept"), 2)
                        wait(e, sem("l0_qk_kept"), 4 * m + max(g - 1, 0))
                        for i in range(4):
                            ins = e.matmul(PS[:, (shift + g) % 2, i * P:i * P + P], QK[:, 4 * g + i],
                                           kvT[:, v, 1], start=True, stop=True)
                        ins.then_inc(sem("l0_projected"), 1)
                if back:
                    transpose_probs(0)
                    transpose_probs(1)
                if head and not opening(k):
                    transpose_kv(k, u, n + 2)
                if front:
                    e.wait_ge(sem("l0_qk_kept"), 4 * m + 4)
                    e.wait_ge(sem("l0_mask_ready"), m + 1)
                    for g in range(4):
                        b = g // 2
                        o = PS[:, 4 + g]
                        e.wait_ge(sem("l0_rel_kept"), kept_rel(m, g) + 1)
                        e.matmul(o.rearrange("p (i k) -> p i k", i=4), twice[:, :],
                                 mask_bias[:, v, b].unsqueeze(1).to_broadcast([S, 4, KL]),
                                 start=True, stop=False, skip_group_check=True)
                        for i in range(4):
                            h = 8 * (g % 2) + 2 * i
                            ins = e.matmul(o[:, i * KL:i * KL + KL], qkT[:, b, h:h + 2],
                                           kvT[:, v, :, b], start=False, stop=(i == 3), skip_group_check=True)
                        ins.then_inc(sem("l0_scores_done"), 1)
                if back:
                    for g in range(2):
                        for b in range(2):
                            o = drained(4 + 2 * g + b)
                            if g == b == 0:
                                e.wait_ge(sem("l0_kv_kept"), n + 1)
                            e.wait_ge(sem("l0_probsT_kept"), 4 * n + 2 * b + g + 1)
                            e.matmul(o, kv_tok[:, u, b], probsT[:, b, 512 * g:512 * g + 512], start=True, stop=True)\
                                .then_inc(sem("l0_context_done"), 1)
                    o = drained(8)
                    for h in range(H):
                        if h % 8 == 0:
                            e.wait_ge(sem("l0_pkvT_kept"), 4 * n + 2 + h // 4)
                        ins = e.matmul(o[:, 0:D], pkvT[:, h], VO[:, h], start=(h == 0), stop=(h == H - 1))
                    ins.then_inc(sem("l0_out_done"), 1)
            def transpose_kv(k, u, m):
                e.wait_ge(sem(f"l0_kv_loaded{u}"), 32 * (k + 2))
                if not opening(k):
                    e.wait_ge(sem("l0_qk_kept"), 4 * (m - 1) + 3)
                for b in range(2):
                    ins = e.transpose(PS[:, u, b * P:b * P + P], kv_in[:, u, b], ident[:, :])
                ins.then_inc(sem("l0_projected"), 1)
            walk(e, NT, step)

        def l0_vector(e, c):
            e.wait_ge(sem("l0_rel_loaded"), 64)
            e.tensor_copy(pb_wide, pbT.unsqueeze(2).to_broadcast([DK, H, P])).then_inc(sem("l0_pb_wide"), 1)
            n = 0
            for q in range(4):
                e.wait_ge(sem("l0_table_done"), n + 1)
                e.tensor_copy(rT[:, 4 * q:4 * q + 4], PS[0:DK, n % 2].rearrange("p (i k) -> p i k", i=4))\
                    .then_inc(sem("l0_table_drained"), 1)
                n += 1
            e.wait_ge(sem("l0_table_done"), n + 1)
            e.tensor_copy(key_bias[:, :], PS[:, n % 2, 0:H]).then_inc(sem("l0_table_drained"), 1)
            n += 1
            for table in ("QK", "QR", "rel_bias", "VO"):
                for q in range(4):
                    product = PS[:, n % 2].rearrange("p (i k) -> p i k", i=4)
                    e.wait_ge(sem("l0_table_done"), n + 1)
                    if table == "QR":
                        hi, lo = (QR_parts[:, i, 4 * q:4 * q + 4] for i in range(2))
                        e.tensor_copy(hi, product).then_inc(sem("l0_QR_rounded"), 1)
                        e.wait_ge(sem("l0_QR_rounded"), q + 1)
                        ins = e.tensor_tensor(lo, product, hi.bitcast(F32), ALU.subtract)
                    else:
                        to = {"QK": QK, "rel_bias": rel_bias, "VO": VO}[table]
                        ins = e.tensor_copy(to[:, 4 * q:4 * q + 4], product)
                    ins.then_inc(sem("l0_table_drained"), 1)
                    n += 1
            meet(e, 0)
            e.wait_ge(sem("l0_rel_pad"), 1)

            def keep_kvT(m, u):
                e.wait_ge(sem("l0_projected"), use_head(m) + 1)
                wait(e, sem("l0_scores_done"), 4 * (m - 1))
                transposed = PS[:, u, 0:2 * KL].rearrange("p (b a k) -> p a b k", b=2, a=2)
                e.tensor_copy(kvT[:, u], transposed)
                e.tensor_copy(own_hi[:, u].rearrange("p (b k) -> p b k", b=2), transposed[:, 1])\
                    .then_inc(sem("l0_rel_kept"), 1)
                e.wait_ge(sem("l0_rel_kept"), kept_head(m) + 1)
                e.tensor_tensor(own_lo[:, u].rearrange("p (b k) -> p b k", b=2), kvT[:, u, 1],
                                own_hi[:, u].bitcast(F32).rearrange("p (b k) -> p b k", b=2), ALU.subtract)\
                    .then_inc(sem("l0_own_split"), 1)

            def step(k, u, head, front, back):
                n = 2 * k + u
                m, v = n + 1, 1 - u
                shift = 0 if opening(k) else u
                if opening(k):
                    keep_kvT(n + 2, u)

                def normalise(b):
                    e.wait_ge(sem("l0_exp_done"), 2 * n + b + 1)
                    e.reciprocal(row_inv[:, u, b], row_sum[:, u, b]).then_inc(sem("l0_inv_ready"), 1)
                    e.wait_ge(sem("l0_inv_ready"), 2 * n + b + 1)
                    e.tensor_tensor(probs[:, u, b], probs[:, u, b],
                                    row_inv[:, u, b].unsqueeze(2).to_broadcast([P, 8, KL]), ALU.mult)\
                        .then_inc(sem("l0_probs_ready"), 1)
                if front:
                    wait(e, sem("l0_rel_written"), 32 * m)
                    for g in range(4):
                        e.wait_ge(sem("l0_projected"), use_rel(m, g) + 1)
                        e.tensor_tensor(rel_sb[:, 4 * g:4 * g + 4, 1:KL + 1],
                                        PS[:, 4 + g].rearrange("p (i k) -> p i k", i=4),
                                        rel_bias[:, 4 * g:4 * g + 4], ALU.add)\
                            .then_inc(sem("l0_rel_kept"), 1)
                if back:
                    normalise(0)
                    normalise(1)
                    wait(e, sem("l0_context_done"), 8 * n)
                    for j in range(4):
                        b, g = j // 2, j % 2
                        e.wait_ge(sem("l0_context_done"), 8 * n + j + 1)
                        e.tensor_copy(probsT[:, b, 512 * g:512 * g + 512], PS[:, 2 + (u + j) % 2])\
                            .then_inc(sem("l0_probsT_kept"), 1)
                if head and not opening(k):
                    keep_kvT(n + 2, u)
                if front:
                    e.wait_ge(sem("l0_rel_read"), 32 * m + 32)
                    for g in range(4):
                        b = g // 2
                        wait_alone(e, sem("l0_scores_done"), 4 * m + g + 1)
                        for i in range(4):
                            hp = 4 * (g % 2) + i
                            ins = e.tensor_tensor_reduce(probs[:, v, b, hp], PS[:, 4 + g, i * KL:i * KL + KL],
                                                         rel_shifted[:, b, hp], 1.0, LOWEST, ALU.add, ALU.max,
                                                         row_max[:, v, b, hp:hp + 1])
                        ins.then_inc(sem("l0_rows_done"), 1)
                        if g % 2:
                            e.wait_ge(sem("l0_rows_done"), 4 * m + g + 1)
                            e.tensor_scalar(neg_max[:, v, b], row_max[:, v, b], -SCALE0, None, ALU.mult)\
                                .then_inc(sem("l0_max_ready"), 1)
                if back:
                    e.wait_ge(sem("l0_out_done"), n + 1)
                    xn = X[:, bass.ds(n, 1)].rearrange("p a d -> p (a d)")
                    e.tensor_tensor(xn, xn, PS[:, 2 + u, 0:D], ALU.add).then_inc(sem("l0_out_added"), 1)
                if back:
                    wait_alone(e, sem("l0_out_added"), n + 1)
                    x_moments_vector(e, "l0", n + 1, n, 1)
            walk(e, NT, step)

        def l0_scalar(e, c):
            meet(e, 0)

            def step(k, u, head, front, back):
                n = 2 * k + u
                if front:
                    m = n + 1
                    shift = 0 if opening(k) else u
                    wait(e, sem("l0_scores_done"), 4 * m)
                    for g in range(4):
                        e.wait_ge(sem("l0_projected"), use_qk(m, g) + 1)
                        for i in range(4):
                            h = 4 * g + i
                            ins = e.activation(qkT[:, :, h], PS[:, (shift + g) % 2, i * P:i * P + P]
                                               .rearrange("p (b q) -> p b q", b=2), ACT.Identity,
                                               bias=key_bias[:, h:h + 1])
                        ins.then_inc(sem("l0_qk_kept"), 1)
                if back:
                    wait(e, sem("l0_out_done"), n)
                    for g in range(2):
                        for b in range(2):
                            j = 4 + 2 * g + b
                            e.wait_ge(sem("l0_context_done"), 8 * n + j + 1)
                            e.activation(pkvT[:, 8 * g:8 * g + 8, S * b:S * b + S],
                                         PS[:, 2 + (u + j) % 2].rearrange("p (h q) -> p h q", h=8), ACT.Copy)\
                                .then_inc(sem("l0_pkvT_kept"), 1)
                if front:
                    m, v = n + 1, 1 - u
                    for b in range(2):
                        e.wait_ge(sem("l0_max_ready"), 2 * m + b + 1)
                        for hp in range(8):
                            ins = e.activation(probs[:, v, b, hp], probs[:, v, b, hp], ACT.Exp,
                                               bias=neg_max[:, v, b, hp:hp + 1], scale=SCALE0,
                                               accum_out=row_sum[:, v, b, hp:hp + 1])
                        ins.then_inc(sem("l0_exp_done"), 1)
            walk(e, NT, step)

        y_tok = carve((2, D), 0)
        c_tok = carve((2, D))
        c_norm = carve((2, D))
        norm_a = carve((D,))
        norm_b = carve((D,))
        yT = carve((2, P))
        cT = carve((2, P))
        q_sb = carve((2, P))
        k_sb = carve((2, P))
        q_masked = carve((2, 2, 4, S))
        k_masked = carve((2, 2, 4, S))
        v_ones = sb("v_ones", [P, 2, 2, H, HD + 1])
        att_probs = carve((2, 2, 8, S))
        att_max = carve((2, 2, 8))
        att_probsT = carve((2, 4, P))
        den_inv = carve((2, 8))
        att_ctx = carve((2, 8, HD))
        att_ctxT = carve((2, 2, S))[0:S]
        mask_int = ctx.enter_context(nc.sbuf_tensor("mask_int", [S, 2, 2, S], I32))
        att_mask = ctx.enter_context(nc.sbuf_tensor("att_mask", [S, 2, 2, S], BF16))

        SCALE1, SCALE3 = float(D) ** -0.5, float(HD) ** -0.5
        ATT = [
            dict(name="msa", i=0, g="ln02_g", b="ln02_b", token_mask=True, mask="mask1", mi=0, cross=None,
                 bias="msa_bo", scale=SCALE1),
            dict(name="ca1", i=1, g="ln11_g", b="ln11_b", token_mask=False, mask="mask2", mi=1, cross=0,
                 bias="ca1_bo", scale=SCALE1),
            dict(name="sa", i=2, pre=("sa_g", "sa_b"), mask=None, cross=None, bias="sa_bo", scale=SCALE3,
                 qkb=("sa_bq", "sa_bk"), vb="sa_bv"),
            dict(name="ca", i=3, pre=("caq_g", "caq_b"), mask=None, cross=1, cnorm=("cakv_g", "cakv_b"),
                 bias="ca_bo", scale=SCALE3, qkb=("ca_bq", "ca_bk"), vb="ca_bv"),
        ]

        def tile(t):
            return X[:, bass.ds(t, 1)].rearrange("p a d -> p (a d)")

        def att_sync(e, c):
            cross, masked = c["cross"], c["mask"]

            def step(k, u, head, front, back, late=False):
                m = 2 * k + u + 2
                if head and cross is not None:
                    if "cnorm" in c:
                        wait_alone(e, sem("att_c_normed"), m - 1)
                    else:
                        wait_alone(e, sem("att_transposed"), c["i"] * NT + m - 1)
                        wait_alone(e, sem("ctx_moments"), m - 1)
                    e.dma_start(c_tok[:, u], ctx_in[bass.ds(2 * m, 2)].rearrange("b s d -> (b s) d"))\
                        .then_inc(sem(f"att_c_loaded{u}"), 16)
                if head and masked:
                    wait_alone(e, sem("att_mask_ready"), c["mi"] * NT + m - 1)
                    e.dma_start(mask_int[:, u], a[masked][bass.ds(2 * m, 2)].rearrange("b s k -> s b k"))\
                        .then_inc(sem(f"att_mask_loaded{u}"), 16)
            walk(e, NT, step)

        def att_pool(e, c):
            base = c["i"] * NT
            cross = c["cross"]

            def step(k, u, head, front, back, late=False):
                n = base + 2 * k + u
                if front:
                    m, v = n + 1, 1 - u
                    e.wait_ge(sem("att_qk_kept"), m + 1)
                    wait(e, sem("att_scores_done"), 2 * (m - 1))
                    e.tensor_tensor(k_masked[:, v], k_sb[:, v].rearrange("p (b k) -> p b k", b=2).unsqueeze(2)
                                    .to_broadcast([P, 2, 4, S]),
                                    col("place").unsqueeze(1).unsqueeze(3).to_broadcast([P, 2, 4, S]), ALU.mult)\
                        .then_inc(sem("att_k_masked"), 1)
                if head:
                    m = n + 2
                    if c["mask"]:
                        kk = (c["mi"] * NT) // 2 + k
                        e.wait_ge(sem(f"att_mask_loaded{u}"), 16 * (kk + 2))
                        wait_alone(e, sem("att_scores_done"), 2 * (m - 1))
                        e.tensor_scalar(att_mask[:, u], mask_int[:, u], 0.0, MASKED, ALU.is_equal, ALU.mult)\
                            .then_inc(sem("att_mask_ready"), 1)
                    e.wait_ge(sem("att_normed"), m + 1)
                    xn = tile(m - base)
                    e.tensor_tensor(xn, xn if "pre" in c else y_tok[:, u], row(c["bias"]), ALU.add)\
                        .then_inc(sem("att_base_ready"), 1)
                if cross == 0 and front:
                    m = n + 1
                    inv_std_pool(e, "ctx", m + 1 - base, c_moments, c_var_eps, ctx_mean, ctx_inv_std, m - base, 1)
                if late:
                    x_inv_std_pool(e, "att", n, n - 1 - base, 1)
            walk_late(e, NT, step)

        def att_tensor(e, c):
            base = c["i"] * NT
            cross, norm_cross = c["cross"], "cnorm" in c
            wq, wk, wv = (w_att[c["name"]][:, i] for i in range(3))
            wo = w_out[c["name"]]

            def step(k, u, head, front, back, late=False):
                n = base + 2 * k + u
                if front:
                    m, v = n + 1, 1 - u
                    e.wait_ge(sem("att_T_kept"), m + 1)
                    wait(e, sem("att_qk_kept"), m)
                    wait(e, sem("att_v_ready"), m)
                    src = yT if cross is None else cT
                    e.matmul(PS[:, 1, 0:P], wq, yT[:, v], start=True, stop=True)
                    e.matmul(PS[:, 1, P:2 * P], wk, src[:, v], start=True, stop=True)
                    for b in range(2):
                        for half in range(2):
                            ins = e.matmul(PS[S * half:S * half + S, 1, (2 + b) * P:(3 + b) * P],
                                           src[:, v, S * b:S * b + S], wv, start=True, stop=True)
                    ins.then_inc(sem("att_projected"), 1)
                if late:
                    e.wait_ge(sem("att_ctx_ready"), n)
                    wait_alone(e, sem("att_added"), n - 1)
                    for b in range(2):
                        ins = e.transpose(PS[0:S, 7, P * b:P * b + P], att_ctx[:, b], ident[:, :])
                    ins.then_inc(sem("att_ctxT_done"), 1)
                if back:
                    for b in range(2):
                        e.wait_ge(sem("att_exp_done"), 2 * n + b + 1)
                        for i in range(4):
                            ins = e.transpose(PS[:, 4 + b, i * P:i * P + P], att_probs[:, u, b, 2 * i:2 * i + 2],
                                              ident[:, :])
                        ins.then_inc(sem("att_probsT_done"), 1)
                if late:
                    e.wait_ge(sem("att_ctxT_kept"), n)
                    for gg in range(2):
                        ins = e.matmul(PS[:, 7, 2 * P:3 * P], att_ctxT[:, gg], wo[:, gg], start=(gg == 0),
                                       stop=(gg == 1))
                    ins.then_inc(sem("att_out_done"), 1)
                if front:
                    e.wait_ge(sem("att_q_masked"), m + 1)
                    e.wait_ge(sem("att_k_masked"), m + 1)
                    if c["mask"]:
                        e.wait_ge(sem("att_mask_ready"), m - base + c["mi"] * NT + 1)
                    for b in range(2):
                        wait(e, sem("att_shifted"), 2 * m + b - 1)
                        o = PS[:, 2 + b]
                        if c["mask"]:
                            e.matmul(o.rearrange("p (i k) -> p i k", i=8), twice[:, :],
                                     att_mask[:, v, b].unsqueeze(1).to_broadcast([S, 8, S]),
                                     start=True, stop=False, skip_group_check=True)
                        for g in range(2):
                            ins = e.matmul(o[:, 256 * g:256 * g + 256], q_masked[:, v, b, 2 * g:2 * g + 2],
                                           k_masked[:, v, b], start=not c["mask"], stop=True,
                                           skip_group_check=True)
                        ins.then_inc(sem("att_scores_done"), 1)
                if head:
                    e.wait_ge(sem("att_normed"), n + 3)
                    wait(e, sem("att_T_kept"), n + 2)
                    ins = e.transpose(PS[:, 0, 0:P], y_tok[:, u], ident[:, :])
                    if cross is not None:
                        if norm_cross:
                            e.wait_ge(sem("att_c_normed"), n - base + 3)
                            ins = e.transpose(PS[:, 0, P:2 * P], c_norm[:, u], ident[:, :])
                        else:
                            e.wait_ge(sem(f"att_c_loaded{u}"), 16 * (cross * NT // 2 + k + 2))
                            ins = e.transpose(PS[:, 0, P:2 * P], c_tok[:, u], ident[:, :])
                    ins.then_inc(sem("att_transposed"), 1)
                if back:
                    e.wait_ge(sem("att_probsT_kept"), 2 * n + 2)
                    wait(e, sem("att_ctx_ready"), n)
                    for b in range(2):
                        for i in range(4):
                            for gg in range(2):
                                h = 4 * (2 * (i // 2) + gg) + 2 * (i % 2)
                                ins = e.matmul(PS[S * gg:S * gg + S, 6, (4 * b + i) * 18:(4 * b + i) * 18 + 18],
                                               att_probsT[:, b, i, S * gg:S * gg + S], v_ones[:, u, b, h:h + 2],
                                               start=True, stop=True, skip_group_check=True)
                    ins.then_inc(sem("att_pv_done"), 1)
            walk_late(e, NT, step)

        def att_vector(e, c):
            base = c["i"] * NT
            cross, norm_cross = c["cross"], "cnorm" in c
            if c["i"] == 0:
                e.memset(v_ones[:, :], 0.0).then_inc(sem("att_v_zeroed"), 1)
                e.wait_ge(sem("att_v_zeroed"), 1)
                for u in range(2):
                    for half in range(2):
                        e.memset(v_ones[S * half:S * half + S, u].rearrange("p b (h two) w -> p (b h) two w", two=2)
                                 [:, :, half, HD:HD + 1], 1.0).then_inc(sem("att_v_zeroed"), 1)
                e.wait_ge(sem("att_v_zeroed"), 5)

            def mask_queries(m, v):
                e.wait_ge(sem("att_qk_kept"), m + 1)
                wait(e, sem("att_scores_done"), 2 * (m - 1))
                e.tensor_tensor(q_masked[:, v], q_sb[:, v].rearrange("p (b q) -> p b q", b=2).unsqueeze(2)
                                .to_broadcast([P, 2, 4, S]),
                                col("group").unsqueeze(1).unsqueeze(3).to_broadcast([P, 2, 4, S]), ALU.mult)\
                    .then_inc(sem("att_q_masked"), 1)

            def step(k, u, head, front, back, late=False):
                n = base + 2 * k + u
                if head:
                    m = n + 2
                    at = bass.ds(m - base, 1)
                    mean = tile_mean[:, at]
                    wait(e, sem("att_transposed"), m - 1)
                    wait(e, sem("att_base_ready"), m - 1)
                    if "pre" in c:
                        if norm_cross:
                            e.wait_ge(sem(f"att_c_loaded{u}"), 16 * (cross * NT // 2 + k + 2))
                            e.tensor_scalar(c_norm[:, u], c_tok[:, u], ctx_mean[:, at], ctx_inv_std[:, at],
                                            ALU.subtract, ALU.mult).then_inc(sem("att_c_normed"), 1)
                        e.tensor_scalar(y_tok[:, u], tile(m - base), mean, tile_inv_std[:, at],
                                        ALU.subtract, ALU.mult).then_inc(sem("att_normed"), 1)
                        if front:
                            mask_queries(n + 1, 1 - u)
                    else:
                        wait(e, sem("att_normed"), m)
                        e.scalar_tensor_tensor(norm_a, tile(m - base), mean, row(c["g"]), ALU.subtract, ALU.mult)\
                            .then_inc(sem("att_scaled"), 1)
                        if front:
                            mask_queries(n + 1, 1 - u)
                        e.wait_ge(sem("att_scaled"), m + 1)
                        to = norm_b if c["token_mask"] else y_tok[:, u]
                        ins = e.scalar_tensor_tensor(to, norm_a, tile_inv_std[:, at], row(c["b"]), ALU.mult, ALU.add)
                        if c["token_mask"]:
                            ins.then_inc(sem("att_biased"), 1)
                            e.wait_ge(sem("att_biased"), m + 1)
                            ins = e.tensor_scalar(y_tok[:, u], norm_b, token_mask[:, bass.ds(m - base, 1)], None, ALU.mult)
                        ins.then_inc(sem("att_normed"), 1)
                if front:
                    m, v = n + 1, 1 - u
                    if not head:
                        mask_queries(m, v)
                    if cross == 0:
                        moments_vector(e, "ctx", m - base + 1, lambda t: c_tok[:, v], c_stats, c_moments, 1)
                        e.tensor_reduce(pooled[:, bass.ds(2 * (m - base), 2)],
                                        cT[:, v].rearrange("p (b s) -> p b s", b=2), AX.X, ALU.add)
                    e.wait_ge(sem("att_projected"), m + 1)
                    wait(e, sem("att_pv_done"), m - 1)
                    for half in range(2):
                        r = slice(S * half, S * half + S)
                        to = v_ones[r, v].rearrange("p b (h two) w -> p (b h) two w", two=2)[:, :, half, 0:HD]
                        of = PS[r, 1, 2 * P:4 * P].rearrange("p (n two w) -> p n two w", two=2, w=HD)[:, :, half]
                        if "vb" in c:
                            for b in range(2):
                                vb = row(c["vb"])[r].rearrange("p (h two w) -> p h two w", two=2, w=HD)[:, :, half]
                                ins = e.tensor_tensor(to[:, 8 * b:8 * b + 8], of[:, 8 * b:8 * b + 8], vb, ALU.add)
                        else:
                            ins = e.tensor_copy(to, of)
                    ins.then_inc(sem("att_v_ready"), 1)
                if late:
                    e.wait_ge(sem("att_out_done"), n)
                    e.wait_ge(sem("att_base_ready"), n)
                    e.tensor_tensor(tile(n - base - 1), tile(n - base - 1), PS[:, 7, 2 * P:3 * P], ALU.add)\
                        .then_inc(sem("att_added"), 1)
                    wait_alone(e, sem("att_added"), n)
                    x_moments_vector(e, "att", n, n - 1 - base, 1)
                if front:
                    m = n + 1
                    for b in range(2):
                        s3 = PS[:, 2 + b].rearrange("p (i k) -> p i k", i=8)
                        e.wait_ge(sem("att_scores_done"), 2 * m + b + 1)
                        e.tensor_reduce(att_max[:, v, b], s3, AX.X, ALU.max).then_inc(sem("att_max_ready"), 1)
                        e.wait_ge(sem("att_max_ready"), 2 * m + b + 1)
                        e.tensor_tensor(att_probs[:, v, b], s3, att_max[:, v, b].unsqueeze(2)
                                        .to_broadcast([P, 8, S]), ALU.subtract).then_inc(sem("att_shifted"), 1)
                if back:
                    e.wait_ge(sem("att_pv_done"), n + 1)
                    pv = PS[:, 6, 0:16 * (HD + 1)].rearrange("p (b i w) -> p b i w", b=2, w=HD + 1)
                    e.reciprocal(den_inv, pv[:, :, :, HD]).then_inc(sem("att_den_ready"), 1)
                    e.wait_ge(sem("att_den_ready"), n + 1)
                    wait(e, sem("att_ctxT_done"), n)
                    e.tensor_tensor(att_ctx, pv[:, :, :, 0:HD], den_inv.unsqueeze(3).to_broadcast([P, 2, 8, HD]),
                                    ALU.mult).then_inc(sem("att_ctx_ready"), 1)
            walk_late(e, NT, step)

        def att_scalar(e, c):
            base = c["i"] * NT
            cross = c["cross"]

            def step(k, u, head, front, back, late=False):
                n = base + 2 * k + u
                if front:
                    m, v = n + 1, 1 - u
                    e.wait_ge(sem("att_projected"), m + 1)
                    wait(e, sem("att_q_masked"), m - 1)
                    wait(e, sem("att_k_masked"), m - 1)
                    for i, (to, of) in enumerate(((q_sb, PS[:, 1, 0:P]), (k_sb, PS[:, 1, P:2 * P]))):
                        if "qkb" in c:
                            ins = e.activation(to[:, v], of, ACT.Identity, bias=col(c["qkb"][i]))
                        else:
                            ins = e.activation(to[:, v], of, ACT.Copy)
                    ins.then_inc(sem("att_qk_kept"), 1)
                if late:
                    e.wait_ge(sem("att_ctxT_done"), n)
                    wait(e, sem("att_out_done"), n - 1)
                    e.activation(att_ctxT.rearrange("p g b q -> p b g q"),
                                 PS[0:S, 7, 0:2 * P].rearrange("p (b g q) -> p b g q", b=2, g=2), ACT.Copy)\
                        .then_inc(sem("att_ctxT_kept"), 1)
                if back:
                    wait(e, sem("att_pv_done"), n)
                    for b in range(2):
                        e.wait_ge(sem("att_probsT_done"), 2 * n + b + 1)
                        e.activation(att_probsT[:, b].rearrange("p i q -> p (i q)"), PS[:, 4 + b], ACT.Copy)\
                            .then_inc(sem("att_probsT_kept"), 1)
                if head:
                    e.wait_ge(sem("att_transposed"), n + 3)
                    wait(e, sem("att_projected"), n + 1)
                    if cross == 0:
                        wait(e, sem("att_v_ready"), n + 1)
                    for i, (to, of, gb) in enumerate(((yT, PS[:, 0, 0:P], c.get("pre")),
                                                      (cT, PS[:, 0, P:2 * P], c.get("cnorm")))[:1 if cross is None else 2]):
                        if gb:
                            ins = e.activation(to[:, u], of, ACT.Identity, bias=col(gb[1]), scale=col(gb[0]))
                        else:
                            ins = e.activation(to[:, u], of, ACT.Copy)
                    ins.then_inc(sem("att_T_kept"), 1)
                if front:
                    for b in range(2):
                        e.wait_ge(sem("att_shifted"), 2 * m + b + 1)
                        e.activation(att_probs[:, v, b], att_probs[:, v, b], ACT.Exp, scale=c["scale"])\
                            .then_inc(sem("att_exp_done"), 1)
            walk_late(e, NT, step)

        q_tok = carve((2, QT, D), 0)
        qT = carve((2, QT * P))
        qT_hi, qT_lo = qT_parts
        qn_a = carve((QT, D))
        qn_b = carve((QT, D))
        quad_end = taken[0]

        def tiles(m):
            return X[:, bass.ds(QT * m, QT)]

        def quad_norm_vector(e, base, k, u, gb, masked, done_before):
            m = base + 2 * k + u + 2
            wait(e, sem("quad_transposed"), m - 1)
            if done_before is not None:
                wait(e, done_before, m - 1)
            one = lambda t: X[:, bass.ds(QT * (m - base) + t, 1)].rearrange("p a d -> p (a d)")
            mean = lambda t: tile_mean[:, bass.ds(QT * (m - base) + t, 1)]
            inv = lambda t: tile_inv_std[:, bass.ds(QT * (m - base) + t, 1)]
            if gb is None:
                for t in range(QT):
                    ins = e.tensor_scalar(q_tok[:, u, t], one(t), mean(t), inv(t),
                                          ALU.subtract, ALU.mult)
                ins.then_inc(sem("quad_normed"), 1)
                return
            wait(e, sem("quad_normed"), m)
            for t in range(QT):
                ins = e.scalar_tensor_tensor(qn_a[:, t], one(t), mean(t), row(gb[0]),
                                             ALU.subtract, ALU.mult)
            ins.then_inc(sem("quad_scaled"), 1)
            e.wait_ge(sem("quad_scaled"), m + 1)
            for t in range(QT):
                ins = e.scalar_tensor_tensor(qn_b[:, t] if masked else q_tok[:, u, t], qn_a[:, t],
                                             inv(t), row(gb[1]), ALU.mult, ALU.add)
            if masked:
                ins.then_inc(sem("quad_shifted"), 1)
                e.wait_ge(sem("quad_shifted"), m + 1)
                ins = e.tensor_tensor(q_tok[:, u], qn_b, token_mask[:, bass.ds(QT * (m - base), QT)].unsqueeze(2)
                                      .to_broadcast([P, QT, D]), ALU.mult)
            ins.then_inc(sem("quad_normed"), 1)

        def quad_transpose_tensor(e, base, k, u):
            m = base + 2 * k + u + 2
            e.wait_ge(sem("quad_normed"), m + 1)
            wait(e, sem("quad_T_kept"), m)
            for t in range(QT):
                ins = e.transpose(PS[:, 0, P * t:P * t + P], q_tok[:, u, t], ident[:, :])
            ins.then_inc(sem("quad_transposed"), 1)

        def quad_keep_scalar(e, base, k, u, gb=None, split=True):
            m = base + 2 * k + u + 2
            e.wait_ge(sem("quad_transposed"), m + 1)
            if gb:
                ins = e.activation(qT[:, u], PS[:, 0], ACT.Identity, bias=col(gb[1]), scale=col(gb[0]))
            else:
                ins = e.activation(qT[:, u], PS[:, 0], ACT.Copy)
            if split:
                if gb:
                    ins = e.activation(qT_hi[:, u], PS[:, 0], ACT.Identity, bias=col(gb[1]), scale=col(gb[0]))
                else:
                    ins = e.activation(qT_hi[:, u], PS[:, 0], ACT.Copy)
            ins.then_inc(sem("quad_T_kept"), 1)

        def quad_split_pool(e, base, split_base, k, u):
            m = 2 * k + u + 2
            e.wait_ge(sem("quad_T_kept"), base + m + 1)
            e.tensor_tensor(qT_lo[:, u], qT[:, u], qT_hi[:, u].bitcast(F32), ALU.subtract)\
                .then_inc(sem("quad_T_split"), 1)

        def product_in_parts(e, o, left, right):
            for i, (l, r) in enumerate(((0, 0), (0, 1), (1, 0))):
                ins = e.matmul(o, left[l], right[r], start=(i == 0), stop=(i == 2))
            return ins

        ff_h = carve((2, FC, QT * P), quad_end)
        FFN = [dict(i=0, q=0, w1=w_l0ff1, w2=w_l0ff2, b1="l0_b1", b2="l0_b2", norm=("ln01_g", "ln01_b"), masked=True),
               dict(i=1, q=1, w1=w_l1ff1, w2=w_l1ff2, b1="l1_b1", b2="l1_b2", norm=("ln12_g", "ln12_b"), masked=False)]

        def ff_sync(e, c):
            if c["i"] == 0:
                e.dma_start(w_e2[:, :, :, :], a["e_W2"]).then_inc(sem("experts_loaded"), 16)

        def ff_pool(e, c):
            hi, lo = w_ff1_parts[c["i"]]
            e.wait_ge(sem("ff_rounded"), c["i"] + 1)
            e.tensor_tensor(lo[:, :], c["w1"][:, :], hi[:, :].bitcast(F32), ALU.subtract)\
                .then_inc(sem("ff_weights_split"), 1)

            def step(k, u, head, front, back):
                if head:
                    m = 2 * k + u + 2
                    e.wait_ge(sem("quad_normed"), c["q"] * NQ + m + 1)
                    e.tensor_tensor(tiles(m), q_tok[:, u], row(c["b2"]).unsqueeze(1).to_broadcast([P, QT, D]), ALU.add)\
                        .then_inc(sem("ff_base_ready"), 1)
                    quad_split_pool(e, c["q"] * NQ, c["i"] * NQ, k, u)
                if back:
                    n = 2 * k + u
                    x_inv_std_pool(e, "ff", c["i"] * NQ + n + 1, QT * n, QT)
                    if c["i"] == 0:
                        w, hi, lo = (x[:, bass.ds(n, 1)] for x in (w_e1, *w_e1_parts))
                        e.wait_ge(sem("experts_loaded"), 16)
                        e.tensor_tensor(hi, w, no_weights, ALU.add).then_inc(sem("expert_rounded"), 1)
                        wait_alone(e, sem("expert_rounded"), n + 1)
                        e.tensor_tensor(lo, w, hi.bitcast(F32), ALU.subtract)
            walk(e, NQ, step)

        def ff_tensor(e, c):
            e.wait_ge(sem("ff_weights_split"), c["i"] + 1)

            def step(k, u, head, front, back):
                n = c["i"] * NQ + 2 * k + u
                if back:
                    e.wait_ge(sem("ff_h_ready"), FC * n + FC)
                    wait(e, sem("ff_added"), n)
                    for t in range(QT):
                        for f in range(FC):
                            ins = e.matmul(PS[:, 5 + u, D * t:D * t + D], ff_h[:, u, f, P * t:P * t + P], c["w2"][:, f],
                                           start=(f == 0), stop=(f == FC - 1))
                    ins.then_inc(sem("ff_out_done"), 1)
                if head:
                    quad_transpose_tensor(e, c["q"] * NQ, k, u)
                if front:
                    m, v = n + 1, 1 - u
                    e.wait_ge(sem("quad_T_split"), c["i"] * NQ + 2 * k + u + 2)
                    for f in range(FC):
                        wait(e, sem("ff_h_ready"), FC * (m - 1) + f + 1)
                        product_in_parts(e, PS[:, 1 + f], [w[:, P * f:P * f + P] for w in w_ff1_parts[c["i"]]],
                                         (qT_hi[:, v], qT_lo[:, v]))\
                            .then_inc(sem("ff_h_done"), 1)
            walk(e, NQ, step)

        def ff_vector(e, c):
            base = c["q"] * NQ

            def step(k, u, head, front, back):
                n = c["i"] * NQ + 2 * k + u
                if head:
                    quad_norm_vector(e, base, k, u, c["norm"], c["masked"], sem("ff_base_ready"))
                if back:
                    e.wait_ge(sem("ff_out_done"), n + 1)
                    e.wait_ge(sem("ff_base_ready"), n + 1)
                    xs = tiles(n - c["i"] * NQ)
                    e.tensor_tensor(xs, xs, PS[:, 5 + u].rearrange("p (t d) -> p t d", t=QT), ALU.add)\
                        .then_inc(sem("ff_added"), 1)
                    wait_alone(e, sem("ff_added"), n + 1)
                    x_moments_vector(e, "ff", n + 1, QT * (n - c["i"] * NQ), QT)
            walk(e, NQ, step)

        def ff_scalar(e, c):
            e.activation(w_ff1_parts[c["i"]][0][:, :], c["w1"][:, :], ACT.Copy).then_inc(sem("ff_rounded"), 1)

            def step(k, u, head, front, back):
                n = c["i"] * NQ + 2 * k + u
                if head:
                    wait(e, sem("ff_h_done"), FC * (n + 1))
                    quad_keep_scalar(e, c["q"] * NQ, k, u)
                if front:
                    m, v = n + 1, 1 - u
                    wait(e, sem("ff_out_done"), m - 1)
                    for f in range(FC):
                        e.wait_ge(sem("ff_h_done"), FC * m + f + 1)
                        e.activation(ff_h[:, v, f], PS[:, 1 + f], ACT.Relu, bias=col(c["b1"])[:, f:f + 1])\
                            .then_inc(sem("ff_h_ready"), 1)
            walk(e, NQ, step)

        NBU = QT * P // S
        vis = carve((NB,), quad_end)
        vis_gate = carve((NB,))
        half_bg = carve((1,))
        ones = carve((P,))
        tp = carve((2, QT * P))
        tv = carve((NBU, S))
        routes = carve((2, NBU, S))
        gate = carve((NBU, S))
        wv = carve((NBU, S))
        gated = carve((NBU, S))
        fused = carve((2, QT * P))
        l2_max = carve((NBU,))
        l2_sum = carve((NBU,))
        l2_inv = carve((NBU,))
        half_vis_over_sum = carve((NBU,))
        vis_gate_over_sum = carve((NBU,))
        f_stats = carve((QT, 6))
        f_moments = carve((QT, 2))
        f_var_eps = carve((QT,))
        f_inv_std = carve((QT,))
        f_scaled = carve((QT, D))
        LQ = 2
        by_batch = lambda x: x.rearrange("p (b s) -> p b s", b=NBU)
        over_tokens = lambda x: x.unsqueeze(2).to_broadcast([P, NBU, S])

        def l2_pool(e, c):
            e.wait_ge(sem("l2_vis_kept"), 2)

            def step(k, u, head, front, back, late):
                n = 2 * k + u
                m, v = n + 1, 1 - u
                if front:
                    e.wait_ge(sem("l2_tp_ready"), m + 1)
                    wait(e, sem("l2_agree_done"), m)
                    e.tensor_tensor(tv, by_batch(tp[:, v]), over_tokens(vis[:, bass.ds(NBU * m, NBU)]), ALU.mult)\
                        .then_inc(sem("l2_tv_ready"), 1)
                if late:
                    wait_alone(e, sem("l2_f_moments"), n)
                    e.tensor_scalar(f_var_eps, f_moments[:, :, 1], EPS, None, ALU.add).then_inc(sem("l2_f_var_eps"), 1)
                if back:
                    e.wait_ge(sem("l2_sums_used"), n + 1)
                    wait(e, sem("l2_gated"), n)
                    e.tensor_tensor(wv, routes[:, u], over_tokens(half_vis_over_sum), ALU.mult).then_inc(sem("l2_wv_ready"), 1)
                if late:
                    wait_alone(e, sem("l2_f_var_eps"), n)
                    e.tensor_tensor(f_inv_std, f_var_eps, half_power[:, :], ALU.pow).then_inc(sem("l2_f_inv_std"), 1)
                if back:
                    e.wait_ge(sem("l2_gated"), n + 1)
                    e.wait_ge(sem("l2_feat_kept"), n + 1)
                    e.tensor_tensor(by_batch(fused[:, u]), by_batch(fused[:, u]), gated, ALU.add)\
                        .then_inc(sem("l2_fused"), 1)
                if late:
                    x_inv_std_pool(e, "l2", n, QT * (n - 1), QT)
            walk_late(e, NQ, step)

        def l2_tensor(e, c):
            e.matmul(PS[:, 5, 0:NB], w_l2[:, 1], pooled[:, :], start=True, stop=True).then_inc(sem("l2_vis_done"), 1)
            e.wait_ge(sem("l2_vis_kept"), 1)
            e.matmul(PS[:, 5, 128:128 + NB], w_l2[:, 3], vis, start=True, stop=True).then_inc(sem("l2_vis_done"), 1)
            e.wait_ge(sem("l2_ones"), 1)

            def step(k, u, head, front, back, late):
                n = 2 * k + u
                if front:
                    m, v = n + 1, 1 - u
                    e.wait_ge(sem("quad_T_kept"), LQ * NQ + m + 1)
                    wait(e, sem("l2_tp_ready"), m)
                    e.matmul(PS[:, 1], w_l2[:, 0], qT[:, v], start=True, stop=True).then_inc(sem("l2_tp_done"), 1)
                    e.wait_ge(sem("l2_tp_ready"), m + 1)
                    wait(e, sem("l2_gate_summed"), m - 1)
                    e.matmul(PS[:, 3 + 3 * v], w_l2[:, 2], tp[:, v], start=True, stop=True)\
                        .then_inc(sem("l2_gate_done"), 1)
                    e.wait_ge(sem("l2_tv_ready"), m + 1)
                    wait(e, sem("l2_agree_shifted"), m)
                    e.matmul(PS[:, 2], ones, tv.rearrange("p b s -> p (b s)"), start=True, stop=True)\
                        .then_inc(sem("l2_agree_done"), 1)
                if head:
                    quad_transpose_tensor(e, LQ * NQ, k, u)
                if back:
                    e.wait_ge(sem("l2_fused"), n + 1)
                    wait(e, sem("l2_f_scaled"), n - 1)
                    for t in range(QT):
                        ins = e.transpose(PS[:, 4 + 3 * u, P * t:P * t + P], fused[:, u, P * t:P * t + P], ident[:, :])
                    ins.then_inc(sem("l2_f_transposed"), 1)
            walk_late(e, NQ, step)

        def l2_vector(e, c):
            e.memset(ones, 1.0).then_inc(sem("l2_ones"), 1)
            e.tensor_scalar(half_bg, col("bg"), 0.5, None, ALU.mult).then_inc(sem("l2_half_bg"), 1)
            e.wait_ge(sem("l2_vis_kept"), 2)

            def step(k, u, head, front, back, late):
                n = 2 * k + u
                m, v = n + 1, 1 - u
                if late:
                    e.wait_ge(sem("l2_f_transposed"), n)
                    wait(e, sem("l2_f_moments"), n - 1)
                    for t in range(QT):
                        ins = e.bn_stats(f_stats[:, t], PS[:, 4 + 3 * v, P * t:P * t + P])
                    ins.then_inc(sem("l2_f_stats"), 1)
                if back:
                    e.wait_ge(sem("l2_exp_done"), n + 1)
                    wait(e, sem("l2_inv_ready"), n)
                    e.tensor_reduce(l2_sum, routes[:, u], AX.X, ALU.add).then_inc(sem("l2_sum_ready"), 1)
                if late:
                    wait_alone(e, sem("l2_f_stats"), n)
                    wait_alone(e, sem("l2_f_inv_std"), n - 1)
                    wait_alone(e, sem("l2_f_scaled"), n - 1)
                    for t in range(QT):
                        ins = e.bn_aggr(f_moments[:, t], f_stats[:, t])
                    ins.then_inc(sem("l2_f_moments"), 1)
                if back:
                    e.wait_ge(sem("l2_sum_ready"), n + 1)
                    wait(e, sem("l2_sums_used"), n)
                    e.reciprocal(l2_inv, l2_sum).then_inc(sem("l2_inv_ready"), 1)
                    e.wait_ge(sem("l2_inv_ready"), n + 1)
                    wait(e, sem("l2_gate_summed"), n)
                    wait(e, sem("l2_wv_ready"), n)
                    e.tensor_tensor(vis_gate_over_sum, vis_gate[:, bass.ds(NBU * n, NBU)], l2_inv, ALU.mult)
                    e.scalar_tensor_tensor(half_vis_over_sum, vis[:, bass.ds(NBU * n, NBU)], 0.5, l2_inv,
                                           ALU.mult, ALU.mult)\
                        .then_inc(sem("l2_sums_used"), 1)
                if late:
                    e.wait_ge(sem("l2_f_moments"), n)
                    wait(e, sem("l2_out_ready"), n - 1)
                    for t in range(QT):
                        ins = e.scalar_tensor_tensor(f_scaled[:, t], PS[:, 4 + 3 * v, P * t:P * t + P],
                                                     f_moments[:, t, 0:1], row("l2_g"), ALU.subtract, ALU.mult)
                    ins.then_inc(sem("l2_f_scaled"), 1)
                if back:
                    e.wait_ge(sem("l2_sums_used"), n + 1)
                    wait(e, sem("l2_gated"), n)
                    e.tensor_tensor(gate, routes[:, u], over_tokens(vis_gate_over_sum), ALU.mult)\
                        .then_inc(sem("l2_gate_routed"), 1)
                    e.wait_ge(sem("l2_gate_routed"), n + 1)
                    e.wait_ge(sem("l2_gate_done"), n + 1)
                    e.tensor_tensor(gate, gate, by_batch(PS[:, 3 + 3 * u]), ALU.add).then_inc(sem("l2_gate_summed"), 1)
                if front:
                    e.wait_ge(sem("l2_agree_done"), m + 1)
                    wait(e, sem("l2_agree_shifted"), m)
                    e.tensor_reduce(l2_max, by_batch(PS[:, 2]), AX.X, ALU.max).then_inc(sem("l2_max_ready"), 1)
                    e.wait_ge(sem("l2_max_ready"), m + 1)
                    wait(e, sem("l2_gate_summed"), m - 1)
                    wait(e, sem("l2_wv_ready"), m - 1)
                    e.tensor_tensor(routes[:, v], by_batch(PS[:, 2]), over_tokens(l2_max), ALU.subtract)\
                        .then_inc(sem("l2_agree_shifted"), 1)
                if late:
                    e.wait_ge(sem("l2_f_scaled"), n)
                    e.wait_ge(sem("l2_f_inv_std"), n)
                    for t in range(QT):
                        ins = e.scalar_tensor_tensor(X[:, bass.ds(QT * (n - 1) + t, 1)].rearrange("p a d -> p (a d)"),
                                                     f_scaled[:, t], f_inv_std[:, t:t + 1], row("l2_b"),
                                                     ALU.mult, ALU.add)
                    ins.then_inc(sem("l2_out_ready"), 1)
                if back:
                    e.wait_ge(sem("l2_gate_tanh"), n + 1)
                    e.wait_ge(sem("l2_wv_ready"), n + 1)
                    wait(e, sem("l2_fused"), n)
                    e.scalar_tensor_tensor(gated, gate, 1.0, wv, ALU.add, ALU.mult).then_inc(sem("l2_gated"), 1)
                if head:
                    quad_norm_vector(e, LQ * NQ, k, u, ("ln13_g", "ln13_b"), False, None)
                if late:
                    wait_alone(e, sem("l2_out_ready"), n)
                    x_moments_vector(e, "l2", n, QT * (n - 1), QT)
            walk_late(e, NQ, step)

        def l2_scalar(e, c):
            e.wait_ge(sem("l2_vis_done"), 1)
            e.activation(vis, PS[:, 5, 0:NB], ACT.Identity, bias=col("bv"), scale=1.0 / S).then_inc(sem("l2_vis_kept"), 1)
            e.wait_ge(sem("l2_vis_done"), 2)
            e.activation(vis_gate, PS[:, 5, 128:128 + NB], ACT.Copy).then_inc(sem("l2_vis_kept"), 1)
            e.wait_ge(sem("l2_half_bg"), 1)

            def step(k, u, head, front, back, late):
                n = 2 * k + u
                m, v = n + 1, 1 - u
                if front:
                    e.wait_ge(sem("l2_tp_done"), m + 1)
                    wait(e, sem("l2_gate_done"), m - 1)
                    wait(e, sem("l2_tv_ready"), m - 1)
                    e.activation(tp[:, v], PS[:, 1], ACT.Identity, bias=col("bt")).then_inc(sem("l2_tp_ready"), 1)
                    wait(e, sem("l2_f_transposed"), m - 1)
                    e.activation(fused[:, v], qT[:, v], ACT.Copy).then_inc(sem("l2_feat_kept"), 1)
                if back:
                    e.wait_ge(sem("l2_gate_summed"), n + 1)
                    e.activation(gate, gate, ACT.Tanh, scale=0.5, bias=half_bg).then_inc(sem("l2_gate_tanh"), 1)
                if front:
                    e.wait_ge(sem("l2_agree_shifted"), m + 1)
                    e.activation(routes[:, v], routes[:, v], ACT.Exp, scale=2.0).then_inc(sem("l2_exp_done"), 1)
                if head:
                    wait(e, sem("l2_tp_done"), n + 1)
                    wait(e, sem("l2_feat_kept"), n + 1)
                    quad_keep_scalar(e, LQ * NQ, k, u, split=False)
            walk_late(e, NQ, step)

        logits = carve((QT, NE), quad_end)
        top = carve((QT, NE))
        gap = carve((QT,))
        gap_exp = carve((QT,))
        euler = carve((QT,))
        gap_den = carve((QT,))
        gates = carve((2, QT))
        top_at_f = carve((2, QT))
        hit = carve((2, QT, NE))
        mix = carve((2, QT, NE))
        mixT = carve((QT, P))[0:NE]
        e_h = carve((2, FC, QT * P))
        top_at = sb("top_at", [P, QT, NE], U32)
        MQ = 3

        def moe_pool(e, c):
            e.memset(euler, float(np.e)).then_inc(sem("moe_euler"), 1)
            e.wait_ge(sem("moe_euler"), 1)

            def step(k, u, head, front, back):
                if front:
                    m = 2 * k + u + 1
                    e.wait_ge(sem("moe_gap_ready"), m + 1)
                    wait(e, sem("moe_gate1_ready"), m)
                    e.tensor_tensor(gap_exp, euler, gap, ALU.pow).then_inc(sem("moe_gap_exp"), 1)
                if head:
                    quad_split_pool(e, MQ * NQ, 2 * NQ, k, u)
            walk(e, NQ, step)

        def moe_tensor(e, c):
            e.wait_ge(sem("experts_loaded"), 32)

            def step(k, u, head, front, back):
                n = 2 * k + u
                m, v = n + 1, 1 - u
                if front:
                    e.wait_ge(sem("quad_T_kept"), MQ * NQ + m + 1)
                    wait(e, sem("moe_base_ready"), m)
                    for t in range(QT):
                        ins = e.matmul(PS[:, 1, NE * t:NE * t + NE], qT[:, v, P * t:P * t + P], w_router[:, :],
                                       start=True, stop=True)
                    ins.then_inc(sem("moe_logits_done"), 1)

                def up(x):
                    if x == 0:
                        e.wait_ge(sem("quad_T_split"), 2 * NQ + n + 1)
                    for f in range(FC):
                        if x:
                            e.wait_ge(sem("moe_h_ready"), (n * NE + x - 1) * FC + f + 1)
                        product_in_parts(e, PS[:, 2 + f],
                                         [w[:, x, P * f:P * f + P] for w in w_e1_parts],
                                         (qT_hi[:, u], qT_lo[:, u]))\
                            .then_inc(sem("moe_h_done"), 1)

                def down(x):
                    e.wait_ge(sem("moe_h_ready"), (n * NE + x + 1) * FC)
                    wait(e, sem("moe_added"), n * NE + max(x - 1, 0))
                    for t in range(QT):
                        for f in range(FC):
                            ins = e.matmul(PS[:, 6 + x % 2, D * t:D * t + D], e_h[:, x % 2, f, P * t:P * t + P],
                                           w_e2[:, x, f], start=(f == 0), stop=(f == FC - 1))
                    ins.then_inc(sem("moe_down_done"), 1)
                for x in range(NE + 1):
                    if back and x < NE:
                        up(x)
                    if back and x:
                        down(x - 1)
                    if front and x == 1:
                        e.wait_ge(sem("moe_mix_ready"), m + 1)
                        for t in range(QT):
                            ins = e.transpose(PS[0:NE, 1, P * t:P * t + P], mix[:, v, t], ident[:, :])
                        ins.then_inc(sem("moe_mixT_done"), 1)
                    if front and x == 3:
                        e.wait_ge(sem("moe_mixT_kept"), m + 1)
                        for t in range(QT):
                            ins = e.matmul(PS[:, 1, D * t:D * t + D], mixT[:, t], w_eb2[:, :], start=True, stop=True)
                        ins.then_inc(sem("moe_biases_done"), 1)
                    if head and x == 5:
                        quad_transpose_tensor(e, MQ * NQ, k, u)
            walk(e, NQ, step)

        def moe_vector(e, c):
            def step(k, u, head, front, back):
                n = 2 * k + u
                m, v = n + 1, 1 - u
                if front:
                    misc = row("misc")
                    each = lambda x: x.unsqueeze(2).to_broadcast([P, QT, NE])
                    e.wait_ge(sem("moe_logits_done"), m + 1)
                    e.tensor_tensor(logits, PS[:, 1, 0:QT * NE].rearrange("p (t x) -> p t x", t=QT),
                                    misc[:, 0:NE].unsqueeze(1).to_broadcast([P, QT, NE]), ALU.add)\
                        .then_inc(sem("moe_logits_ready"), 1)
                    wait_alone(e, sem("moe_logits_ready"), m + 1)
                    for t in range(QT):
                        ins = e.max(top[:, t], logits[:, t])
                    ins.then_inc(sem("moe_top_ready"), 1)
                    e.wait_ge(sem("moe_top_ready"), m + 1)
                    e.tensor_tensor(gap, top[:, :, 1], top[:, :, 0], ALU.subtract).then_inc(sem("moe_gap_ready"), 1)
                    for t in range(QT):
                        ins = e.max_index(top_at[:, t], top[:, t], logits[:, t])
                    ins.then_inc(sem("moe_top_at_ready"), 1)
                    e.wait_ge(sem("moe_top_at_ready"), m + 1)
                    e.tensor_copy(top_at_f, top_at[:, :, 0:2].rearrange("p t i -> p i t")).then_inc(sem("moe_at_f_ready"), 1)
                    e.wait_ge(sem("moe_gap_exp"), m + 1)
                    e.tensor_scalar(gap_den, gap_exp, 1.0, None, ALU.add).then_inc(sem("moe_den_ready"), 1)
                    e.wait_ge(sem("moe_at_f_ready"), m + 1)
                    for i in range(2):
                        ins = e.tensor_tensor(hit[:, i], misc[:, NE:2 * NE].unsqueeze(1).to_broadcast([P, QT, NE]),
                                              each(top_at_f[:, i]), ALU.is_equal)
                    ins.then_inc(sem("moe_hits_ready"), 1)
                    e.wait_ge(sem("moe_den_ready"), m + 1)
                    e.reciprocal(gates[:, 0], gap_den).then_inc(sem("moe_gate0_ready"), 1)
                    e.wait_ge(sem("moe_gate0_ready"), m + 1)
                    e.tensor_tensor(gates[:, 1], gap_exp, gates[:, 0], ALU.mult).then_inc(sem("moe_gate1_ready"), 1)
                    e.wait_ge(sem("moe_hits_ready"), m + 1)
                    e.wait_ge(sem("moe_gate1_ready"), m + 1)
                    for i in range(2):
                        ins = e.tensor_tensor(hit[:, i], hit[:, i], each(gates[:, i]), ALU.mult)
                    ins.then_inc(sem("moe_parts_ready"), 1)
                    e.wait_ge(sem("moe_parts_ready"), m + 1)
                    e.tensor_tensor(mix[:, v], hit[:, 0], hit[:, 1], ALU.add).then_inc(sem("moe_mix_ready"), 1)
                for x in range(NE):
                    if back:
                        e.wait_ge(sem("moe_down_done"), n * NE + x + 1)
                        if x:
                            e.wait_ge(sem("moe_added"), n * NE + x)
                        else:
                            e.wait_ge(sem("moe_base_ready"), n + 1)
                        for t in range(QT):
                            xt = X[:, bass.ds(QT * n + t, 1)].rearrange("p a d -> p (a d)")
                            ins = e.scalar_tensor_tensor(xt, PS[:, 6 + x % 2, D * t:D * t + D], mix[:, u, t, x:x + 1], xt,
                                                         ALU.mult, ALU.add)
                        ins.then_inc(sem("moe_added"), 1)
                    if front and x == 3:
                        e.wait_ge(sem("moe_biases_done"), m + 1)
                        e.tensor_tensor(tiles(m), tiles(m), PS[:, 1].rearrange("p (t d) -> p t d", t=QT), ALU.add)\
                            .then_inc(sem("moe_base_ready"), 1)
                    if head and x == 3:
                        quad_norm_vector(e, MQ * NQ, k, u, None, False, None)
            walk(e, NQ, step)

        def moe_scalar(e, c):
            def step(k, u, head, front, back):
                n = 2 * k + u
                m, v = n + 1, 1 - u
                for x in range(NE):
                    if back:
                        if x:
                            wait(e, sem("moe_down_done"), n * NE + x - 1)
                        for f in range(FC):
                            e.wait_ge(sem("moe_h_done"), (n * NE + x) * FC + f + 1)
                            e.activation(e_h[:, x % 2, f], PS[:, 2 + f], ACT.Gelu,
                                         bias=col("e_b1")[:, FC * x + f:FC * x + f + 1]).then_inc(sem("moe_h_ready"), 1)
                    if front and x == 1:
                        e.wait_ge(sem("moe_mixT_done"), m + 1)
                        wait(e, sem("moe_biases_done"), m)
                        e.activation(mixT.rearrange("p t c -> p (t c)"), PS[0:NE, 1], ACT.Copy)\
                            .then_inc(sem("moe_mixT_kept"), 1)
                    if head and x == 7:
                        wait(e, sem("moe_h_done"), (n + 1) * NE * FC)
                        quad_keep_scalar(e, MQ * NQ, k, u, ("moe_g", "moe_b"))
            walk(e, NQ, step)

        def moe_sync(e, c):
            def step(k, u, head, front, back):
                n = 2 * k + u
                if back:
                    wait_alone(e, sem("moe_added"), (n + 1) * NE)
                    e.dma_start(out[bass.ds(NBU * n, NBU)].rearrange("(t b) s d -> (b s) t d", b=2), tiles(n))\
                        .then_inc(sem(f"out_written{u}"), 16)
            walk(e, NQ, step)

        L0 = dict(sync=l0_sync, gpsimd=l0_pool, tensor=l0_tensor, vector=l0_vector, scalar=l0_scalar)
        AT = dict(sync=att_sync, gpsimd=att_pool, tensor=att_tensor, vector=att_vector, scalar=att_scalar)
        FN = dict(sync=ff_sync, gpsimd=ff_pool, tensor=ff_tensor, vector=ff_vector, scalar=ff_scalar)
        L2 = dict(gpsimd=l2_pool, tensor=l2_tensor, vector=l2_vector, scalar=l2_scalar)
        MOE = dict(sync=moe_sync, gpsimd=moe_pool, tensor=moe_tensor, vector=moe_vector, scalar=moe_scalar)
        PHASES = [(L0, None), (FN, FFN[0]), (AT, ATT[0]), (AT, ATT[1]), (FN, FFN[1]), (L2, None), (AT, ATT[2]),
                  (AT, ATT[3]), (MOE, None)]
        block = ctx.enter_context(nc.Block())

        @block.sync
        def _(e):
            for n, (kind, c) in enumerate(PHASES):
                if "sync" in kind:
                    kind["sync"](e, c)
                meet(e, n + 1)
            for u in range(2):
                e.wait_ge(sem(f"out_written{u}"), 16 * NQ // 2)

        @block.gpsimd
        def _(e):
            for n, (kind, c) in enumerate(PHASES):
                if "gpsimd" in kind:
                    kind["gpsimd"](e, c)
                meet(e, n + 1)

        @block.tensor
        def _(e):
            for n, (kind, c) in enumerate(PHASES):
                kind["tensor"](e, c)
                meet(e, n + 1)

        @block.vector
        def _(e):
            for n, (kind, c) in enumerate(PHASES):
                kind["vector"](e, c)
                meet(e, n + 1)

        @block.scalar
        def _(e):
            for n, (kind, c) in enumerate(PHASES):
                kind["scalar"](e, c)
                meet(e, n + 1)


def lay_out(i):
    c = np.ascontiguousarray
    f = {k: np.asarray(v) for k, v in i.items()}
    T = {}
    NB = f["x"].shape[0]
    T["x"] = f["x"]
    T["ctx"] = f["ctx_1024"]
    T["token_mask"] = c(f["mask_BxSx1_ff1"].reshape(NB * S // P, P).T)
    T["mask0"] = f["mask_BxSx1024_bf0"]
    T["mask1"] = f["mask_Bx1xSxS2_ik0"].reshape(NB, S, S)
    T["mask2"] = f["mask_Bx1xSxS2_if1"].reshape(NB, S, S)
    L0, L1, L2, L3 = ({k[len(p):]: v for k, v in f.items() if k.startswith(p)}
                      for p in ("L0_xattn_", "L1_xattn_", "L2_xattn_", "L3_xattn_"))
    for n in ("Wq", "Wk", "Wv"):
        T[f"l0_{n}T"] = c(L0[n].reshape(D, H, DK).transpose(2, 1, 0))
    T["l0_Wr"] = L0["Wr"].reshape(D, H, DK)
    T["l0_Wo"] = c(L0["Wo"].reshape(H, DK, D).transpose(1, 0, 2))
    T["l0_cb"] = c(L0["content_bias"].T)
    T["l0_pb"] = c(L0["position_bias"].T)
    T["l0_W1"] = L0["W1"]
    T["l0_W2"] = c(L0["W2"].reshape(FC, P, D).transpose(1, 0, 2))
    T["l1_W1"] = c(L1["ff_W1"].T)
    T["l1_W2"] = c(L1["ff_W2"].T.reshape(FC, P, D).transpose(1, 0, 2))

    def blocks(w):
        o = np.zeros((D, D), np.float32)
        for h in range(H):
            o[HD * h:HD * h + HD, HD * h:HD * h + HD] = w.T
        return o
    def out_rows(w):
        return c(w.T.reshape(2, 2, 4, HD, D).transpose(0, 2, 3, 1, 4).reshape(S, 2, D))
    for n, p in (("msa", "msa"), ("ca1", "ca")):
        T["w_" + n] = c(np.stack([blocks(L1[f"{p}_W{x}"]) for x in "qkv"], axis=1))
        T["wo_" + n] = out_rows(L1[f"{p}_Wo"])
    for n in ("sa", "ca"):
        T["w_" + n] = c(L3[n + "_in_w"].reshape(3, D, D).transpose(2, 0, 1))
        T["wo_" + n] = out_rows(L3[n + "_out_w"])
    T["l2_W"] = c(np.stack([L2["Wt"].T, L2["Wv"].T, L2["Wg"][:, :D].T, L2["Wg"][:, D:].T], axis=1))
    T["router"] = c(L3["router_w"].T)
    T["e_b2"] = L3["e_fc2_b"]
    T["e_W1"] = c(L3["e_fc1_w"].transpose(2, 0, 1))
    T["e_W2"] = c(L3["e_fc2_w"].reshape(NE, D, FC, P).transpose(3, 0, 2, 1))
    group = np.zeros((P, 4), np.float32)
    place = np.zeros((P, 4), np.float32)
    for p in range(P):
        group[p, p // 32] = 1
        place[p, p // HD % 4] = 1
    by_chunk = lambda b: b.reshape(-1, P).T
    vals = {"l0_b1": by_chunk(L0["b1"]), "l1_b1": by_chunk(L1["ff_b1"]), "bt": L2["bt"], "bv": L2["bv"],
            "bg": L2["bg"], "sa_g": L3["sa_ln_g"], "sa_b": L3["sa_ln_b"], "caq_g": L3["ca_q_ln_g"],
            "caq_b": L3["ca_q_ln_b"], "cakv_g": L3["ca_kv_ln_g"], "cakv_b": L3["ca_kv_ln_b"],
            "moe_g": L3["moe_ln_g"], "moe_b": L3["moe_ln_b"], "sa_bq": L3["sa_in_b"][:D],
            "sa_bk": L3["sa_in_b"][D:2 * D], "ca_bq": L3["ca_in_b"][:D], "ca_bk": L3["ca_in_b"][D:2 * D],
            "e_b1": L3["e_fc1_b"].reshape(NE * FC, P).T, "group": group, "place": place}
    T["cols"] = c(np.concatenate([vals[n].reshape(P, -1) for n in COLS], axis=1))
    misc = np.zeros(D, np.float32)
    misc[:NE] = L3["router_b"]
    misc[NE:2 * NE] = np.arange(NE)
    rowvals = {"ln01_g": L0["ln1_g"], "ln01_b": L0["ln1_b"], "l0_b2": L0["b2"], "ln02_g": L0["ln2_g"],
               "ln02_b": L0["ln2_b"], "msa_bo": L1["msa_bo"], "ln11_g": L1["ln1_g"], "ln11_b": L1["ln1_b"],
               "ca1_bo": L1["ca_bo"], "ln12_g": L1["ln2_g"], "ln12_b": L1["ln2_b"], "l1_b2": L1["ff_b2"],
               "ln13_g": L1["ln3_g"], "ln13_b": L1["ln3_b"], "l2_g": L2["gamma"], "l2_b": L2["beta"],
               "sa_bv": L3["sa_in_b"][2 * D:], "sa_bo": L3["sa_out_b"], "ca_bv": L3["ca_in_b"][2 * D:],
               "ca_bo": L3["ca_out_b"], "misc": misc}
    T["rows"] = c(np.stack([rowvals[n] for n in ROWS]))
    T["ident"] = np.eye(P, dtype=np.float32)
    pos = np.arange(KL - 1, -1, -1, dtype=np.float32)
    freq = (1.0 / 10000.0 ** (np.arange(0, D, 2, dtype=np.float32) / D)).astype(np.float32)
    angle = pos[:, None] * freq
    T["peT"] = c(np.concatenate([np.sin(angle), np.cos(angle)], axis=-1).T.astype(np.float32))
    return T


def kernel(**inputs):
    import concourse.bacc as _bacc
    from concourse.bass_utils import run_bass_kernel_spmd as _run

    T = lay_out(inputs)
    nc = _bacc.Bacc("TRN2", target_bir_lowering=False, num_devices=1)
    a = {n: nc.dram_tensor(n, v.shape, mybir.dt.from_np(v.dtype), kind="ExternalInput").ap() for n, v in T.items()}
    out = nc.dram_tensor("out_0_dram", T["x"].shape, F32, kind="ExternalOutput").ap()
    build(nc, a, out)
    r = _run(nc, [T], core_ids=[0])
    return r.results[0]["out_0_dram"]
```
